# Optimizing a Trainium2 kernel written in Bass

```python
import numpy as np
import jax
import jax.numpy as jnp

def _softmax(x, axis=-1):
    return jax.nn.softmax(x, axis=axis)

def _gelu(x):
    return jax.nn.gelu(x, approximate=True)

def _silu(x):
    return jax.nn.silu(x)

def _sigmoid(x):
    return jax.nn.sigmoid(x)

def _layernorm(x, axis=-1, eps=1e-05):
    m = jnp.mean(x, axis=axis, keepdims=True)
    v = jnp.var(x, axis=axis, keepdims=True)
    return (x - m) / jnp.sqrt(v + eps)

def _scatter_add(tgt, idx, src, axis=0):
    return tgt.at[idx].add(src)

def _segment_sum(src, seg, n):
    return jax.ops.segment_sum(src, seg, n)
kernel_name = 'mk_adj_ffn_d2_adj_r2_ccd601'

def setup_inputs(seed: int=0):
    np.random.seed(seed)
    _w = jnp.asarray

    def _rec_inputs():
        import jax
        import jax.numpy as jnp
        _gk = jax.random.key(seed)
        x = -0.0002928 + 1 * jax.random.normal(jax.random.fold_in(_gk, 1), (2048, 256), jnp.float32)
        _a = jax.random.bernoulli(jax.random.fold_in(_gk, 2), 0.00390625, (2048, 2048))
        _a = jnp.logical_or(_a, jnp.swapaxes(_a, -1, -2))
        _a = jnp.logical_or(_a, jnp.eye(2048, dtype=bool))
        adj = _a.astype(jnp.int32)
        return (x, adj)
    x, adj = _rec_inputs()

    def _L0_gnn_setup():
        import jax, jax.numpy as jnp
        import numpy as np
        N, D_IN, D_OUT = (4096, 256, 256)
        key = jax.random.key(seed)
        ks = jax.random.split(key, 8)
        scale_in = 1.0 / np.sqrt(D_IN)
        scale_cat = 1.0 / np.sqrt(2 * D_OUT)
        return {'x': jax.random.normal(ks[0], (N, D_IN), dtype=jnp.float32), 'adj': jax.random.randint(ks[1], (N, N), 0, 2, dtype=jnp.int32), 'W_self': jax.random.uniform(ks[2], (D_IN, D_OUT), jnp.float32, -scale_in, scale_in), 'b_self': jax.random.uniform(ks[3], (D_OUT,), jnp.float32, -scale_in, scale_in), 'W_nb': jax.random.uniform(ks[4], (D_IN, D_OUT), jnp.float32, -scale_in, scale_in), 'b_nb': jax.random.uniform(ks[5], (D_OUT,), jnp.float32, -scale_in, scale_in), 'W_comb': jax.random.uniform(ks[6], (2 * D_OUT, D_OUT), jnp.float32, -scale_cat, scale_cat), 'b_comb': jax.random.uniform(ks[7], (D_OUT,), jnp.float32, -scale_cat, scale_cat)}
    _L0_gnn_all = _L0_gnn_setup()
    _L0_gnn_in = {k: v for k, v in _L0_gnn_all.items() if k in ('W_self', 'b_self', 'W_nb', 'b_nb', 'W_comb', 'b_comb')}
    del _L0_gnn_all

    def _L0_ffn_setup():
        import jax, jax.numpy as jnp
        import numpy as np
        B, S, D = (4, 1024, 256)
        I = 192
        E = 16
        K = 2

        def _inv_softplus(v):
            return float(np.log(np.expm1(v)))

        def swiglu5(h, alpha, gate_scale, up_shift, gate_clamp_raw, up_clamp_raw):
            gate_clamp = jax.nn.softplus(gate_clamp_raw)
            up_clamp = jax.nn.softplus(up_clamp_raw)
            g = jnp.clip(h[..., ::2], -gate_clamp, gate_clamp)
            u = jnp.clip(h[..., 1::2], -up_clamp, up_clamp)
            return g * jax.nn.sigmoid(g * alpha) * gate_scale * (u + up_shift)
        key = jax.random.key(seed)
        ks = jax.random.split(key, 10)
        std = 0.02
        raw = _inv_softplus(7.0)
        act = jnp.array([1.702, 1.0, 1.0, raw, raw], dtype=jnp.float32)
        return {'x': jax.random.normal(ks[0], (B, S, D), dtype=jnp.float32), 'gate_w': jax.random.normal(ks[1], (D, E), dtype=jnp.float32) * 0.01, 'gate_b': jnp.zeros((E,), dtype=jnp.float32), 'shared_w1': jax.random.normal(ks[2], (D, 2 * I), dtype=jnp.float32) * std, 'shared_b1': jnp.zeros((2 * I,), dtype=jnp.float32), 'shared_w2': jax.random.normal(ks[3], (I, D), dtype=jnp.float32) * std, 'shared_b2': jnp.zeros((D,), dtype=jnp.float32), 'shared_act': act, 'expert_w1': jax.random.normal(ks[4], (E, D, 2 * I), dtype=jnp.float32) * std, 'expert_b1': jnp.zeros((E, 2 * I), dtype=jnp.float32), 'expert_w2': jax.random.normal(ks[5], (E, I, D), dtype=jnp.float32) * std, 'expert_b2': jnp.zeros((E, D), dtype=jnp.float32), 'expert_act': jnp.tile(act[None, :], (E, 1))}
    _L0_ffn_all = _L0_ffn_setup()
    _L0_ffn_in = {k: v for k, v in _L0_ffn_all.items() if k in ('gate_w', 'gate_b', 'shared_w1', 'shared_b1', 'shared_w2', 'shared_b2', 'shared_act', 'expert_w1', 'expert_b1', 'expert_w2', 'expert_b2', 'expert_act')}
    del _L0_ffn_all

    def _L1_gnn_setup():
        import jax, jax.numpy as jnp
        import numpy as np
        N = 4096
        EMB2 = 256
        HID = 128
        NEG_SLOPE = 0.01
        key = jax.random.key(seed)
        ks = jax.random.split(key, 7)
        inlayer = jax.random.normal(ks[0], (N, EMB2), dtype=jnp.float32)
        adj_mat = jax.random.randint(ks[1], (N, N), 0, 2, dtype=jnp.int32)
        W1 = jax.random.normal(ks[2], (HID, EMB2), dtype=jnp.float32) * (1.0 / np.sqrt(EMB2))
        w2 = jax.random.normal(ks[3], (HID,), dtype=jnp.float32) * (1.0 / np.sqrt(HID))
        b2 = jax.random.normal(ks[4], (1,), dtype=jnp.float32) * 0.01
        w3 = jax.random.normal(ks[5], (HID,), dtype=jnp.float32) * (1.0 / np.sqrt(HID))
        b3 = jax.random.normal(ks[6], (1,), dtype=jnp.float32) * 0.01
        return {'inlayer': inlayer, 'adj_mat': adj_mat, 'W1': W1, 'w2': w2, 'b2': b2, 'w3': w3, 'b3': b3}
    _L1_gnn_all = _L1_gnn_setup()
    _L1_gnn_in = {k: v for k, v in _L1_gnn_all.items() if k in ('W1', 'w2', 'b2', 'w3', 'b3')}
    del _L1_gnn_all

    def _L1_ffn_setup():
        import jax, jax.numpy as jnp
        import numpy as np
        FP8_MAX = 448.0
        K, N = (256, 256)
        key = jax.random.key(seed)
        kx, kw = jax.random.split(key)
        x = jax.random.normal(kx, (8, 4096, K), dtype=jnp.float32)
        weight = jax.random.normal(kw, (K, N), dtype=jnp.float32) * 0.02
        return {'x': x, 'weight': weight}
    _L1_ffn_all = _L1_ffn_setup()
    _L1_ffn_in = {k: v for k, v in _L1_ffn_all.items() if k in ('weight',)}
    del _L1_ffn_all
    return {'x': x, 'adj': adj, 'L0_gnn_W_self': _L0_gnn_in['W_self'], 'L0_gnn_b_self': _L0_gnn_in['b_self'], 'L0_gnn_W_nb': _L0_gnn_in['W_nb'], 'L0_gnn_b_nb': _L0_gnn_in['b_nb'], 'L0_gnn_W_comb': _L0_gnn_in['W_comb'], 'L0_gnn_b_comb': _L0_gnn_in['b_comb'], 'L0_ffn_gate_w': _L0_ffn_in['gate_w'], 'L0_ffn_gate_b': _L0_ffn_in['gate_b'], 'L0_ffn_shared_w1': _L0_ffn_in['shared_w1'], 'L0_ffn_shared_b1': _L0_ffn_in['shared_b1'], 'L0_ffn_shared_w2': _L0_ffn_in['shared_w2'], 'L0_ffn_shared_b2': _L0_ffn_in['shared_b2'], 'L0_ffn_shared_act': _L0_ffn_in['shared_act'], 'L0_ffn_expert_w1': _L0_ffn_in['expert_w1'], 'L0_ffn_expert_b1': _L0_ffn_in['expert_b1'], 'L0_ffn_expert_w2': _L0_ffn_in['expert_w2'], 'L0_ffn_expert_b2': _L0_ffn_in['expert_b2'], 'L0_ffn_expert_act': _L0_ffn_in['expert_act'], 'L1_gnn_W1': _L1_gnn_in['W1'], 'L1_gnn_w2': _L1_gnn_in['w2'], 'L1_gnn_b2': _L1_gnn_in['b2'], 'L1_gnn_w3': _L1_gnn_in['w3'], 'L1_gnn_b3': _L1_gnn_in['b3'], 'L1_ffn_weight': _L1_ffn_in['weight']}

def reference(x, adj, L0_gnn_W_self, L0_gnn_b_self, L0_gnn_W_nb, L0_gnn_b_nb, L0_gnn_W_comb, L0_gnn_b_comb, L0_ffn_gate_w, L0_ffn_gate_b, L0_ffn_shared_w1, L0_ffn_shared_b1, L0_ffn_shared_w2, L0_ffn_shared_b2, L0_ffn_shared_act, L0_ffn_expert_w1, L0_ffn_expert_b1, L0_ffn_expert_w2, L0_ffn_expert_b2, L0_ffn_expert_act, L1_gnn_W1, L1_gnn_w2, L1_gnn_b2, L1_gnn_w3, L1_gnn_b3, L1_ffn_weight):
    import jax
    import jax.numpy as jnp

    def _L0_gnn_ref(x, adj, W_self, b_self, W_nb, b_nb, W_comb, b_comb):
        import jax, jax.numpy as jnp
        import numpy as np
        N, D_IN, D_OUT = (4096, 256, 256)
        mask = (adj > 0).astype(x.dtype)
        deg = jnp.sum(mask, axis=1, keepdims=True)
        agg = mask @ x / jnp.maximum(deg, 1.0)
        self_f = x @ W_self + b_self
        nb_f = agg @ W_nb + b_nb
        combined = jnp.concatenate([self_f, nb_f], axis=-1)
        out = combined @ W_comb + b_comb
        return jax.nn.relu(out)

    def _L0_ffn_ref(x, gate_w, gate_b, shared_w1, shared_b1, shared_w2, shared_b2, shared_act, expert_w1, expert_b1, expert_w2, expert_b2, expert_act):
        import jax, jax.numpy as jnp
        import numpy as np
        B, S, D = (4, 1024, 256)
        I = 192
        E = 16
        K = 2

        def _inv_softplus(v):
            return float(np.log(np.expm1(v)))

        def swiglu5(h, alpha, gate_scale, up_shift, gate_clamp_raw, up_clamp_raw):
            gate_clamp = jax.nn.softplus(gate_clamp_raw)
            up_clamp = jax.nn.softplus(up_clamp_raw)
            g = jnp.clip(h[..., ::2], -gate_clamp, gate_clamp)
            u = jnp.clip(h[..., 1::2], -up_clamp, up_clamp)
            return g * jax.nn.sigmoid(g * alpha) * gate_scale * (u + up_shift)
        shape = x.shape
        xf = x.reshape(-1, shape[-1])
        h = xf @ shared_w1 + shared_b1
        t = swiglu5(h, shared_act[0], shared_act[1], shared_act[2], shared_act[3], shared_act[4])
        z = t @ shared_w2 + shared_b2
        gate_logits = xf @ gate_w + gate_b
        gate_probs = jax.nn.softmax(gate_logits, -1)
        w, idx = jax.lax.top_k(gate_probs, K)
        w = w / jnp.sum(w, axis=-1, keepdims=True)
        cw = jnp.sum(jax.nn.one_hot(idx, E, dtype=xf.dtype) * w[..., None], axis=1)
        he = jnp.einsum('nd,edh->enh', xf, expert_w1) + expert_b1[:, None, :]
        a = expert_act
        te = swiglu5(he, a[:, 0, None, None], a[:, 1, None, None], a[:, 2, None, None], a[:, 3, None, None], a[:, 4, None, None])
        oe = jnp.einsum('enh,ehd->end', te, expert_w2) + expert_b2[:, None, :]
        y = jnp.einsum('ne,end->nd', cw, oe)
        return (y + z).reshape(shape)

    def _L1_gnn_ref(inlayer, adj_mat, W1, w2, b2, w3, b3):
        import jax, jax.numpy as jnp
        import numpy as np
        N = 4096
        EMB2 = 256
        HID = 128
        NEG_SLOPE = 0.01
        in_fts = jnp.einsum('ne,he->nh', inlayer, W1)
        f_1 = in_fts @ w2 + b2[0]
        f_2 = in_fts @ w3 + b3[0]
        logits = f_1[:, None] + f_2[None, :]
        adj_f = adj_mat.astype(jnp.float32)
        logits = adj_f * logits
        bias_mat = -1000000000.0 * (1.0 - (adj_mat > 0).astype(jnp.float32))
        coefs = jax.nn.softmax(jax.nn.leaky_relu(logits, NEG_SLOPE) + bias_mat, axis=1)
        vals = coefs @ inlayer
        return jax.nn.relu(vals)

    def _L1_ffn_ref(x, weight):
        import jax, jax.numpy as jnp
        import numpy as np
        FP8_MAX = 448.0
        K, N = (256, 256)
        B, S, _ = x.shape
        x2d = x.reshape(-1, K)
        x_amax = jnp.max(jnp.abs(x2d))
        x_scale = FP8_MAX / jnp.maximum(x_amax, 1e-12)
        x_fp8 = jnp.clip(x2d * x_scale, -FP8_MAX, FP8_MAX).astype(jnp.float8_e4m3fn)
        w_amax = jnp.max(jnp.abs(weight))
        w_scale = FP8_MAX / jnp.maximum(w_amax, 1e-12)
        w_fp8 = jnp.clip(weight.T * w_scale, -FP8_MAX, FP8_MAX).astype(jnp.float8_e4m3fn)
        res = jnp.matmul(x_fp8.astype(jnp.float32), w_fp8.astype(jnp.float32).T)
        out = res * (1.0 / x_scale * (1.0 / w_scale))
        return out.reshape(B, S, N).astype(x.dtype)
    x = x + _L0_gnn_ref(_layernorm(x, axis=-1), adj, L0_gnn_W_self, L0_gnn_b_self, L0_gnn_W_nb, L0_gnn_b_nb, L0_gnn_W_comb, L0_gnn_b_comb)
    x = x + _L0_ffn_ref(_layernorm(x, axis=-1)[None], L0_ffn_gate_w, L0_ffn_gate_b, L0_ffn_shared_w1, L0_ffn_shared_b1, L0_ffn_shared_w2, L0_ffn_shared_b2, L0_ffn_shared_act, L0_ffn_expert_w1, L0_ffn_expert_b1, L0_ffn_expert_w2, L0_ffn_expert_b2, L0_ffn_expert_act)[0]
    x = x + _L1_gnn_ref(_layernorm(x, axis=-1), adj, L1_gnn_W1, L1_gnn_w2, L1_gnn_b2, L1_gnn_w3, L1_gnn_b3)
    x = x + _L1_ffn_ref(_layernorm(x, axis=-1)[None], L1_ffn_weight)[0]
    return x

_drawn_inputs = setup_inputs


def setup_inputs(seed=0):
    import zlib

    import numpy as np

    out = dict(_drawn_inputs(seed))
    spreads = {'L0_ffn_gate_b': (0.0, 0.1),
     'L0_ffn_shared_b1': (0.0, 0.356),
     'L0_ffn_shared_b2': (0.0, 0.1),
     'L0_ffn_expert_b1': (0.0, 0.541),
     'L0_ffn_expert_b2': (0.0, 0.1)}
    factors = {'L0_gnn_b_self': 3.929, 'L0_gnn_b_nb': 3.244}
    for name, (base, spread) in spreads.items():
        noise = np.random.default_rng([zlib.crc32(name.encode()), seed]).standard_normal(out[name].shape)
        drawn = base * np.exp(spread * noise) if base else spread * noise
        out[name] = jnp.asarray(drawn.astype(out[name].dtype))
    for name, factor in factors.items():
        out[name] = (out[name] * factor).astype(out[name].dtype)
    return out
```

```python
from contextlib import ExitStack

import numpy as np

import concourse.bass as bass
from concourse import mybir

F32 = mybir.dt.float32
BF16 = mybir.dt.bfloat16
FP16 = mybir.dt.float16
I32 = mybir.dt.int32
U32 = mybir.dt.uint32
ALU = mybir.AluOpType
ACT = mybir.ActivationFunctionType
AX = mybir.AxisListType.X

P = 128
N = 2048
D = 256
NT = N // P
KD = D // P
NJ = N // P
E = 16
NE = E + 1
I2 = 384
I = I2 // 2
KI = 2
IH = I // KI
TOPK = 2
NS = N * TOPK // P + E
PARTS = 3
NB = NE * PARTS
EPS = 1e-5
SCALE16 = 2048.0
NO_EDGE = -float(2 ** 30)
FP8_MAX = 448.0

X_AT = N // P * D


class Region:

    def __init__(self, tensor, words):
        self.tensor, self.words, self.at = tensor, words, 0

    def take(self, dtype, *shape, rows=P):
        size = int(np.prod(shape))
        words = -(-size * (2 if dtype in (BF16, FP16) else 4) // 4)
        words += words % 2
        assert self.at + words <= self.words, (self.at, words, self.words)
        view = self.tensor[0:rows, self.at:self.at + words]
        self.at += words
        if dtype != F32:
            view = view.bitcast(dtype)
        view = view[:, 0:size]
        if len(shape) == 2:
            view = view.rearrange("p (a b) -> p a b", b=shape[1])
        elif len(shape) == 3:
            view = view.rearrange("p (a b c) -> p a b c", b=shape[1], c=shape[2])
        return view


class Chain:

    def __init__(self, engine, semaphore):
        self.engine, self.semaphore, self.count = engine, semaphore, 0

    def link(self, instruction):
        self.count += 1
        instruction.then_inc(self.semaphore, 1)
        self.engine.wait_ge(self.semaphore, self.count)


def at(view, i):
    if isinstance(i, int):
        return view[:, i]
    one = view[:, bass.ds(i, 1)]
    return one.squeeze(1) if len(one.shape) > 2 else one


def build(nc, a, stop="D"):
    ctx = ExitStack()
    with ctx:
        _build(nc, a, stop, ctx)


def _build(nc, a, stop, ctx):
    dram = {}
    for name, v in a.items():
        dram[name] = nc.dram_tensor(name, v.shape, mybir.dt.from_np(v.dtype), kind="ExternalInput").ap()
    out = nc.dram_tensor("out_0_dram", (N, D), F32, kind="ExternalOutput").ap()
    slot_x = nc.dram_tensor("slot_x", (NS * P, D), F32, kind="Internal").ap()
    slot_y = nc.dram_tensor("slot_y", (NS * P, D), F32, kind="Internal").ap()

    def sb(name, words):
        return ctx.enter_context(nc.sbuf_tensor(name, [P, words], F32))

    ARENA_WORDS = NE * KD * I2 + NE * KI * D
    mem = {
        "X": sb("X", NT * D), "XLN": sb("XLN", NT * D), "EDGES": sb("EDGES", NT * N // 2),
        "ARENA": sb("ARENA", ARENA_WORDS), "SMALL": sb("SMALL", 5700),
        "PSUM": ctx.enter_context(nc.psum_tensor("PSUM", [P, 8 * 512], F32)),
        "slot_x": slot_x, "slot_y": slot_y, "out": out,
    }
    mem["x"] = mem["X"][:, :].rearrange("p (t d) -> p t d", d=D)
    mem["xln"] = mem["XLN"][:, :].rearrange("p (t d) -> p t d", d=D)
    mem["edges"] = mem["EDGES"][:, :].bitcast(BF16).rearrange("p (t n) -> p t n", n=N)
    CONST_WORDS = 1100
    mem["CONST"] = sb("CONST", CONST_WORDS)
    mem["const"] = const = Region(mem["CONST"], CONST_WORDS)
    mem["identity"] = const.take(F32, P)
    mem["identity16"] = const.take(BF16, P)
    mem["ones"] = const.take(F32, P)
    mem["mean"] = const.take(F32, NT)
    mem["rstd"] = const.take(F32, NT)
    sem_count = [0]

    def sem(name):
        return ctx.enter_context(nc.semaphore(name))

    mean_aggregate(nc, dram, mem, sem)
    if stop == "A":
        return
    mixture(nc, dram, mem, sem)
    if stop == "B":
        return
    attention(nc, dram, mem, sem)
    if stop == "C":
        return
    fp8_product(nc, dram, mem, sem)


def layernorm_sums(dve, nc, x, stats, done):
    with dve.Fori(0, NT) as t:
        nc.vector.bn_stats(at(stats, t), at(x, t)).then_inc(done, 1)


def layernorm_spread(dve, nc, chain, stats, mean, var, tmp, done, count):
    dve.wait_ge(done, count)
    me, mo, se, so = stats[:, :, 1], stats[:, :, 4], stats[:, :, 2], stats[:, :, 5]
    chain.link(nc.vector.tensor_tensor(mean, me, mo, ALU.add))
    chain.link(nc.vector.tensor_tensor(tmp, me, mo, ALU.subtract))
    chain.link(nc.vector.tensor_tensor(var, se, so, ALU.add))
    chain.link(nc.vector.tensor_scalar(mean, mean, 0.5, None, ALU.mult))
    chain.link(nc.vector.scalar_tensor_tensor(out=tmp, in0=tmp, scalar=0.25, in1=tmp, op0=ALU.mult, op1=ALU.mult))
    chain.link(nc.vector.tensor_scalar(var, var, 1.0 / D, EPS, ALU.mult, ALU.add))
    return nc.vector.tensor_tensor(var, var, tmp, ALU.add)



def mean_aggregate(nc, dram, mem, sem):
    x, edges = mem["x"], mem["edges"]
    identity, identity16, ones = mem["identity"], mem["identity16"], mem["ones"]
    mean, rstd = mem["mean"], mem["rstd"]
    psum = mem["PSUM"]
    arena = Region(mem["ARENA"], mem["ARENA"].shape[1])
    STAGES = 4
    adj_in = arena.take(I32, STAGES, N)
    ln16 = arena.take(FP16, NT, 2 * D)
    maskT = arena.take(BF16, 2, NJ, P)
    mask = arena.take(BF16, 2, N)
    w_self, w_nb = arena.take(F32, KD, D), arena.take(F32, KD, D)
    w_comb = arena.take(F32, 2 * KD, D)
    small = Region(mem["SMALL"], 5700)
    w_selfT, w_nbT = small.take(F32, KD, D), small.take(F32, KD, D)
    wx, wa = small.take(F32, KD, D), small.take(F32, KD, D)
    b_cols = small.take(F32, 2 * KD, 1)
    b_wide = small.take(F32, 2 * KD, P)
    b_comb = small.take(F32, D, rows=1)
    bias = small.take(F32, D)
    stats = small.take(F32, NT, 6)
    var, tmp = small.take(F32, NT), small.take(F32, NT)
    deg, rdeg = small.take(F32, STAGES), small.take(F32, STAGES)
    xn = small.take(F32, 2, D)
    agg_low, agg = small.take(F32, 2, D), small.take(F32, 2, D)
    xnT, aggT = arena.take(F32, 2, KD, P), arena.take(F32, 2, KD, P)
    out_b = small.take(F32, 2, D)
    zeros = mem["XLN"][:, 0:2048]

    ps_mask = [psum[:, 1024 * s:1024 * (s + 1)].bitcast(BF16).rearrange("p (j q) -> p j q", q=P)[:, 0:NJ, :] for s in range(2)]
    ps_agg = [psum[:, 2048 + 512 * s:2048 + 512 * (s + 1)] for s in range(2)]
    ps_turn = psum[:, 3072:3584].rearrange("p (k q) -> p k q", q=P)
    ps_out = psum[:, 3584:3584 + D]

    x_in = sem("a_x_in")
    w_in = sem("a_w_in")
    adj_landed = [sem(f"a_adj_landed{s}") for s in range(STAGES)]
    zeros_ready = sem("a_zeros_ready")
    slots_zeroed = sem("slots_zeroed")
    mem["slots_zeroed"] = slots_zeroed
    const_ready = sem("a_const_ready")
    dve_chain = sem("a_dve_chain")
    stats_done, var_ready, sd_ready = sem("a_stats_done"), sem("a_var_ready"), sem("a_sd_ready")
    mask_ready, turned, maskT_ready = sem("a_mask_ready"), sem("a_turned"), sem("a_maskT_ready")
    agg_summed, agg_ready = sem("a_agg_summed"), sem("a_agg_ready")
    xn_ready, low_ready = sem("a_xn_ready"), sem("a_low_ready")
    both_turned, both_ready = sem("a_both_turned"), sem("a_both_ready")
    out_summed, out_read, x_added = sem("a_out_summed"), sem("a_out_read"), sem("a_x_added")
    wT_turned, wT_ready, w_summed, w_ready = (sem("a_" + n) for n in ("wT_turned", "wT_ready", "w_summed", "w_ready"))
    bias_summed, bias_ready, b_ready = sem("a_bias_summed"), sem("a_bias_ready"), sem("a_b_ready")
    split_done, edges_ready, rdeg_steps = sem("a_split_done"), sem("a_edges_ready"), sem("a_rdeg_steps")

    with nc.Block() as block:

        @block.sync
        def _(sp):
            sp.dma_start(x, dram["x"].rearrange("(t p) d -> p t d", p=P)).then_inc(x_in, 16)
            adj = dram["adj"].rearrange("(t p) n -> t p n", p=P)
            for s in range(STAGES):
                sp.dma_start(adj_in[:, s], adj[s]).then_inc(adj_landed[s], 16)
            with sp.Fori(1, NT // STAGES) as g:
                i0 = g * STAGES
                for s in range(STAGES):
                    sp.wait_ge(mask_ready, i0 + (s - STAGES + 1))
                    sp.dma_start(adj_in[:, s], at2(adj, i0 + s)).then_inc(adj_landed[s], 16)
            sp.wait_ge(zeros_ready, 1)
            per = 2048 // D
            zero_rows = mem["slot_x"].rearrange("(c p r) d -> c p (r d)", p=P, r=per)
            for c in range(NS // per):
                sp.dma_start(zero_rows[c], zeros).then_inc(slots_zeroed, 16)
            sp.wait_ge(slots_zeroed, 16 * (NS // per))

        @block.gpsimd
        def _(pool):
            nc.gpsimd.memset(identity, 0.0).then_inc(const_ready, 1)
            nc.gpsimd.memset(ones, 1.0).then_inc(const_ready, 1)
            nc.gpsimd.memset(zeros, 0.0).then_inc(zeros_ready, 1)
            pool.wait_ge(const_ready, 2)
            nc.gpsimd.affine_select(out=identity, in_=identity, compare_op=ALU.not_equal, fill=1.0, base=0,
                                    pattern=[[-1, P]], channel_multiplier=1).then_inc(const_ready, 1)
            pool.wait_ge(const_ready, 3)
            nc.gpsimd.tensor_copy(identity16, identity).then_inc(const_ready, 1)

        @block.scalar
        def _(act):
            for view, name in ((w_self, "L0_gnn_W_self"), (w_nb, "L0_gnn_W_nb"), (w_comb, "L0_gnn_W_comb")):
                act.dma_start(view, dram[name].rearrange("(k p) d -> p k d", p=P)).then_inc(w_in, 16)
            for k0, name in ((0, "L0_gnn_b_self"), (KD, "L0_gnn_b_nb")):
                act.dma_start(b_cols[:, k0:k0 + KD, :], dram[name].rearrange("(k p o) -> p k o", p=P, o=1),
                              allow_slow_non_contiguous=True).then_inc(w_in, 16)
            act.dma_start(b_comb, dram["L0_gnn_b_comb"].rearrange("(o d) -> o d", o=1)).then_inc(w_in, 16)
            act.wait_ge(var_ready, 1)
            nc.scalar.activation(var, var, ACT.Sqrt).then_inc(sd_ready, 1)
            for n, view in enumerate((w_selfT, w_nbT)):
                act.wait_ge(wT_turned, n + 1)
                nc.scalar.activation(view.rearrange("p k d -> p (k d)"), ps_agg[n], ACT.Copy).then_inc(wT_ready, 1)
            for n, view in enumerate((wx, wa)):
                act.wait_ge(w_summed, n + 1)
                nc.scalar.activation(view.rearrange("p k d -> p (k d)"), ps_agg[n], ACT.Copy).then_inc(w_ready, 1)

            def mask_out(i, s):
                act.wait_ge(turned, i + 1)
                nc.scalar.activation(maskT[:, s], ps_mask[s], ACT.Copy).then_inc(maskT_ready, 1)

            def both_out(i, s):
                act.wait_ge(both_turned, i + 1)
                nc.scalar.activation(xnT[:, s], ps_turn[:, 0:KD], ACT.Copy)
                nc.scalar.activation(aggT[:, s], ps_turn[:, KD:2 * KD], ACT.Copy).then_inc(both_ready, 1)

            mask_out(0, 0)
            mask_out(1, 1)
            with act.Fori(1, NT // 2) as g:
                i0 = g * 2
                for u in range(2):
                    both_out(i0 + (u - 2), u)
                    mask_out(i0 + u, u)
            both_out(NT - 2, 0)
            both_out(NT - 1, 1)

        @block.tensor
        def _(pe):
            pe.wait_ge(const_ready, 4)
            pe.wait_ge(w_in, 6 * 16)
            for n, (w, k0) in enumerate(((w_self, 0), (w_nb, KD))):
                for k in range(KD):
                    for m in range(KD):
                        last = nc.tensor.transpose(ps_agg[n][:, m * D + k * P:m * D + (k + 1) * P],
                                                   w[:, k, m * P:(m + 1) * P], identity)
                last.then_inc(wT_turned, 1)
            for n, wT in enumerate((w_selfT, w_nbT)):
                pe.wait_ge(wT_ready, n + 1)
                for rows in range(KD):
                    for m in range(KD):
                        last = nc.tensor.matmul(ps_agg[n][:, rows * D:(rows + 1) * D], wT[:, m, rows * P:(rows + 1) * P],
                                                w_comb[:, n * KD + m, :], start=(m == 0), stop=(m == KD - 1))
                last.then_inc(w_summed, 1)
            pe.wait_ge(b_ready, 1)
            for m in range(2 * KD):
                nc.tensor.matmul(ps_out, b_wide[:, m, :], w_comb[:, m, :], start=(m == 0), stop=False)
            nc.tensor.matmul(ps_out, ones[0:1, :], b_comb, start=False, stop=True).then_inc(bias_summed, 1)

            def turn_mask(i, s):
                pe.wait_ge(mask_ready, i + 1)
                for j in range(NJ):
                    last = nc.tensor.transpose(ps_mask[s][:, j, :], mask[:, s, j * P:(j + 1) * P], identity16)
                last.then_inc(turned, 1)

            def sum_neighbours(i, s):
                pe.wait_ge(maskT_ready, i + 1)
                for j in range(NJ):
                    last = nc.tensor.matmul(ps_agg[s], maskT[:, s, j, :], ln16[:, j, :], start=(j == 0), stop=(j == NJ - 1))
                last.then_inc(agg_summed, 1)

            def turn_both(i, s):
                pe.wait_ge(agg_ready, i + 1)
                pe.wait_ge(xn_ready, i + 1)
                for n, rows in enumerate((xn, agg)):
                    for k in range(KD):
                        last = nc.tensor.transpose(ps_turn[:, n * KD + k, :], rows[:, s, k * P:(k + 1) * P], identity)
                last.then_inc(both_turned, 1)

            def combine(i, s):
                pe.wait_ge(both_ready, i + 1)
                pe.wait_ge(out_read, i)
                for n, (lhs, w) in enumerate(((xnT, wx), (aggT, wa))):
                    for k in range(KD):
                        last = nc.tensor.matmul(ps_out, lhs[:, s, k, :], w[:, k, :], start=(n == 0 and k == 0),
                                                stop=(n == 1 and k == KD - 1))
                last.then_inc(out_summed, 1)

            turn_mask(0, 0)
            turn_mask(1, 1)
            pe.wait_ge(split_done, 3 * NT)
            pe.wait_ge(w_ready, 2)
            pe.wait_ge(bias_ready, 1)
            sum_neighbours(0, 0)
            with pe.Fori(0, NT // 2 - 1) as g:
                i0 = g * 2 + 1
                for u in range(2):
                    s = (1 + u) % 2
                    turn_mask(i0 + (u + 1), 1 - s)
                    turn_both(i0 + (u - 1), 1 - s)
                    sum_neighbours(i0 + u, s)
                    combine(i0 + (u - 1), 1 - s)
            turn_both(NT - 2, 0)
            sum_neighbours(NT - 1, 1)
            combine(NT - 2, 0)
            turn_both(NT - 1, 1)
            combine(NT - 1, 1)

        @block.vector
        def _(dve):
            chain = Chain(dve, dve_chain)
            dve.wait_ge(w_in, 6 * 16)
            nc.vector.tensor_copy(b_wide, b_cols.to_broadcast([P, 2 * KD, P])).then_inc(b_ready, 1)
            dve.wait_ge(x_in, 16)
            layernorm_sums(dve, nc, x, stats, stats_done)
            layernorm_spread(dve, nc, chain, stats, mean, var, tmp, stats_done, NT).then_inc(var_ready, 1)
            dve.wait_ge(sd_ready, 1)
            chain.link(nc.vector.reciprocal(rstd, var))
            with dve.Fori(0, NT // 2) as g:
                t0 = g * 2
                dve.wait_ge(split_done, t0 * 3)
                for u in range(2):
                    nc.vector.tensor_scalar(xn[:, u], at(x, t0 + u), col(mean, t0 + u), col(rstd, t0 + u),
                                            ALU.subtract, ALU.mult).then_inc(split_done, 1)
                dve.wait_ge(split_done, t0 * 3 + 2)
                for u in range(2):
                    nc.vector.tensor_scalar(at(ln16, t0 + u)[:, 0:D], xn[:, u], SCALE16, None, ALU.mult).then_inc(split_done, 1)
                dve.wait_ge(split_done, t0 * 3 + 4)
                for u in range(2):
                    nc.vector.scalar_tensor_tensor(out=at(ln16, t0 + u)[:, D:2 * D], in0=xn[:, u], scalar=SCALE16,
                                                   in1=at(ln16, t0 + u)[:, 0:D], op0=ALU.mult, op1=ALU.subtract
                                                   ).then_inc(split_done, 1)
            dve.wait_ge(split_done, 3 * NT)
            dve.wait_ge(bias_summed, 1)
            nc.vector.tensor_copy(bias, ps_out).then_inc(bias_ready, 1)

            def normalise(i, s):
                nc.vector.tensor_scalar(xn[:, s], at(x, i), col(mean, i), col(rstd, i), ALU.subtract, ALU.mult
                                        ).then_inc(xn_ready, 1)

            def make_mask(i, s, stage, landed):
                dve.wait_ge(adj_landed[stage], landed)
                dve.wait_ge(edges_ready, i)
                nc.vector.tensor_scalar(mask[:, s], adj_in[:, stage], 0.0, 0.0, ALU.is_gt, ALU.add,
                                        accum_out=col(deg, stage)).then_inc(mask_ready, 1)
                dve.wait_ge(mask_ready, i + 1)
                nc.vector.tensor_scalar(at(edges, i), mask[:, s], 1.0, -NO_EDGE, ALU.subtract, ALU.mult
                                        ).then_inc(edges_ready, 1)

            def mean_of_neighbours(i, s, stage):
                rdeg_i = col(rdeg, stage)
                nc.vector.tensor_scalar(rdeg_i, col(deg, stage), 1.0, SCALE16, ALU.max, ALU.mult).then_inc(rdeg_steps, 1)
                dve.wait_ge(rdeg_steps, i * 2 + 1)
                nc.vector.reciprocal(rdeg_i, rdeg_i).then_inc(rdeg_steps, 1)
                dve.wait_ge(rdeg_steps, i * 2 + 2)
                dve.wait_ge(agg_summed, i + 1)
                nc.vector.tensor_scalar(agg_low[:, s], ps_agg[s][:, D:2 * D], rdeg_i, None, ALU.mult
                                        ).then_inc(low_ready, 1)
                dve.wait_ge(low_ready, i + 1)
                nc.vector.scalar_tensor_tensor(out=agg[:, s], in0=ps_agg[s][:, 0:D], scalar=rdeg_i,
                                               in1=agg_low[:, s], op0=ALU.mult, op1=ALU.add).then_inc(agg_ready, 1)

            def add_result(i, s):
                dve.wait_ge(out_summed, i + 1)
                dve.wait_ge(x_added, i)
                nc.vector.tensor_tensor(out_b[:, s], ps_out, bias, ALU.add).then_inc(out_read, 1)
                dve.wait_ge(out_read, i + 1)
                nc.vector.scalar_tensor_tensor(out=at(x, i), in0=out_b[:, s], scalar=0.0, in1=at(x, i),
                                               op0=ALU.max, op1=ALU.add).then_inc(x_added, 1)

            def step(i, stage, first=False, more=True, landed=None):
                s = stage % 2
                mean_of_neighbours(i - 1, 1 - s, (stage - 1) % STAGES)
                if not first:
                    dve.wait_ge(both_turned, i - 1)
                normalise(i, s)
                if not first:
                    add_result(i - 2, s)
                if more:
                    dve.wait_ge(turned, i + 1)
                    make_mask(i + 2, s, (stage + 2) % STAGES, landed)

            make_mask(0, 0, 0, 16)
            make_mask(1, 1, 1, 16)
            dve.wait_ge(turned, 1)
            make_mask(2, 0, 2, 16)
            normalise(0, 0)
            step(1, 1, first=True, landed=16)
            with dve.Fori(0, (NT - 4) // STAGES) as g:
                i0 = g * STAGES + 2
                for u in range(STAGES):
                    step(i0 + u, (2 + u) % STAGES, landed=i0 * 4 + 24)
            step(NT - 2, 2, more=False)
            step(NT - 1, 3, more=False)
            mean_of_neighbours(NT - 1, 1, 3)
            add_result(NT - 2, 0)
            add_result(NT - 1, 1)
            dve.wait_ge(edges_ready, NT)
            dve.wait_ge(x_added, NT)


def at2(view, i):
    return view[bass.ds(i, 1)].rearrange("o p n -> (o p) n")


def col(view, i):
    return view[:, i:i + 1] if isinstance(i, int) else view[:, bass.ds(i, 1)]


def mixture(nc, dram, mem, sem):
    x, xln = mem["x"], mem["xln"]
    identity, ones = mem["identity"], mem["ones"]
    mean, rstd = mem["mean"], mem["rstd"]
    psum = mem["PSUM"]
    slot_x, slot_y = mem["slot_x"], mem["slot_y"]
    arena = Region(mem["ARENA"], mem["ARENA"].shape[1])
    w1 = arena.take(F32, NE, KD, I2)
    w2 = arena.take(F32, NE, KI, D)
    small = Region(mem["SMALL"], 5700)
    xT = small.take(F32, 2, KD, P)
    setup_words = small.at
    gate, up, sig = (small.take(F32, 2, I) for _ in range(3))
    tT = small.take(F32, 2, KI, P)
    tiles_words, small.at = small.at, setup_words
    bias_in = small.take(F32, I2 + D)
    act_wide = small.take(F32, 7, P)
    small.at = tiles_words
    pick = small.take(BF16, 4, P)
    pick_shared = small.take(BF16, P)
    biases = small.take(BF16, I2 + D)
    onehot = small.take(F32, NS + 1)
    onehot16 = small.take(BF16, NS + 2)
    params = small.take(F32, 7, NS + 1)
    tile_expert = small.take(I32, NS)
    slots = small.take(U32, TOPK, NT)
    weight = small.take(F32, TOPK, NT)
    stats, var, tmp = small.take(F32, NT, 6), small.take(F32, NT), small.take(F32, NT)
    act_table = small.take(F32, 8)
    soft = small.take(F32, 3, 2)
    shared_words = small.at
    xn = small.take(F32, 2, D)
    part16 = xn.rearrange("p s d -> p (s d)").bitcast(BF16)[:, 0:I2 + D]
    from_last = small.take(F32, E)
    prob, equal, first = (small.take(F32, NT, E) for _ in range(3))
    best = [small.take(F32, NT, E) for _ in range(TOPK)]
    chosen = small.take(BF16, NT, NE + 1)
    top = small.take(F32, 4, NT)
    route_end = small.at
    small.at = shared_words
    x_in = small.take(F32, 4, D)
    y_out = small.take(F32, 4, D)
    small.at = shared_words
    y_in = small.take(F32, 4, TOPK * D)
    edge = mem["const"]
    before = edge.take(BF16, P)
    ones16 = edge.take(BF16, P)
    before_e, same_e = edge.take(BF16, NB), edge.take(BF16, NB)
    gate_w, gate_b = edge.take(F32, KD, E), edge.take(F32, E, rows=1)
    steps128, tile_no = edge.take(F32, E), edge.take(F32, NS)
    expert_no = edge.take(BF16, 2)
    part_is = edge.take(F32, 4)
    count, count16, start, stop = edge.take(F32, 2), edge.take(BF16, 4), edge.take(F32, 2), edge.take(F32, 2)
    count_wide = edge.take(BF16, P)
    base = edge.take(F32, E)

    bank = [psum[:, 512 * b:512 * (b + 1)] for b in range(8)]
    ps_x = [bank[s][:, 0:KD * P].rearrange("p (k q) -> p k q", q=P) for s in range(2)]
    ps_h = [bank[2 + s][:, 0:I2] for s in range(2)]
    ps_t = [bank[4 + s][:, 0:KI * P].rearrange("p (k q) -> p k q", q=P) for s in range(2)]
    ps_y = [bank[6 + s][:, 0:D] for s in range(2)]
    ps_logits = bank[4][:, 0:NT * E].rearrange("p (t e) -> p t e", e=E)
    ps_rank = bank[5][:, 0:NT * E].rearrange("p (t e) -> p t e", e=E)
    ps_count = bank[6][0:NE, 0:1]
    ps_base, ps_start = bank[7][:, 0:E], bank[7][0:NB, 32:34]
    ps_tile = bank[6][0:1, 64:64 + NS]
    ps_params = bank[4][:, 0:7 * (NS + 1)].rearrange("p (c s) -> p c s", s=NS + 1)

    names = ("consts", "small_in", "w_shared_in", "w1_in", "w2_in", "dve_chain", "stats_done", "var_ready", "sd_ready",
             "xn_ready", "xln_ready", "x_turned", "xT_ready", "logits_done", "soft_in", "soft_out", "wide_ready",
             "shifted", "exped", "chosen_ready", "ranked", "counted", "wide_count", "started", "onehot_ready",
             "tables_done", "tables_out", "slots_ready", "sent", "ex_turned", "exT_ready", "h_summed", "swi",
             "sig_ready", "t_turned", "tT_ready", "y_summed", "z_added", "y_copied", "pick_ready", "combined",
             "combined_half")
    S = {name: sem("b_" + name) for name in names}
    x_landed = [sem(f"b_x_landed{q}") for q in range(4)]
    y_stored = [sem(f"b_y_stored{q}") for q in range(4)]
    y_landed = [sem(f"b_y_landed{q}") for q in range(4)]
    SMALL_DMAS = 4 * PARTS + 3 + 1

    def w1_rows(name, e=None):
        return dram[name].rearrange("(k p) h -> p k h", p=P) if e is None else \
            dram[name][e].rearrange("(k p) h -> p k h", p=P)

    with nc.Block() as block:

        @block.sync
        def _(sp):
            sp.dma_start(w1[:, E], dram["L0_ffn_shared_w1"].rearrange("(k p) h -> p k h", p=P)).then_inc(S["w_shared_in"], 16)
            sp.dma_start(w2[0:IH, E], dram["L0_ffn_shared_w2"].rearrange("(k p) d -> p k d", p=IH)).then_inc(S["w_shared_in"], 16)
            for e in range(E):
                sp.dma_start(w1[:, e], dram["L0_ffn_expert_w1"][e].rearrange("(k p) h -> p k h", p=P)).then_inc(S["w1_in"], 16)
                sp.dma_start(w2[0:IH, e], dram["L0_ffn_expert_w2"][e].rearrange("(k p) d -> p k d", p=IH)).then_inc(S["w2_in"], 16)
            sp.wait_ge(S["xln_ready"], NT)

            def load(n, q, shared):
                if shared:
                    sp.dma_start(x_in[:, q], at(xln, n)).then_inc(x_landed[q], 16)
                else:
                    sp.dma_start(x_in[:, q], rows(slot_x, n - NT)).then_inc(x_landed[q], 16)

            def store(n, q):
                sp.wait_ge(S["y_copied"], n - NT + 2)
                sp.dma_start(rows(slot_y, n - NT), y_out[:, q]).then_inc(y_stored[q], 16)

            sp.wait_ge(S["slots_ready"], 1)
            for n in range(4):
                load(n, n, True)
            with sp.Fori(1, NT // 4) as g:
                for q in range(4):
                    sp.wait_ge(S["ex_turned"], g * 4 + (q - 3))
                    load(g * 4 + q, q, True)
            sp.wait_ge(S["sent"], 16 * NT * TOPK)
            for n in range(NT, NT + 8):
                sp.wait_ge(S["ex_turned"], n - 3)
                load(n, n % 4, False)
                if n >= NT + 6:
                    store(n - 6, (n - 6) % 4)
            with sp.Fori((NT + 8) // 4, (NT + NS) // 4) as g:
                for q in range(4):
                    sp.wait_ge(S["ex_turned"], g * 4 + (q - 3))
                    load(g * 4 + q, q, False)
                    store(g * 4 + (q - 6), (q - 6) % 4)
            for n in range(NT + NS - 6, NT + NS):
                store(n, n % 4)
            for q in range(4):
                sp.wait_ge(y_stored[q], 16 * NS // 4)

        @block.gpsimd
        def _(pool):
            chain = Chain(pool, S["consts"])
            link = chain.link
            for view, value in ((before, 1.0), (ones16, 1.0), (before_e, 1.0), (same_e, 0.0), (chosen, 0.0), (onehot, 0.0),
                                (part_is, 0.0), (pick_shared, 1.0)):
                link(nc.gpsimd.memset(view, value))
            link(nc.gpsimd.affine_select(out=before, in_=before, compare_op=ALU.is_gt, fill=0.0, base=0,
                                         pattern=[[1, P]], channel_multiplier=-1))
            link(nc.gpsimd.affine_select(out=before_e, in_=before_e, compare_op=ALU.is_gt, fill=0.0, base=0,
                                         pattern=[[0, PARTS], [1, NE]], channel_multiplier=-1))
            link(nc.gpsimd.affine_select(out=same_e, in_=same_e, compare_op=ALU.not_equal, fill=1.0, base=0,
                                         pattern=[[0, PARTS], [1, NE]], channel_multiplier=-1))
            for part in range(PARTS):
                link(nc.gpsimd.affine_select(out=onehot[:, NS:NS + 1], in_=onehot[:, NS:NS + 1], compare_op=ALU.not_equal,
                                             fill=1.0, base=-(part * NE + E), pattern=[[0, 1]], channel_multiplier=1))
                view = part_is[:, part:part + 1]
                link(nc.gpsimd.memset(view, 1.0))
                link(nc.gpsimd.affine_select(out=view, in_=view, compare_op=ALU.is_ge, fill=0.0, base=-part * NE,
                                             pattern=[[0, 1]], channel_multiplier=1))
                link(nc.gpsimd.affine_select(out=view, in_=view, compare_op=ALU.is_ge, fill=0.0, base=(part + 1) * NE - 1,
                                             pattern=[[0, 1]], channel_multiplier=-1))
            link(nc.gpsimd.iota(from_last, pattern=[[1, E]], base=-E, channel_multiplier=0, allow_small_or_imprecise_dtypes=True))
            link(nc.gpsimd.iota(steps128, pattern=[[P, E]], base=0, channel_multiplier=0, allow_small_or_imprecise_dtypes=True))
            link(nc.gpsimd.iota(tile_no, pattern=[[1, NS]], base=0, channel_multiplier=0, allow_small_or_imprecise_dtypes=True))
            link(nc.gpsimd.iota(expert_no[:, 0:1], pattern=[[0, 1]], base=0, channel_multiplier=1, allow_small_or_imprecise_dtypes=True))
            mem["b_consts"] = chain.count
            pool.wait_ge(S["slots_ready"], 1)
            pool.wait_ge(S["xln_ready"], NT)
            for t in range(NT):
                for k in range(TOPK):
                    nc.gpsimd.indirect_dma_start(
                        out=slot_x, out_offset=bass.IndirectOffsetOnAxis(ap=slots[:, k, t:t + 1], axis=0),
                        in_=xln[:, t, :], in_offset=None).then_inc(S["sent"], 16)
            for q in range(4):
                pool.wait_ge(y_stored[q], 16 * NS // 4)
            for t in range(NT):
                if t >= 4:
                    pool.wait_ge(S["combined"], t - 3)
                for k in range(TOPK):
                    nc.gpsimd.indirect_dma_start(
                        out=y_in[:, t % 4, k * D:(k + 1) * D], out_offset=None, in_=slot_y,
                        in_offset=bass.IndirectOffsetOnAxis(ap=slots[:, k, t:t + 1], axis=0)).then_inc(y_landed[t % 4], 16)

        consts = mem["b_consts"]

        @block.scalar
        def _(act):
            def small_load(view, ap):
                act.dma_start(view, ap).then_inc(S["small_in"], 16)

            for part in range(PARTS):
                p0 = part * NE
                small_load(bias_in[p0:p0 + E, 0:I2], dram["L0_ffn_expert_b1"])
                small_load(bias_in[p0 + E:p0 + NE, 0:I2], dram["L0_ffn_shared_b1"].rearrange("(o h) -> o h", o=1))
                small_load(bias_in[p0:p0 + E, I2:I2 + D], dram["L0_ffn_expert_b2"])
                small_load(bias_in[p0 + E:p0 + NE, I2:I2 + D], dram["L0_ffn_shared_b2"].rearrange("(o h) -> o h", o=1))
            small_load(act_table[0:E, 0:5], dram["L0_ffn_expert_act"])
            small_load(act_table[E:NE, 0:5], dram["L0_ffn_shared_act"].rearrange("(o h) -> o h", o=1))
            small_load(gate_w, dram["L0_ffn_gate_w"].rearrange("(k p) e -> p k e", p=P))
            small_load(gate_b, dram["L0_ffn_gate_b"].rearrange("(o e) -> o e", o=1))
            act.wait_ge(S["var_ready"], 1)
            nc.scalar.activation(var, var, ACT.Sqrt).then_inc(S["sd_ready"], 1)

            def xT_out(s, wait, ready):
                act.wait_ge(*wait)
                nc.scalar.activation(xT[:, s], ps_x[s], ACT.Copy).then_inc(ready, 1)

            with act.Fori(0, NT // 2) as g:
                for u in range(2):
                    xT_out(u, (S["x_turned"], g * 2 + (u + 1)), S["xT_ready"])
            act.wait_ge(S["soft_in"], 1)
            nc.scalar.activation(soft[0:NE, 0], soft[0:NE, 0], ACT.Exp, scale=-1.0).then_inc(S["soft_out"], 1)
            act.wait_ge(S["shifted"], 1)
            nc.scalar.activation(prob, prob, ACT.Exp).then_inc(S["exped"], 1)
            act.wait_ge(S["soft_in"], 2)
            nc.scalar.activation(soft[0:NE, 0], soft[0:NE, 0], ACT.Ln).then_inc(S["soft_out"], 1)

            def tT_out(n, s):
                act.wait_ge(S["t_turned"], n + 1)
                nc.scalar.activation(tT[0:IH, s], ps_t[s][0:IH], ACT.Copy).then_inc(S["tT_ready"], 1)

            def y_out_copy(n, s, q, stored):
                act.wait_ge(S["y_summed"], n + 1)
                act.wait_ge(y_stored[q], stored)
                nc.scalar.activation(y_out[:, q], ps_y[s], ACT.Copy).then_inc(S["y_copied"], 1)

            def step(n, q, g, tail=True, more=True, shared=False, shared_tail=False):
                s = q % 2
                if tail:
                    tT_out(n - 2, s)
                if more:
                    xT_out(1 - s, (S["ex_turned"], n + 2), S["exT_ready"])
                act.wait_ge(S["swi"], n * 4 + 1)
                alpha = params[:, 0, NS:NS + 1] if shared else params_at(params, 0, n - NT)
                nc.scalar.activation(sig[:, s], gate[:, s], ACT.Sigmoid, scale=alpha).then_inc(S["sig_ready"], 1)
                if tail and not shared_tail:
                    y_out_copy(n - 2, s, (q - 2) % 4, (g - NT // 4) * 16)

            act.wait_ge(S["tables_out"], 2)
            xT_out(0, (S["ex_turned"], 1), S["exT_ready"])
            run_tiles(act, step)
            for n in (NT + NS - 2, NT + NS - 1):
                tT_out(n, n % 2)
                y_out_copy(n, n % 2, n % 4, (n // 4 - NT // 4) * 16)

        @block.tensor
        def _(pe):
            def turn(s, rows_, ready):
                for k in range(KD):
                    last = nc.tensor.transpose(ps_x[s][:, k, :], rows_[:, k * P:(k + 1) * P], identity)
                last.then_inc(ready, 1)

            def turn_xn(t, s):
                pe.wait_ge(S["xn_ready"], t + 1)
                turn(s, xn[:, s], S["x_turned"])

            def logits(t, s):
                pe.wait_ge(S["xT_ready"], t + 1)
                for k in range(KD):
                    nc.tensor.matmul(at(ps_logits, t), xT[:, s, k, :], gate_w[:, k, :], start=(k == 0), stop=False)
                nc.tensor.matmul(at(ps_logits, t), ones[0:1, :], gate_b, start=False, stop=True
                                 ).then_inc(S["logits_done"], 1)

            pe.wait_ge(S["small_in"], 16 * SMALL_DMAS)
            turn_xn(0, 0)
            with pe.Fori(0, NT // 2 - 1) as g:
                turn_xn(g * 2 + 1, 1)
                logits(g * 2, 0)
                turn_xn(g * 2 + 2, 0)
                logits(g * 2 + 1, 1)
            turn_xn(NT - 1, 1)
            logits(NT - 2, 0)
            logits(NT - 1, 1)
            pe.wait_ge(S["consts"], consts)
            pe.wait_ge(S["chosen_ready"], 1)
            nc.tensor.matmul(ps_rank, before, chosen[:, :, 0:E], start=True, stop=False)
            for back in range(1, NT):
                last = nc.tensor.matmul(ps_rank[:, back:NT, :], ones16, chosen[:, 0:NT - back, 0:E], start=False,
                                        stop=(back == NT - 1))
            last.then_inc(S["ranked"], 1)
            for t in range(NT):
                last = nc.tensor.matmul(ps_count, chosen[:, t, 0:NE], ones16[:, 0:1],
                                        start=(t == 0), stop=(t == NT - 1))
            last.then_inc(S["counted"], 1)
            pe.wait_ge(S["wide_count"], 1)
            nc.tensor.matmul(ps_base, count_wide[0:NE], before_e[0:NE, 0:E], start=True, stop=True)
            nc.tensor.matmul(ps_start[:, 0:1], before_e[0:NE], count16[0:NE, 0:1], start=True, stop=True)
            nc.tensor.matmul(ps_start[:, 1:2], same_e[0:NE], count16[0:NE, 0:1], start=True, stop=True
                             ).then_inc(S["started"], 1)
            pe.wait_ge(S["onehot_ready"], 1)
            pe.wait_ge(S["wide_ready"], 1)
            nc.tensor.matmul(ps_tile, expert_no[0:NE, 0:1], onehot16[0:NE, 0:NS], start=True, stop=True)
            for c in range(7):
                last = nc.tensor.matmul(ps_params[:, c, :], act_wide[0:NE, c, :], onehot[0:NE, :], start=True, stop=True)
            last.then_inc(S["tables_done"], 1)

            def turn_x(n, q, landed):
                pe.wait_ge(x_landed[q], landed)
                turn(q % 2, x_in[:, q], S["ex_turned"])

            def expand(n, q, e, shared):
                s = q % 2
                pe.wait_ge(S["exT_ready"], n + 1)
                if not shared:
                    pe.wait_ge(S["pick_ready"], n - NT + 1)
                for k in range(KD):
                    nc.tensor.matmul(ps_h[s], xT[:, s, k, :], of_expert(w1, e, k), start=(k == 0), stop=False)
                nc.tensor.matmul(ps_h[s], pick_shared[0:NB] if shared else pick[0:NB, q], biases[0:NB, 0:I2],
                                 start=False, stop=True).then_inc(S["h_summed"], 1)

            def turn_t(n, s):
                pe.wait_ge(S["swi"], n * 4 + 4)
                for k in range(KI):
                    last = nc.tensor.transpose(ps_t[s][0:IH, k, :], up[:, s, k * IH:(k + 1) * IH], identity)
                last.then_inc(S["t_turned"], 1)

            def contract(n, q, e, shared):
                s = q % 2
                pe.wait_ge(S["tT_ready"], n + 1)
                if shared:
                    pe.wait_ge(S["z_added"], n)
                else:
                    if q < 2:
                        pe.wait_ge(S["z_added"], NT + q)
                    pe.wait_ge(S["y_copied"], n - NT)
                for k in range(KI):
                    nc.tensor.matmul(ps_y[s], tT[0:IH, s, k, :], of_expert(w2, e, k, IH), start=(k == 0), stop=False)
                nc.tensor.matmul(ps_y[s], pick_shared[0:NB] if shared else pick[0:NB, q], biases[0:NB, I2:I2 + D],
                                 start=False, stop=True).then_inc(S["y_summed"], 1)

            def expert(n, shared):
                if shared:
                    return E
                return pe.value_load(tile_expert[0:1, n - NT:n - NT + 1] if isinstance(n, int)
                                     else tile_expert[0:1, bass.ds(n - NT, 1)], min_val=0, max_val=E - 1)

            def step(n, q, g, tail=True, more=True, shared=False, shared_tail=False):
                if tail:
                    turn_t(n - 2, q % 2)
                if more:
                    turn_x(n + 1, (q + 1) % 4, (g + (0 if q == 2 else 1)) * 16 + 16 if tail else 16)
                if isinstance(n, int) and n == NT:
                    pe.wait_ge(S["w1_in"], 16 * E)
                    pe.wait_ge(S["w2_in"], 16 * E)
                expand(n, q, expert(n, shared), shared)
                if tail:
                    contract(n - 2, (q - 2) % 4, expert(n - 2, shared_tail), shared_tail)

            pe.wait_ge(S["tables_out"], 2)
            pe.wait_ge(S["w_shared_in"], 32)
            pe.sem_inc(S["z_added"], 1)
            pe.sem_inc(S["y_copied"], 1)
            turn_x(0, 0, 16)
            run_tiles(pe, step)
            for n in (NT + NS - 2, NT + NS - 1):
                turn_t(n, n % 2)
                contract(n, n % 4, expert(n, False), False)

        @block.vector
        def _(dve):
            chain = Chain(dve, S["dve_chain"])
            link = chain.link
            layernorm_sums(dve, nc, x, stats, S["stats_done"])
            layernorm_spread(dve, nc, chain, stats, mean, var, tmp, S["stats_done"], NT).then_inc(S["var_ready"], 1)
            dve.wait_ge(S["sd_ready"], 1)
            link(nc.vector.reciprocal(rstd, var))

            def normalise(t, s):
                nc.vector.tensor_scalar(xn[:, s], at(x, t), col(mean, t), col(rstd, t), ALU.subtract, ALU.mult
                                        ).then_inc(S["xn_ready"], 1)
                nc.vector.tensor_scalar(at(xln, t), at(x, t), col(mean, t), col(rstd, t), ALU.subtract, ALU.mult
                                        ).then_inc(S["xln_ready"], 1)

            normalise(0, 0)
            normalise(1, 1)
            with dve.Fori(1, NT // 2) as g:
                for u in range(2):
                    dve.wait_ge(S["x_turned"], g * 2 + (u - 1))
                    normalise(g * 2 + u, u)

            dve.wait_ge(S["small_in"], 16 * SMALL_DMAS)
            raw = act_table[0:NE, 3:5]
            link(nc.vector.scalar_tensor_tensor(out=soft[0:NE, 0], in0=raw, scalar=-1.0, in1=raw, op0=ALU.mult, op1=ALU.max))
            nc.vector.tensor_scalar(soft[0:NE, 1], raw, 0.0, None, ALU.max).then_inc(S["soft_in"], 1)
            dve.wait_ge(S["soft_out"], 1)
            nc.vector.tensor_scalar(soft[0:NE, 0], soft[0:NE, 0], 1.0, None, ALU.add).then_inc(S["soft_in"], 1)

            dve.wait_ge(S["consts"], consts)
            rest = bias_in[0:NB]
            dve.wait_ge(S["x_turned"], NT)
            for part in range(PARTS):
                link(nc.vector.tensor_copy(part16[0:NB], rest))
                if part:
                    link(nc.vector.scalar_tensor_tensor(out=biases[0:NB], in0=part16[0:NB], scalar=part_is[0:NB, part:part + 1],
                                                        in1=biases[0:NB], op0=ALU.mult, op1=ALU.add))
                else:
                    link(nc.vector.tensor_scalar(biases[0:NB], part16[0:NB], part_is[0:NB, 0:1], None, ALU.mult))
                if part < PARTS - 1:
                    link(nc.vector.tensor_tensor(rest, rest, part16[0:NB], ALU.subtract))
            link(nc.vector.tensor_scalar(pick_shared[0:NB], ones16[0:NB], onehot[0:NB, NS:NS + 1], None, ALU.mult))

            def over_experts(v):
                return v.unsqueeze(2).to_broadcast([P, NT, E])

            ranks = from_last.unsqueeze(1).to_broadcast([P, NT, E])
            dve.wait_ge(S["logits_done"], NT)
            link(nc.vector.tensor_reduce(top[:, 0], ps_logits, AX, ALU.max))
            nc.vector.tensor_tensor(prob, ps_logits, over_experts(top[:, 0]), ALU.subtract).then_inc(S["shifted"], 1)
            dve.wait_ge(S["exped"], 1)
            link(nc.vector.tensor_reduce(top[:, 0], prob, AX, ALU.add))
            link(nc.vector.reciprocal(top[:, 0], top[:, 0]))
            link(nc.vector.tensor_tensor(prob, prob, over_experts(top[:, 0]), ALU.mult))
            for k in range(TOPK):
                link(nc.vector.tensor_reduce(weight[:, k], prob, AX, ALU.max))
                link(nc.vector.tensor_tensor(equal, prob, over_experts(weight[:, k]), ALU.is_equal))
                link(nc.vector.tensor_tensor(first, equal, ranks, ALU.mult))
                link(nc.vector.tensor_reduce(top[:, 1], first, AX, ALU.min))
                link(nc.vector.tensor_tensor(best[k], ranks, over_experts(top[:, 1]), ALU.is_equal))
                if k < TOPK - 1:
                    link(nc.vector.scalar_tensor_tensor(out=prob, in0=best[k], scalar=-4.0, in1=prob, op0=ALU.mult, op1=ALU.add))
            nc.vector.tensor_tensor(chosen[:, :, 0:E], best[0], best[1], ALU.add).then_inc(S["chosen_ready"], 1)
            link(nc.vector.tensor_tensor(top[:, 2], weight[:, 0], weight[:, 1], ALU.add))
            link(nc.vector.reciprocal(top[:, 2], top[:, 2]))
            for k in range(TOPK):
                link(nc.vector.tensor_tensor(weight[:, k], weight[:, k], top[:, 2], ALU.mult))
            dve.wait_ge(S["soft_out"], 2)
            link(nc.vector.tensor_tensor(act_table[0:NE, 3:5], soft[0:NE, 0], soft[0:NE, 1], ALU.add))
            link(nc.vector.tensor_scalar(act_table[0:NE, 5:7], act_table[0:NE, 3:5], -1.0, None, ALU.mult))
            nc.vector.tensor_copy(act_wide[0:NE], act_table[0:NE, 0:7].unsqueeze(2).to_broadcast([NE, 7, P])
                                  ).then_inc(S["wide_ready"], 1)

            dve.wait_ge(S["counted"], 1)
            link(nc.vector.tensor_copy(count[0:NE, 0:1], ps_count))
            link(nc.vector.tensor_scalar(first[0:NE, 0, :], steps128[0:NE], count[0:NE, 0:1], 0.0, ALU.is_lt, ALU.add,
                                         accum_out=count[0:NE, 1:2]))
            link(nc.vector.tensor_copy(count16[0:NE, 0:1], count[0:NE, 1:2]))
            nc.vector.tensor_scalar(count_wide[0:NE], ones16[0:NE], count[0:NE, 1:2], None, ALU.mult).then_inc(S["wide_count"], 1)
            dve.wait_ge(S["started"], 1)
            link(nc.vector.tensor_copy(start[0:NB], ps_start))
            link(nc.vector.tensor_tensor(stop[0:NB, 0:1], start[0:NB, 0:1], start[0:NB, 1:2], ALU.add))
            link(nc.vector.tensor_scalar(onehot[0:NB, 0:NS], tile_no[0:NB], start[0:NB, 0:1], None, ALU.is_ge))
            link(nc.vector.scalar_tensor_tensor(out=onehot[0:NB, 0:NS], in0=tile_no[0:NB], scalar=stop[0:NB, 0:1],
                                                in1=onehot[0:NB, 0:NS], op0=ALU.is_lt, op1=ALU.mult))
            nc.vector.tensor_copy(onehot16[0:NE, 0:NS], onehot[0:NE, 0:NS]).then_inc(S["onehot_ready"], 1)
            link(nc.vector.tensor_scalar(base, ps_base, float(P), None, ALU.mult))
            dve.wait_ge(S["ranked"], 1)
            link(nc.vector.tensor_tensor(first, ps_rank, base.unsqueeze(1).to_broadcast([P, NT, E]), ALU.add))
            for k in range(TOPK):
                link(nc.vector.tensor_tensor(best[k], best[k], first, ALU.mult))
                link(nc.vector.tensor_reduce(top[:, 2 + k], best[k], AX, ALU.add))
                link(nc.vector.tensor_copy(slots[:, k], top[:, 2 + k]))
            nc.vector.tensor_copy(top[:, 0], top[:, 1]).then_inc(S["slots_ready"], 1)
            dve.wait_ge(S["tables_done"], 1)
            nc.vector.tensor_copy(tile_expert[0:1], ps_tile).then_inc(S["tables_out"], 1)
            nc.vector.tensor_copy(params, ps_params).then_inc(S["tables_out"], 1)
            dve.wait_ge(S["tables_out"], 2)

            def pick_expert(n, q):
                nc.vector.tensor_scalar(pick[0:NB, q], ones16[0:NB], col(onehot[0:NB], n - NT), None, ALU.mult
                                        ).then_inc(S["pick_ready"], 1)

            def step(n, q, g, tail=True, more=True, shared=False, shared_tail=False):
                s = q % 2
                tile = NS if shared else n - NT
                if more and not (shared and not (isinstance(n, int) and n == NT - 1)):
                    dve.wait_ge(S["y_summed"], n - 2)
                    pick_expert(n + 1, (q + 1) % 4)
                dve.wait_ge(S["h_summed"], n + 1)
                h = ps_h[s].rearrange("p (i two) -> p i two", two=2)

                def c(which):
                    return params_at(params, which, tile)

                nc.vector.tensor_scalar(gate[:, s], h[:, :, 0], c(3), c(5), ALU.min, ALU.max).then_inc(S["swi"], 1)
                nc.vector.tensor_scalar(up[:, s], h[:, :, 1], c(4), c(6), ALU.min, ALU.max).then_inc(S["swi"], 1)
                dve.wait_ge(S["swi"], n * 4 + 2)
                nc.vector.scalar_tensor_tensor(out=up[:, s], in0=up[:, s], scalar=c(2), in1=gate[:, s],
                                               op0=ALU.add, op1=ALU.mult).then_inc(S["swi"], 1)
                dve.wait_ge(S["sig_ready"], n + 1)
                dve.wait_ge(S["swi"], n * 4 + 3)
                nc.vector.scalar_tensor_tensor(out=up[:, s], in0=up[:, s], scalar=c(1), in1=sig[:, s],
                                               op0=ALU.mult, op1=ALU.mult).then_inc(S["swi"], 1)
                if tail and shared_tail:
                    dve.wait_ge(S["y_summed"], n - 1)
                    nc.vector.tensor_tensor(at(x, n - 2), ps_y[s], at(x, n - 2), ALU.add).then_inc(S["z_added"], 1)

            run_tiles(dve, step)
            dve.wait_ge(S["z_added"], NT + 1)

            def combine(t, q, landed):
                dve.wait_ge(y_landed[q], landed)
                nc.vector.scalar_tensor_tensor(out=at(x, t), in0=y_in[:, q, 0:D], scalar=col(weight[:, 0], t), in1=at(x, t),
                                               op0=ALU.mult, op1=ALU.add).then_inc(S["combined_half"], 1)
                dve.wait_ge(S["combined_half"], t + 1)
                nc.vector.scalar_tensor_tensor(out=at(x, t), in0=y_in[:, q, D:2 * D], scalar=col(weight[:, 1], t), in1=at(x, t),
                                               op0=ALU.mult, op1=ALU.add).then_inc(S["combined"], 1)

            with dve.Fori(0, NT // 4) as g:
                for q in range(4):
                    combine(g * 4 + q, q, g * 32 + 32)
            dve.wait_ge(S["combined"], NT)


def run_tiles(engine, step):
    for n in (0, 1):
        step(n, n, 0, tail=False, shared=True)
    with engine.Fori(0, (NT - 4) // 4) as g:
        for u in range(4):
            step(g * 4 + (2 + u), (2 + u) % 4, g, shared=True, shared_tail=True)
    for n in range(NT - 2, NT + 2):
        step(n, n % 4, (n - 2) // 4, shared=n < NT, shared_tail=True)
    with engine.Fori(NT // 4, (NT + NS - 4) // 4) as g:
        for u in range(4):
            step(g * 4 + (2 + u), (2 + u) % 4, g)
    for n in (NT + NS - 2, NT + NS - 1):
        step(n, n % 4, (n - 2) // 4, more=n < NT + NS - 1)


def rows(view, i):
    tiles = view.rearrange("(t p) d -> t p d", p=P)
    return tiles[i] if isinstance(i, int) else tiles[bass.ds(i, 1)].rearrange("o p d -> (o p) d")


def params_at(params, which, tile):
    return params[:, which, tile:tile + 1] if isinstance(tile, int) else params[:, which, bass.ds(tile, 1)]


def of_expert(w, e, k, rows_=P):
    if isinstance(e, int):
        return w[0:rows_, e, k, :]
    return w[0:rows_, bass.ds(e, 1), k, :].squeeze(1)


def attention(nc, dram, mem, sem):
    x, xln, edges = mem["x"], mem["xln"], mem["edges"]
    identity = mem["identity"]
    mean, rstd = mem["mean"], mem["rstd"]
    psum = mem["PSUM"]
    H = 128
    SLOPE = 0.01
    CHUNK = 4
    CHUNKS = NJ // CHUNK
    arena = Region(mem["ARENA"], mem["ARENA"].shape[1])
    edge_in = arena.take(BF16, 2, N)
    s_row, l_row, p_row = arena.take(F32, 2, N), arena.take(F32, 2, N), arena.take(F32, 2, N)
    pT = arena.take(F32, CHUNKS, CHUNK * P)
    f2 = arena.take(F32, N)
    small = Region(mem["SMALL"], 5700)
    w1, w23 = small.take(F32, D), small.take(F32, 2)
    b2, b3 = small.take(F32, 2), small.take(F32, 2)
    u = small.take(F32, KD, 2)
    u3_wide = small.take(F32, KD, P)
    stats, var, tmp = small.take(F32, NT, 6), small.take(F32, NT), small.take(F32, NT)
    xn = small.take(F32, 2, D)
    xT = small.take(F32, 2, KD, P)
    f1, f1_low, total, inverse = (small.take(F32, NT) for _ in range(4))
    largest, minus, bound, waited = (small.take(F32, 2) for _ in range(4))
    vals = small.take(F32, 2, D)

    bank = [psum[:, 512 * b:512 * (b + 1)] for b in range(8)]
    ps_u = bank[6][:, 0:2 * KD].rearrange("p (k c) -> p k c", c=2)
    ps_x = [bank[s][:, 0:KD * P].rearrange("p (k q) -> p k q", q=P) for s in range(2)]
    ps_f1 = [bank[2 + s][:, 0:1] for s in range(2)]
    ps_f2 = [bank[4 + s][:, 0:P] for s in range(2)]
    ps_sum = [bank[6 + s][:, 0:D] for s in range(2)]

    names = ("w_in", "dve_chain", "stats_done", "var_ready", "sd_ready", "u_summed", "u_ready", "xn_ready", "xln_ready",
             "x_turned", "xT_ready", "f1_summed", "f2_summed", "f1_out", "f2_out", "f1_low_ready", "s_ready", "minus_ready",
             "low_ready", "l_ready", "p_ready", "p_turned", "pT_even", "pT_odd", "summed", "inverse_ready", "vals_ready",
             "x_added", "bound_ready")
    S = {name: sem("c_" + name) for name in names}
    edge_landed = [sem(f"c_edge_landed{s}") for s in range(2)]

    with nc.Block() as block:

        @block.sync
        def _(sp):
            sp.dma_start(w1, dram["L1_gnn_W1"]).then_inc(S["w_in"], 16)
            for c, name in enumerate(("L1_gnn_w2", "L1_gnn_w3")):
                sp.dma_start(w23[:, c:c + 1], dram[name].rearrange("(p o) -> p o", o=1),
                             allow_slow_non_contiguous=True).then_inc(S["w_in"], 16)
            for view, name in ((b2, "L1_gnn_b2"), (b3, "L1_gnn_b3")):
                sp.dma_start(view[:, 0:1], dram[name].rearrange("(p o) -> p o", o=1).to_broadcast([P, 1]),
                             allow_slow_non_contiguous=True).then_inc(S["w_in"], 16)
            for i in range(2):
                sp.dma_start(edge_in[:, i], edges[:, i]).then_inc(edge_landed[i], 16)
            with sp.Fori(1, NT // 2) as g:
                for q in range(2):
                    sp.wait_ge(S["s_ready"], g * 2 + (q - 1))
                    sp.dma_start(edge_in[:, q], at(edges, g * 2 + q)).then_inc(edge_landed[q], 16)

        @block.scalar
        def _(act):
            act.wait_ge(S["var_ready"], 1)
            nc.scalar.activation(var, var, ACT.Sqrt).then_inc(S["sd_ready"], 1)

            def xT_out(t, s):
                act.wait_ge(S["x_turned"], t + 1)
                nc.scalar.activation(xT[:, s], ps_x[s], ACT.Copy).then_inc(S["xT_ready"], 1)

            def f_out(t, s):
                act.wait_ge(S["f1_summed"], t + 1)
                nc.scalar.activation(col(f1, t), ps_f1[s], ACT.Identity, bias=b2[:, 0:1]).then_inc(S["f1_out"], 1)
                act.wait_ge(S["f2_summed"], t + 1)
                where = f2[:, bass.ds(t * P, P)] if not isinstance(t, int) else f2[:, t * P:(t + 1) * P]
                nc.scalar.activation(where, ps_f2[s], ACT.Identity, bias=b3[:, 0:1]).then_inc(S["f2_out"], 1)

            xT_out(0, 0)
            act.wait_ge(S["w_in"], 16 * 5)
            with act.Fori(0, NT // 2 - 1) as g:
                xT_out(g * 2 + 1, 1)
                f_out(g * 2, 0)
                xT_out(g * 2 + 2, 0)
                f_out(g * 2 + 1, 1)
            xT_out(NT - 1, 1)
            f_out(NT - 2, 0)
            f_out(NT - 1, 1)

            def low(i, s):
                act.wait_ge(S["s_ready"], i + 1)
                nc.scalar.activation(l_row[:, s], s_row[:, s], ACT.Identity, bias=col(f1_low, i), scale=SLOPE
                                     ).then_inc(S["low_ready"], 1)

            def exponent(i, s):
                act.wait_ge(S["l_ready"], i + 1)
                act.wait_ge(S["minus_ready"], i + 1)
                nc.scalar.activation(p_row[:, s], l_row[:, s], ACT.Exp, bias=minus[:, s:s + 1],
                                     accum_out=col(total, i)).then_inc(S["p_ready"], 1)

            def turned_out(i, c):
                act.wait_ge(S["p_turned"], i * CHUNKS + (c + 1))
                nc.scalar.activation(pT[:, c], bank[c], ACT.Copy).then_inc(S["pT_even"], 1)

            def step(i, s, more=2):
                turned_out(i, 0)
                turned_out(i, 2)
                if more >= 1:
                    exponent(i + 1, 1 - s)
                if more >= 2:
                    act.wait_ge(S["p_ready"], i + 1)
                    low(i + 2, s)

            act.wait_ge(S["f1_low_ready"], 1)
            low(0, 0)
            low(1, 1)
            exponent(0, 0)
            step(0, 0)
            with act.Fori(0, (NT - 4) // 2) as g:
                for q in range(2):
                    step(g * 2 + (1 + q), (1 + q) % 2)
            step(NT - 3, 1)
            step(NT - 2, 0, more=1)
            step(NT - 1, 1, more=0)

        @block.tensor
        def _(pe):
            pe.wait_ge(S["w_in"], 16 * 5)
            for k in range(KD):
                last = nc.tensor.matmul(ps_u[:, k, :], w1[:, k * P:(k + 1) * P], w23, start=True, stop=True)
            last.then_inc(S["u_summed"], 1)

            def turn_x(t, s):
                pe.wait_ge(S["xn_ready"], t + 1)
                for k in range(KD):
                    last = nc.tensor.transpose(ps_x[s][:, k, :], xn[:, s, k * P:(k + 1) * P], identity)
                last.then_inc(S["x_turned"], 1)

            def project(t, s):
                pe.wait_ge(S["xT_ready"], t + 1)
                pe.wait_ge(S["f2_out"], t)
                for k in range(KD):
                    last = nc.tensor.matmul(ps_f1[s], xT[:, s, k, :], u[:, k, 0:1], start=(k == 0), stop=(k == KD - 1))
                last.then_inc(S["f1_summed"], 1)
                for k in range(KD):
                    last = nc.tensor.matmul(ps_f2[s], u3_wide[:, k, :], xT[:, s, k, :], start=(k == 0), stop=(k == KD - 1))
                last.then_inc(S["f2_summed"], 1)

            turn_x(0, 0)
            pe.wait_ge(S["u_ready"], 2)
            with pe.Fori(0, NT // 2 - 1) as g:
                turn_x(g * 2 + 1, 1)
                project(g * 2, 0)
                turn_x(g * 2 + 2, 0)
                project(g * 2 + 1, 1)
            turn_x(NT - 1, 1)
            project(NT - 2, 0)
            project(NT - 1, 1)

            def turn(i, s, c):
                pe.wait_ge(S["p_ready"], i + 1)
                for b in range(CHUNK):
                    j = c * CHUNK + b
                    last = nc.tensor.transpose(bank[c][:, b * P:(b + 1) * P], p_row[:, s, j * P:(j + 1) * P], identity)
                last.then_inc(S["p_turned"], 1)

            def weigh(i, s, c):
                if c % 2:
                    pe.wait_ge(S["pT_odd"], i * 2 + (c // 2 + 1))
                else:
                    pe.wait_ge(S["pT_even"], i * 2 + (c // 2 + 1))
                if c == 0:
                    pe.wait_ge(S["vals_ready"], i)
                for b in range(CHUNK):
                    j = c * CHUNK + b
                    last = nc.tensor.matmul(ps_sum[s], pT[:, c, b * P:(b + 1) * P], xln[:, j, :], start=(j == 0), stop=(j == NJ - 1))
                if c == CHUNKS - 1:
                    last.then_inc(S["summed"], 1)

            def step(i, s, more=True):
                turn(i, s, 2)
                weigh(i, s, 0)
                turn(i, s, 3)
                weigh(i, s, 1)
                weigh(i, s, 2)
                if more:
                    turn(i + 1, 1 - s, 0)
                    turn(i + 1, 1 - s, 1)
                weigh(i, s, 3)

            pe.sem_inc(S["vals_ready"], 1)
            pe.wait_ge(S["f1_out"], NT)
            pe.wait_ge(S["f2_out"], NT)
            turn(0, 0, 0)
            turn(0, 0, 1)
            step(0, 0)
            with pe.Fori(0, (NT - 2) // 2) as g:
                for q in range(2):
                    step(g * 2 + (1 + q), (1 + q) % 2)
            step(NT - 1, 1, more=False)

        @block.vector
        def _(dve):
            chain = Chain(dve, S["dve_chain"])
            link = chain.link
            layernorm_sums(dve, nc, x, stats, S["stats_done"])
            layernorm_spread(dve, nc, chain, stats, mean, var, tmp, S["stats_done"], NT).then_inc(S["var_ready"], 1)
            dve.wait_ge(S["u_summed"], 1)
            nc.vector.tensor_copy(u, ps_u).then_inc(S["u_ready"], 1)
            dve.wait_ge(S["u_ready"], 1)
            nc.vector.tensor_copy(u3_wide, u[:, :, 1:2].to_broadcast([P, KD, P])).then_inc(S["u_ready"], 1)
            dve.wait_ge(S["sd_ready"], 1)
            link(nc.vector.reciprocal(rstd, var))

            def normalise(t, s):
                nc.vector.tensor_scalar(xn[:, s], at(x, t), col(mean, t), col(rstd, t), ALU.subtract, ALU.mult
                                        ).then_inc(S["xn_ready"], 1)
                nc.vector.tensor_scalar(at(xln, t), at(x, t), col(mean, t), col(rstd, t), ALU.subtract, ALU.mult
                                        ).then_inc(S["xln_ready"], 1)

            normalise(0, 0)
            normalise(1, 1)
            with dve.Fori(1, NT // 2) as g:
                for q in range(2):
                    dve.wait_ge(S["x_turned"], g * 2 + (q - 1))
                    normalise(g * 2 + q, q)
            dve.wait_ge(S["xln_ready"], NT)
            dve.wait_ge(S["f1_out"], NT)
            nc.vector.tensor_scalar(f1_low, f1, SLOPE, None, ALU.mult).then_inc(S["f1_low_ready"], 1)
            dve.wait_ge(S["f2_out"], NT)

            def masked(i, s, landed):
                dve.wait_ge(S["stats_done"], NT)
                dve.wait_ge(edge_landed[s], landed)
                if not (isinstance(i, int) and i < 2):
                    dve.wait_ge(S["l_ready"], i - 1)
                nc.vector.memset(waited[:, s:s + 1], 0.0)
                nc.vector.tensor_tensor_reduce(out=s_row[:, s], in0=f2, in1=edge_in[:, s], scale=1.0, scalar=-3.0e38,
                                               op0=ALU.add, op1=ALU.max, accum_out=largest[:, s:s + 1]
                                               ).then_inc(S["s_ready"], 1)
                dve.wait_ge(S["s_ready"], i + 1)
                nc.vector.tensor_scalar(bound[:, s:s + 1], largest[:, s:s + 1], col(f1, i), -1.0, ALU.add, ALU.mult
                                        ).then_inc(S["bound_ready"], 1)
                dve.wait_ge(S["bound_ready"], i + 1)
                nc.vector.scalar_tensor_tensor(out=minus[:, s:s + 1], in0=bound[:, s:s + 1], scalar=SLOPE,
                                               in1=bound[:, s:s + 1], op0=ALU.mult, op1=ALU.min).then_inc(S["minus_ready"], 1)

            def leaky(i, s):
                dve.wait_ge(S["low_ready"], i + 1)
                nc.vector.scalar_tensor_tensor(out=l_row[:, s], in0=s_row[:, s], scalar=col(f1, i), in1=l_row[:, s],
                                               op0=ALU.add, op1=ALU.max).then_inc(S["l_ready"], 1)

            def turned_out(i, c):
                dve.wait_ge(S["p_turned"], i * CHUNKS + (c + 1))
                nc.vector.tensor_copy(pT[:, c], bank[c]).then_inc(S["pT_odd"], 1)

            def finish(i, s):
                dve.wait_ge(S["summed"], i + 1)
                dve.wait_ge(S["x_added"], i)
                dve.wait_ge(S["f2_out"], NT)
                nc.vector.reciprocal(col(inverse, i), col(total, i)).then_inc(S["inverse_ready"], 1)
                dve.wait_ge(S["inverse_ready"], i + 1)
                nc.vector.tensor_scalar(vals[:, s], ps_sum[s], col(inverse, i), 0.0, ALU.mult, ALU.max).then_inc(S["vals_ready"], 1)
                dve.wait_ge(S["vals_ready"], i + 2)
                nc.vector.tensor_tensor(at(x, i), vals[:, s], at(x, i), ALU.add).then_inc(S["x_added"], 1)

            def step(i, s, more=2, landed=None, first=False):
                turned_out(i, 1)
                if more >= 1:
                    leaky(i + 1, 1 - s)
                turned_out(i, 3)
                if more >= 2:
                    dve.wait_ge(S["p_ready"], i + 1)
                    masked(i + 2, s, landed)
                if not first:
                    finish(i - 1, 1 - s)

            masked(0, 0, 16)
            masked(1, 1, 16)
            leaky(0, 0)
            step(0, 0, landed=32, first=True)
            with dve.Fori(0, (NT - 4) // 2) as g:
                for q in range(2):
                    step(g * 2 + (1 + q), (1 + q) % 2, landed=(g + (1 + (3 + q) // 2)) * 16)
            step(NT - 3, 1, landed=NT // 2 * 16)
            step(NT - 2, 0, more=1)
            step(NT - 1, 1, more=0)
            finish(NT - 1, 1)
            dve.wait_ge(S["x_added"], NT)



def fp8_product(nc, dram, mem, sem):
    x = mem["x"]
    identity, identity16, ones = mem["identity"], mem["identity16"], mem["ones"]
    mean, rstd = mem["mean"], mem["rstd"]
    psum = mem["PSUM"]
    arena = Region(mem["ARENA"], mem["ARENA"].shape[1])
    PAIR = 2
    NPAIR = NT // PAIR
    weight, w_clip = arena.take(F32, KD * D), arena.take(F32, KD * D)
    w_exp, w_c, w_sum = (arena.take(F32, KD * D) for _ in range(3))
    w8 = arena.take(BF16, KD, D)
    v, clip, exponent_, c_, sum_ = (arena.take(F32, 2, PAIR * D) for _ in range(5))
    q8 = arena.take(BF16, 2, PAIR * D)
    qT = arena.take(BF16, 2, PAIR * KD, P)
    result = arena.take(F32, 2, PAIR, D)
    small = Region(mem["SMALL"], 5700)
    stats, var, tmp = small.take(F32, NT, 6), small.take(F32, NT), small.take(F32, NT)
    high, low = small.take(F32, NT), small.take(F32, NT)
    w_high = small.take(F32, 2)
    largest = small.take(F32, 2)
    largest_row = small.take(F32, 2)
    amax, scale8, unscale = (small.take(F32, 2) for _ in range(3))
    out_scale = small.take(F32, 2)
    slope, offset = small.take(F32, NT), small.take(F32, NT)
    MAGIC = 1.5 * 2.0 ** (23 - 3)
    LEAST = 2.0 ** -6

    bank = [psum[:, 512 * b:512 * (b + 1)] for b in range(8)]
    ps_rows = bank[6][0:1, 0:2 * P].rearrange("p (c q) -> p c q", q=P)
    ps_wide = bank[7][:, 0:2]
    ps_q = [bank[s][:, 0:PAIR * KD * P // 2].bitcast(BF16).rearrange("p (b q) -> p b q", q=P) for s in range(2)]
    ps_out = [bank[2 + s] for s in range(2)]

    names = ("w_in", "dve_chain", "stats_done", "var_ready", "sd_ready", "largest_ready", "rows_turned", "row_ready",
             "wide_ready", "scales_ready", "v_ready", "rounded", "q_ready", "q_turned", "qT_ready", "summed", "result_ready")
    S = {name: sem("d_" + name) for name in names}
    stored = [sem(f"d_stored{s}") for s in range(2)]
    out_pairs = mem["out"].rearrange("(h t p) d -> h p t d", t=PAIR, p=P)

    with nc.Block() as block:

        @block.sync
        def _(sp):
            sp.dma_start(weight.rearrange("p (k d) -> p k d", d=D), dram["L1_ffn_weight"].rearrange("(k p) d -> p k d", p=P)
                         ).then_inc(S["w_in"], 16)
            with sp.Fori(0, NPAIR // 2) as g:
                for s in range(2):
                    sp.wait_ge(S["result_ready"], g * 2 + (s + 1))
                    sp.dma_start(out_pairs[bass.ds(g * 2 + s, 1)].rearrange("o p t d -> (o p) t d"), result[:, s]
                                 ).then_inc(stored[s], 16)
            for s in range(2):
                sp.wait_ge(stored[s], 16 * NPAIR // 2)

        @block.scalar
        def _(act):
            act.wait_ge(S["var_ready"], 1)
            nc.scalar.activation(var, var, ACT.Sqrt).then_inc(S["sd_ready"], 1)

            def scaled(h, s):
                for t in range(PAIR):
                    nc.scalar.activation(v[:, s, t * D:(t + 1) * D], at(x, h * PAIR + t), ACT.Identity,
                                         bias=col(offset, h * PAIR + t), scale=col(slope, h * PAIR + t)
                                         ).then_inc(S["v_ready"], 1)

            def qT_out(h, s):
                act.wait_ge(S["q_turned"], h + 1)
                nc.scalar.activation(qT[:, s], ps_q[s], ACT.Copy).then_inc(S["qT_ready"], 1)

            act.wait_ge(S["scales_ready"], 1)
            scaled(0, 0)
            with act.Fori(0, NPAIR // 2 - 1) as g:
                for s in range(2):
                    act.wait_ge(S["rounded"], (g * 2 + s) * 4)
                    scaled(g * 2 + (s + 1), 1 - s)
                    qT_out(g * 2 + s, s)
            act.wait_ge(S["rounded"], (NPAIR - 2) * 4)
            scaled(NPAIR - 1, 1)
            qT_out(NPAIR - 2, 0)
            qT_out(NPAIR - 1, 1)

        @block.tensor
        def _(pe):
            pe.wait_ge(S["largest_ready"], 1)
            for c in range(2):
                last = nc.tensor.transpose(ps_rows[:, c, :], largest[:, c:c + 1], identity)
            last.then_inc(S["rows_turned"], 1)
            pe.wait_ge(S["row_ready"], 1)
            nc.tensor.matmul(ps_wide, ones[0:1, :], largest_row[0:1], start=True, stop=True).then_inc(S["wide_ready"], 1)

            def turn(h, s):
                pe.wait_ge(S["q_ready"], h + 2)
                for b in range(PAIR * KD):
                    last = nc.tensor.transpose(ps_q[s][:, b, :], q8[:, s, b * P:(b + 1) * P], identity16)
                last.then_inc(S["q_turned"], 1)

            def product(h, s):
                pe.wait_ge(S["qT_ready"], h + 1)
                pe.wait_ge(S["result_ready"], h)
                for t in range(PAIR):
                    for k in range(KD):
                        last = nc.tensor.matmul(ps_out[s][:, t * D:(t + 1) * D], qT[:, s, t * KD + k, :], w8[:, k, :],
                                                start=(k == 0), stop=(k == KD - 1))
                last.then_inc(S["summed"], 1)

            turn(0, 0)
            with pe.Fori(0, NPAIR // 2 - 1) as g:
                turn(g * 2 + 1, 1)
                product(g * 2, 0)
                turn(g * 2 + 2, 0)
                product(g * 2 + 1, 1)
            turn(NPAIR - 1, 1)
            product(NPAIR - 2, 0)
            product(NPAIR - 1, 1)

        @block.vector
        def _(dve):
            chain = Chain(dve, S["dve_chain"])
            link = chain.link
            layernorm_sums(dve, nc, x, stats, S["stats_done"])
            layernorm_spread(dve, nc, chain, stats, mean, var, tmp, S["stats_done"], NT).then_inc(S["var_ready"], 1)
            link(nc.vector.tensor_reduce(high, x, AX, ALU.max))
            link(nc.vector.tensor_reduce(low, x, AX, ALU.min))
            dve.wait_ge(S["w_in"], 16)
            link(nc.vector.tensor_reduce(w_high[:, 0:1], weight, AX, ALU.max))
            link(nc.vector.tensor_reduce(w_high[:, 1:2], weight, AX, ALU.min))
            link(nc.vector.scalar_tensor_tensor(out=largest[:, 1:2], in0=w_high[:, 1:2], scalar=-1.0, in1=w_high[:, 0:1],
                                                op0=ALU.mult, op1=ALU.max))
            dve.wait_ge(S["sd_ready"], 1)
            link(nc.vector.reciprocal(rstd, var))
            for view in (high, low):
                link(nc.vector.tensor_tensor(view, view, mean, ALU.subtract))
                link(nc.vector.tensor_tensor(view, view, rstd, ALU.mult))
            link(nc.vector.scalar_tensor_tensor(out=high, in0=low, scalar=-1.0, in1=high, op0=ALU.mult, op1=ALU.max))
            nc.vector.tensor_reduce(largest[:, 0:1], high, AX, ALU.max).then_inc(S["largest_ready"], 1)
            dve.wait_ge(S["rows_turned"], 1)
            nc.vector.tensor_reduce(largest_row[0:1], ps_rows, AX, ALU.max).then_inc(S["row_ready"], 1)
            dve.wait_ge(S["wide_ready"], 1)
            link(nc.vector.tensor_scalar(amax, ps_wide, 1e-12, None, ALU.max))
            link(nc.vector.reciprocal(scale8, amax))
            link(nc.vector.tensor_scalar(scale8, scale8, FP8_MAX, None, ALU.mult))
            link(nc.vector.reciprocal(unscale, scale8))
            link(nc.vector.tensor_tensor(out_scale[:, 0:1], unscale[:, 0:1], unscale[:, 1:2], ALU.mult))
            link(nc.vector.tensor_scalar(slope, rstd, scale8[:, 0:1], None, ALU.mult))
            nc.vector.scalar_tensor_tensor(out=offset, in0=mean, scalar=-1.0, in1=slope, op0=ALU.mult, op1=ALU.mult
                                           ).then_inc(S["scales_ready"], 1)
            I32_ = I32
            link(nc.vector.tensor_scalar(w_clip, weight, scale8[:, 1:2], FP8_MAX, ALU.mult, ALU.min))
            link(nc.vector.tensor_scalar(w_clip, w_clip, -FP8_MAX, None, ALU.max))
            link(nc.vector.tensor_scalar(w_exp.bitcast(I32_), w_clip.bitcast(I32_), 0x7F800000, None, ALU.bitwise_and))
            link(nc.vector.tensor_scalar(w_c, w_exp, LEAST, MAGIC, ALU.max, ALU.mult))
            link(nc.vector.tensor_tensor(w_sum, w_clip, w_c, ALU.add))
            nc.vector.tensor_tensor(w8.rearrange("p k d -> p (k d)"), w_sum, w_c, ALU.subtract).then_inc(S["q_ready"], 1)

            def round_pair(h, s):
                dve.wait_ge(S["v_ready"], (h + 1) * PAIR)
                nc.vector.tensor_scalar(clip[:, s], v[:, s], FP8_MAX, -FP8_MAX, ALU.min, ALU.max).then_inc(S["rounded"], 1)
                dve.wait_ge(S["rounded"], h * 4 + 1)
                nc.vector.tensor_scalar(exponent_[:, s].bitcast(I32_), clip[:, s].bitcast(I32_), 0x7F800000, None,
                                        ALU.bitwise_and).then_inc(S["rounded"], 1)
                dve.wait_ge(S["rounded"], h * 4 + 2)
                nc.vector.tensor_scalar(c_[:, s], exponent_[:, s], LEAST, MAGIC, ALU.max, ALU.mult).then_inc(S["rounded"], 1)
                dve.wait_ge(S["rounded"], h * 4 + 3)
                nc.vector.tensor_tensor(sum_[:, s], clip[:, s], c_[:, s], ALU.add).then_inc(S["rounded"], 1)
                dve.wait_ge(S["rounded"], h * 4 + 4)
                nc.vector.tensor_tensor(q8[:, s], sum_[:, s], c_[:, s], ALU.subtract).then_inc(S["q_ready"], 1)

            def finish(h, s, stored_):
                dve.wait_ge(S["summed"], h + 1)
                dve.wait_ge(stored[s], stored_)
                nc.vector.scalar_tensor_tensor(out=result[:, s].rearrange("p t d -> p (t d)"), in0=ps_out[s],
                                               scalar=out_scale[:, 0:1], in1=pair_of(x, h), op0=ALU.mult, op1=ALU.add
                                               ).then_inc(S["result_ready"], 1)

            round_pair(0, 0)
            round_pair(1, 1)
            finish(0, 0, 0)
            with dve.Fori(1, NPAIR // 2) as g:
                for s in range(2):
                    dve.wait_ge(S["q_turned"], g * 2 + (s - 1))
                    dve.wait_ge(S["q_ready"], g * 2 + (s + 1))
                    round_pair(g * 2 + s, s)
                    finish(g * 2 + (s - 1), 1 - s, (g - (1 - s)) * 16)
            finish(NPAIR - 1, 1, (NPAIR // 2 - 1) * 16)


def pair_of(view, h):
    if isinstance(h, int):
        return view[:, 2 * h:2 * h + 2].rearrange("p t d -> p (t d)")
    return view[:, bass.ds(h * 2, 2)].rearrange("p t d -> p (t d)")


def lay_out(inputs):
    return {name: np.ascontiguousarray(inputs[name]) for name in inputs}


def kernel(**inputs):
    import concourse.bacc as bacc
    from concourse.bass_utils import run_bass_kernel_spmd

    nc = bacc.Bacc("TRN2", target_bir_lowering=False, num_devices=1)
    arrays = lay_out(inputs)
    build(nc, arrays)
    r = run_bass_kernel_spmd(nc, [arrays], core_ids=[0])
    return r.results[0]["out_0_dram"]
```

```python
from contextlib import ExitStack

import numpy as np

import concourse.bass as bass
from concourse import mybir

F32 = mybir.dt.float32
BF16 = mybir.dt.bfloat16
FP16 = mybir.dt.float16
I32 = mybir.dt.int32
U32 = mybir.dt.uint32
ALU = mybir.AluOpType
ACT = mybir.ActivationFunctionType
AX = mybir.AxisListType.X

P = 128
N = 2048
D = 256
NT = N // P
KD = D // P
NJ = N // P
E = 16
NE = E + 1
I2 = 384
I = I2 // 2
KI = 2
IH = I // KI
TOPK = 2
NS = N * TOPK // P + E
ZERO_ROWS = 8
SPARE = ZERO_ROWS * P
PARTS = 3
NB = NE * PARTS
EPS = 1e-5
SCALE16 = 2048.0
NO_EDGE = -float(2 ** 30)
FP8_MAX = 448.0
SMALL_WORDS = 5660

X_AT = N // P * D


class Region:

    def __init__(self, tensor, words):
        self.tensor, self.words, self.at = tensor, words, 0

    def take(self, dtype, *shape, rows=P):
        size = int(np.prod(shape))
        words = -(-size * (2 if dtype in (BF16, FP16) else 4) // 4)
        words += words % 2
        assert self.at + words <= self.words, (self.at, words, self.words)
        view = self.tensor[0:rows, self.at:self.at + words]
        self.at += words
        if dtype != F32:
            view = view.bitcast(dtype)
        view = view[:, 0:size]
        if len(shape) == 2:
            view = view.rearrange("p (a b) -> p a b", b=shape[1])
        elif len(shape) == 3:
            view = view.rearrange("p (a b c) -> p a b c", b=shape[1], c=shape[2])
        return view


class Chain:

    def __init__(self, engine, semaphore):
        self.engine, self.semaphore, self.count = engine, semaphore, 0

    def link(self, instruction):
        self.count += 1
        instruction.then_inc(self.semaphore, 1)
        self.engine.wait_ge(self.semaphore, self.count)


def at(view, i):
    if isinstance(i, int):
        return view[:, i]
    one = view[:, bass.ds(i, 1)]
    return one.squeeze(1) if len(one.shape) > 2 else one


def build(nc, a, stop="D"):
    ctx = ExitStack()
    with ctx:
        _build(nc, a, stop, ctx)


def _build(nc, a, stop, ctx):
    dram = {}
    for name, v in a.items():
        dram[name] = nc.dram_tensor(name, v.shape, mybir.dt.from_np(v.dtype), kind="ExternalInput").ap()
    out = nc.dram_tensor("out_0_dram", (N, D), F32, kind="ExternalOutput").ap()
    slot_x = nc.dram_tensor("slot_x", (NS * P, D + 1), F32, kind="Internal").ap()
    token_y = nc.dram_tensor("token_y", (SPARE + TOPK * N, D), F32, kind="Internal").ap()

    def sb(name, words):
        return ctx.enter_context(nc.sbuf_tensor(name, [P, words], F32))

    ARENA_WORDS = NE * KD * I2 + NE * KI * D
    mem = {
        "X": sb("X", NT * D), "XLN": sb("XLN", NT * (D + 2)), "EDGES": sb("EDGES", NT * N // 2),
        "ARENA": sb("ARENA", ARENA_WORDS), "SMALL": sb("SMALL", SMALL_WORDS),
        "PSUM": ctx.enter_context(nc.psum_tensor("PSUM", [P, 8 * 512], F32)),
        "slot_x": slot_x, "token_y": token_y, "out": out,
    }
    mem["x"] = mem["X"][:, :].rearrange("p (t d) -> p t d", d=D)
    mem["xln_row"] = mem["XLN"][:, :].rearrange("p (t d) -> p t d", d=D + 2)
    mem["xln"] = mem["xln_row"][:, :, 0:D]
    mem["edges"] = mem["EDGES"][:, :].bitcast(BF16).rearrange("p (t n) -> p t n", n=N)
    CONST_WORDS = 1176
    mem["CONST"] = sb("CONST", CONST_WORDS)
    mem["const"] = const = Region(mem["CONST"], CONST_WORDS)
    mem["identity"] = const.take(F32, P)
    mem["identity16"] = const.take(BF16, P)
    mem["ones"] = const.take(F32, P)
    mem["mean"] = const.take(F32, NT)
    mem["rstd"] = const.take(F32, NT)
    mem["stats"] = const.take(F32, NT, 6)
    mem["most"], mem["least"] = const.take(F32, NT), const.take(F32, NT)
    def sem(name):
        return ctx.enter_context(nc.semaphore(name))

    mem["gate_w"], mem["gate_b"] = const.take(F32, KD, E), const.take(F32, E, rows=1)
    mem["gate_in"] = sem("gate_in")

    mean_aggregate(nc, dram, mem, sem)
    if stop == "A":
        return
    mixture(nc, dram, mem, sem)
    if stop == "B":
        return
    attention(nc, dram, mem, sem)
    if stop == "C":
        return
    fp8_product(nc, dram, mem, sem)


def layernorm_sums(dve, nc, x, stats, done, first=0, last=NT):
    with dve.Fori(first, last) as t:
        nc.vector.bn_stats(at(stats, t), at(x, t)).then_inc(done, 1)


def layernorm_spread(dve, nc, chain, stats, mean, var, tmp):
    me, mo, se, so = stats[:, :, 1], stats[:, :, 4], stats[:, :, 2], stats[:, :, 5]
    chain.link(nc.vector.tensor_tensor(mean, me, mo, ALU.add))
    chain.link(nc.vector.tensor_tensor(tmp, me, mo, ALU.subtract))
    chain.link(nc.vector.tensor_tensor(var, se, so, ALU.add))
    chain.link(nc.vector.tensor_scalar(mean, mean, 0.5, None, ALU.mult))
    chain.link(nc.vector.scalar_tensor_tensor(out=tmp, in0=tmp, scalar=0.25, in1=tmp, op0=ALU.mult, op1=ALU.mult))
    chain.link(nc.vector.tensor_scalar(var, var, 1.0 / D, EPS, ALU.mult, ALU.add))
    return nc.vector.tensor_tensor(var, var, tmp, ALU.add)



def mean_aggregate(nc, dram, mem, sem):
    x, edges = mem["x"], mem["edges"]
    identity, identity16, ones = mem["identity"], mem["identity16"], mem["ones"]
    mean, rstd = mem["mean"], mem["rstd"]
    psum = mem["PSUM"]
    arena = Region(mem["ARENA"], mem["ARENA"].shape[1])
    STAGES = 4
    adj_in = arena.take(I32, STAGES, N)
    ln16 = arena.take(FP16, NT, 2 * D)
    maskT = arena.take(BF16, 2, NJ, P)
    mask = arena.take(BF16, 2, N)
    w_self, w_nb = arena.take(F32, KD, D), arena.take(F32, KD, D)
    w_comb = arena.take(F32, 2 * KD, D)
    small = Region(mem["SMALL"], SMALL_WORDS)
    wx, wa = small.take(F32, KD, D), small.take(F32, KD, D)
    b_row = small.take(F32, 2 * D, rows=1)
    b_wide = small.take(F32, 2 * KD * P)
    b_comb = small.take(F32, D, rows=1)
    bias = small.take(F32, D)
    stats = mem["stats"]
    var, tmp, slope, offset = (small.take(F32, NT) for _ in range(4))
    deg, rdeg = small.take(F32, STAGES), small.take(F32, STAGES)
    xn = small.take(F32, 2, D)
    agg_low, agg = small.take(F32, 2, D), small.take(F32, 2, D)
    w_selfT, w_nbT = agg_low, agg
    assert KD == 2
    xnT, aggT = arena.take(F32, 2, KD, P), arena.take(F32, 2, KD, P)
    out_b = small.take(F32, 2, D)
    scaled = mem["xln"]
    zeros = arena.take(F32, ZERO_ROWS * (D + 1))

    ps_mask = [psum[:, 1024 * s:1024 * (s + 1)].bitcast(BF16).rearrange("p (j q) -> p j q", q=P)[:, 0:NJ, :] for s in range(2)]
    ps_agg = [psum[:, 2048 + 512 * s:2048 + 512 * (s + 1)] for s in range(2)]
    ps_turn = psum[:, 3072:3584].rearrange("p (k q) -> p k q", q=P)
    ps_out = psum[:, 3584:3584 + D]

    XCHUNK = 4
    x_in = [sem(f"a_x_in{c}") for c in range(NT // XCHUNK)]
    w_in = sem("a_w_in")
    adj_landed = [sem(f"a_adj_landed{s}") for s in range(STAGES)]
    zeros_ready = sem("a_zeros_ready")
    slots_zeroed = sem("slots_zeroed")
    mem["slots_zeroed"] = slots_zeroed
    const_ready = sem("a_const_ready")
    dve_chain = sem("a_dve_chain")
    stats_done, var_ready, sd_ready = sem("a_stats_done"), sem("a_var_ready"), sem("a_sd_ready")
    mask_ready, turned, maskT_ready = sem("a_mask_ready"), sem("a_turned"), sem("a_maskT_ready")
    agg_summed, agg_ready = sem("a_agg_summed"), sem("a_agg_ready")
    xn_ready, low_ready = sem("a_xn_ready"), sem("a_low_ready")
    both_turned, both_ready = sem("a_both_turned"), sem("a_both_ready")
    out_summed, out_read, x_added = sem("a_out_summed"), sem("a_out_read"), sem("a_x_added")
    wT_turned, wT_ready, w_summed, w_ready = (sem("a_" + n) for n in ("wT_turned", "wT_ready", "w_summed", "w_ready"))
    bias_summed, bias_ready, b_ready = sem("a_bias_summed"), sem("a_bias_ready"), sem("a_b_ready")
    b_widened, slope_ready, scaled_ready, high_ready = (sem("a_" + n) for n in (
        "b_widened", "slope_ready", "scaled_ready", "high_ready"))
    split_done, edges_ready, rdeg_steps = sem("a_split_done"), sem("a_edges_ready"), sem("a_rdeg_steps")

    with nc.Block() as block:

        @block.sync
        def _(sp):
            x_rows = dram["x"].rearrange("(t p) d -> p t d", p=P)
            for c in range(NT // XCHUNK):
                here = slice(c * XCHUNK, (c + 1) * XCHUNK)
                sp.dma_start(x[:, here], x_rows[:, here]).then_inc(x_in[c], 16)
            adj = dram["adj"].rearrange("(t p) n -> t p n", p=P)
            for s in range(STAGES):
                sp.dma_start(adj_in[:, s], adj[s]).then_inc(adj_landed[s], 16)
            with sp.Fori(1, NT // STAGES) as g:
                i0 = g * STAGES
                for s in range(STAGES):
                    sp.wait_ge(mask_ready, i0 + (s - STAGES + 1))
                    sp.dma_start(adj_in[:, s], at2(adj, i0 + s)).then_inc(adj_landed[s], 16)
            sp.wait_ge(zeros_ready, 2)
            zero_rows = mem["slot_x"].rearrange("(c p r) d -> c p (r d)", p=P, r=ZERO_ROWS)
            for c in range(NS // ZERO_ROWS):
                sp.dma_start(zero_rows[c], zeros).then_inc(slots_zeroed, 16)
            sp.wait_ge(slots_zeroed, 16 * (NS // ZERO_ROWS))

        @block.gpsimd
        def _(pool):
            nc.gpsimd.memset(identity, 0.0).then_inc(const_ready, 1)
            nc.gpsimd.memset(ones, 1.0).then_inc(const_ready, 1)
            nc.gpsimd.memset(zeros, 0.0).then_inc(zeros_ready, 1)
            pool.wait_ge(zeros_ready, 1)
            nc.gpsimd.iota(zeros.rearrange("p (r d) -> p r d", d=D + 1)[:, :, D:D + 1], pattern=[[1, ZERO_ROWS], [1, 1]],
                           base=0, channel_multiplier=ZERO_ROWS, allow_small_or_imprecise_dtypes=True).then_inc(zeros_ready, 1)
            pool.wait_ge(const_ready, 2)
            nc.gpsimd.affine_select(out=identity, in_=identity, compare_op=ALU.not_equal, fill=1.0, base=0,
                                    pattern=[[-1, P]], channel_multiplier=1).then_inc(const_ready, 1)
            pool.wait_ge(const_ready, 3)
            nc.gpsimd.tensor_copy(identity16, identity).then_inc(const_ready, 1)
            pool.wait_ge(slope_ready, 1)
            for t in range(NT):
                nc.gpsimd.tensor_scalar(scaled[:, t], x[:, t], col(slope, t), col(offset, t), ALU.mult, ALU.add
                                        ).then_inc(scaled_ready, 1)

        @block.scalar
        def _(act):
            for view, name in ((w_self, "L0_gnn_W_self"), (w_nb, "L0_gnn_W_nb"), (w_comb, "L0_gnn_W_comb")):
                act.dma_start(view, dram[name].rearrange("(k p) d -> p k d", p=P)).then_inc(w_in, 16)
            for n, name in enumerate(("L0_gnn_b_self", "L0_gnn_b_nb")):
                act.dma_start(b_row[:, n * D:(n + 1) * D], dram[name].rearrange("(o d) -> o d", o=1)).then_inc(w_in, 16)
            act.dma_start(b_comb, dram["L0_gnn_b_comb"].rearrange("(o d) -> o d", o=1)).then_inc(w_in, 16)
            act.dma_start(mem["gate_w"], dram["L0_ffn_gate_w"].rearrange("(k p) e -> p k e", p=P)).then_inc(mem["gate_in"], 16)
            act.dma_start(mem["gate_b"], dram["L0_ffn_gate_b"].rearrange("(o e) -> o e", o=1)).then_inc(mem["gate_in"], 16)
            act.wait_ge(var_ready, 1)
            nc.scalar.activation(var, var, ACT.Sqrt).then_inc(sd_ready, 1)
            act.wait_ge(slope_ready, 1)
            with act.Fori(0, NT) as t:
                nc.scalar.activation(at(ln16, t)[:, 0:D], at(x, t), ACT.Identity, bias=col(offset, t), scale=col(slope, t)
                                     ).then_inc(high_ready, 1)

            def mask_out(i, s):
                act.wait_ge(turned, i + 1)
                nc.scalar.activation(maskT[:, s], ps_mask[s], ACT.Copy).then_inc(maskT_ready, 1)

            def both_out(i, s):
                act.wait_ge(both_turned, i + 1)
                nc.scalar.activation(xnT[:, s], ps_turn[:, 0:KD], ACT.Copy)
                nc.scalar.activation(aggT[:, s], ps_turn[:, KD:2 * KD], ACT.Copy).then_inc(both_ready, 1)

            mask_out(0, 0)
            mask_out(1, 1)
            act.wait_ge(b_widened, 1)
            nc.scalar.activation(b_wide, psum[:, 3072:3584], ACT.Copy).then_inc(b_ready, 1)
            for n, view in enumerate((w_selfT, w_nbT)):
                act.wait_ge(wT_turned, n + 1)
                nc.scalar.activation(view.rearrange("p k d -> p (k d)"), ps_agg[n], ACT.Copy).then_inc(wT_ready, 1)
            for n, view in enumerate((wx, wa)):
                act.wait_ge(w_summed, n + 1)
                nc.scalar.activation(view.rearrange("p k d -> p (k d)"), ps_agg[n], ACT.Copy).then_inc(w_ready, 1)
            with act.Fori(1, NT // 2) as g:
                i0 = g * 2
                for u in range(2):
                    both_out(i0 + (u - 2), u)
                    mask_out(i0 + u, u)
            both_out(NT - 2, 0)
            both_out(NT - 1, 1)

        @block.tensor
        def _(pe):
            pe.wait_ge(const_ready, 4)
            def turn_mask(i, s):
                pe.wait_ge(mask_ready, i + 1)
                for j in range(NJ):
                    last = nc.tensor.transpose(ps_mask[s][:, j, :], mask[:, s, j * P:(j + 1) * P], identity16)
                last.then_inc(turned, 1)

            def sum_neighbours(i, s):
                pe.wait_ge(maskT_ready, i + 1)
                for j in range(NJ):
                    last = nc.tensor.matmul(ps_agg[s], maskT[:, s, j, :], ln16[:, j, :], start=(j == 0), stop=(j == NJ - 1))
                last.then_inc(agg_summed, 1)

            def turn_both(i, s):
                pe.wait_ge(agg_ready, i + 1)
                pe.wait_ge(xn_ready, i + 1)
                for n, rows in enumerate((xn, agg)):
                    for k in range(KD):
                        last = nc.tensor.transpose(ps_turn[:, n * KD + k, :], rows[:, s, k * P:(k + 1) * P], identity)
                last.then_inc(both_turned, 1)

            def combine(i, s):
                pe.wait_ge(both_ready, i + 1)
                pe.wait_ge(out_read, i + 1)
                for n, (lhs, w) in enumerate(((xnT, wx), (aggT, wa))):
                    for k in range(KD):
                        last = nc.tensor.matmul(ps_out, lhs[:, s, k, :], w[:, k, :], start=(n == 0 and k == 0),
                                                stop=(n == 1 and k == KD - 1))
                last.then_inc(out_summed, 1)

            turn_mask(0, 0)
            turn_mask(1, 1)

            pe.wait_ge(w_in, 6 * 16)
            for m in range(2 * KD):
                last = nc.tensor.matmul(ps_turn[:, m, :], b_row[0:1, m * P:(m + 1) * P], ones[0:1, :], start=True, stop=True)
            last.then_inc(b_widened, 1)
            for n, w in enumerate((w_self, w_nb)):
                for k in range(KD):
                    for m in range(KD):
                        last = nc.tensor.transpose(ps_agg[n][:, m * D + k * P:m * D + (k + 1) * P],
                                                   w[:, k, m * P:(m + 1) * P], identity)
                last.then_inc(wT_turned, 1)
            for n, wT in enumerate((w_selfT, w_nbT)):
                pe.wait_ge(wT_ready, n + 1)
                for rows in range(KD):
                    for m in range(KD):
                        last = nc.tensor.matmul(ps_agg[n][:, rows * D:(rows + 1) * D], wT[:, m, rows * P:(rows + 1) * P],
                                                w_comb[:, n * KD + m, :], start=(m == 0), stop=(m == KD - 1))
                last.then_inc(w_summed, 1)
            pe.wait_ge(b_ready, 1)
            for m in range(2 * KD):
                nc.tensor.matmul(ps_out, b_wide[:, m * P:(m + 1) * P], w_comb[:, m, :], start=(m == 0), stop=False)
            nc.tensor.matmul(ps_out, ones[0:1, :], b_comb, start=False, stop=True).then_inc(bias_summed, 1)

            pe.wait_ge(split_done, NT)
            pe.wait_ge(w_ready, 2)
            pe.wait_ge(bias_ready, 1)
            sum_neighbours(0, 0)
            with pe.Fori(0, NT // 2 - 1) as g:
                i0 = g * 2 + 1
                for u in range(2):
                    s = (1 + u) % 2
                    turn_mask(i0 + (u + 1), 1 - s)
                    turn_both(i0 + (u - 1), 1 - s)
                    sum_neighbours(i0 + u, s)
                    combine(i0 + (u - 1), 1 - s)
            turn_both(NT - 2, 0)
            sum_neighbours(NT - 1, 1)
            combine(NT - 2, 0)
            turn_both(NT - 1, 1)
            combine(NT - 1, 1)

        @block.vector
        def _(dve):
            chain = Chain(dve, dve_chain)
            dve.sem_inc(x_added, 1)
            dve.sem_inc(out_read, 1)
            for c in range(NT // XCHUNK):
                dve.wait_ge(x_in[c], 16)
                layernorm_sums(dve, nc, x, stats, stats_done, c * XCHUNK, (c + 1) * XCHUNK)
            dve.wait_ge(stats_done, NT)
            layernorm_spread(dve, nc, chain, stats, mean, var, tmp).then_inc(var_ready, 1)
            dve.wait_ge(sd_ready, 1)
            chain.link(nc.vector.reciprocal(rstd, var))
            chain.link(nc.vector.tensor_scalar(slope, rstd, SCALE16, None, ALU.mult))
            nc.vector.scalar_tensor_tensor(out=offset, in0=mean, scalar=-1.0, in1=slope, op0=ALU.mult, op1=ALU.mult
                                           ).then_inc(slope_ready, 1)

            def normalise(i, s):
                nc.vector.tensor_scalar(xn[:, s], at(x, i), col(mean, i), col(rstd, i), ALU.subtract, ALU.mult
                                        ).then_inc(xn_ready, 1)

            def make_mask(i, s, stage, landed):
                dve.wait_ge(adj_landed[stage], landed)
                dve.wait_ge(edges_ready, i)
                nc.vector.tensor_scalar(mask[:, s], adj_in[:, stage], 0.0, 0.0, ALU.is_gt, ALU.add,
                                        accum_out=col(deg, stage)).then_inc(mask_ready, 1)
                dve.wait_ge(mask_ready, i + 1)
                nc.vector.tensor_scalar(at(edges, i), mask[:, s], 1.0, -NO_EDGE, ALU.subtract, ALU.mult
                                        ).then_inc(edges_ready, 1)

            def mean_of_neighbours(i, s, stage):
                rdeg_i = col(rdeg, stage)
                nc.vector.tensor_scalar(rdeg_i, col(deg, stage), 1.0, SCALE16, ALU.max, ALU.mult).then_inc(rdeg_steps, 1)
                dve.wait_ge(rdeg_steps, i * 2 + 1)
                nc.vector.reciprocal(rdeg_i, rdeg_i).then_inc(rdeg_steps, 1)
                dve.wait_ge(rdeg_steps, i * 2 + 2)
                dve.wait_ge(agg_summed, i + 1)
                nc.vector.tensor_scalar(agg_low[:, s], ps_agg[s][:, D:2 * D], rdeg_i, None, ALU.mult
                                        ).then_inc(low_ready, 1)
                dve.wait_ge(low_ready, i + 1)
                nc.vector.scalar_tensor_tensor(out=agg[:, s], in0=ps_agg[s][:, 0:D], scalar=rdeg_i,
                                               in1=agg_low[:, s], op0=ALU.mult, op1=ALU.add).then_inc(agg_ready, 1)

            def add_result(i, s):
                dve.wait_ge(out_summed, i + 1)
                nc.vector.tensor_tensor(out_b[:, s], ps_out, bias, ALU.add).then_inc(out_read, 1)
                dve.wait_ge(x_added, i + 1)
                dve.wait_ge(out_read, i + 2)
                nc.vector.scalar_tensor_tensor(out=at(x, i), in0=out_b[:, s], scalar=0.0, in1=at(x, i),
                                               op0=ALU.max, op1=ALU.add).then_inc(x_added, 1)

            def new_stats(i):
                dve.wait_ge(x_added, i + 2)
                nc.vector.bn_stats(at(stats, i), at(x, i)).then_inc(stats_done, 1)

            def step(i, stage, first=False, more=True, landed=None):
                s = stage % 2
                mean_of_neighbours(i - 1, 1 - s, (stage - 1) % STAGES)
                if not first:
                    dve.wait_ge(both_turned, i - 1)
                normalise(i, s)
                if not first:
                    add_result(i - 2, s)
                if more:
                    dve.wait_ge(turned, i + 1)
                    make_mask(i + 2, s, (stage + 2) % STAGES, landed)
                if not first:
                    new_stats(i - 2)

            make_mask(0, 0, 0, 16)
            make_mask(1, 1, 1, 16)
            with dve.Fori(0, NT) as t:
                dve.wait_ge(high_ready, t + 1)
                dve.wait_ge(scaled_ready, t + 1)
                nc.vector.tensor_tensor(at(ln16, t)[:, D:2 * D], at(scaled, t), at(ln16, t)[:, 0:D], ALU.subtract
                                        ).then_inc(split_done, 1)
            dve.wait_ge(bias_summed, 1)
            nc.vector.tensor_copy(bias, ps_out).then_inc(bias_ready, 1)
            dve.wait_ge(turned, 1)
            make_mask(2, 0, 2, 16)
            normalise(0, 0)
            step(1, 1, first=True, landed=16)
            with dve.Fori(0, (NT - 4) // STAGES) as g:
                i0 = g * STAGES + 2
                for u in range(STAGES):
                    step(i0 + u, (2 + u) % STAGES, landed=i0 * 4 + 24)
            step(NT - 2, 2, more=False)
            step(NT - 1, 3, more=False)
            mean_of_neighbours(NT - 1, 1, 3)
            add_result(NT - 2, 0)
            add_result(NT - 1, 1)
            dve.wait_ge(edges_ready, NT)
            new_stats(NT - 2)
            new_stats(NT - 1)
            dve.wait_ge(stats_done, 2 * NT)


def at2(view, i):
    return view[bass.ds(i, 1)].rearrange("o p n -> (o p) n")


def col(view, i):
    return view[:, i:i + 1] if isinstance(i, int) else view[:, bass.ds(i, 1)]


def mixture(nc, dram, mem, sem):
    x, xln = mem["x"], mem["xln"]
    identity, ones = mem["identity"], mem["ones"]
    mean, rstd = mem["mean"], mem["rstd"]
    psum = mem["PSUM"]
    slot_x, token_y = mem["slot_x"], mem["token_y"]
    row_no = mem["xln_row"][:, :, D:D + 1]
    arena = Region(mem["ARENA"], mem["ARENA"].shape[1])
    w1 = arena.take(F32, NE, KD, I2)
    w2 = arena.take(F32, NE, KI, D)
    small = Region(mem["SMALL"], SMALL_WORDS)
    xT = small.take(F32, 2, KD, P)
    setup_words = small.at
    gate, up, sig = (small.take(F32, 2, I) for _ in range(3))
    tT = small.take(F32, 2, KI, P)
    tiles_words, small.at = small.at, setup_words
    bias_in = small.take(F32, I2 + D)
    act_wide = small.take(F32, 7, P)
    small.at = tiles_words
    pick = small.take(BF16, 4, P)
    pick_shared = small.take(BF16, P)
    biases = small.take(BF16, I2 + D)
    onehot = small.take(F32, NS + 1)
    onehot16 = small.take(BF16, NS + 2)
    params = small.take(F32, 7, NS + 1)
    tile_expert = small.take(I32, NS)
    slots = small.take(U32, TOPK, NT)
    weight = small.take(F32, TOPK, NT)
    stats, var, tmp = mem["stats"], small.take(F32, NT), small.take(F32, NT)
    act_table = small.take(F32, 8)
    soft = small.take(F32, 3, 2)
    shared_words = small.at
    xn = small.take(F32, 2, D)
    part16 = xn.rearrange("p s d -> p (s d)").bitcast(BF16)[:, 0:I2 + D]
    from_last = small.take(F32, E)
    prob, equal, first = (small.take(F32, NT, E) for _ in range(3))
    best = [small.take(F32, NT, E) for _ in range(TOPK)]
    chosen = small.take(BF16, NT, NE + 1)
    top = small.take(F32, 4, NT)
    route_end = small.at
    small.at = shared_words
    x_in = small.take(F32, 4, D + 2)
    y_row = small.take(U32, 4, 1)
    y_out = small.take(F32, 4, D)
    small.at = shared_words
    y_in = small.take(F32, 4, TOPK, D)
    edge = mem["const"]
    before = edge.take(BF16, P)
    ones16 = edge.take(BF16, P)
    before_e, same_e = edge.take(BF16, NB), edge.take(BF16, NB)
    gate_w, gate_b, gate_in = mem["gate_w"], mem["gate_b"], mem["gate_in"]
    steps128, tile_no = edge.take(F32, E), edge.take(F32, NS)
    expert_no = edge.take(BF16, 2)
    part_is = edge.take(F32, 4)
    count, count16, start, stop = edge.take(F32, 2), edge.take(BF16, 4), edge.take(F32, 2), edge.take(F32, 2)
    count_wide = edge.take(BF16, P)
    base = edge.take(F32, E)

    bank = [psum[:, 512 * b:512 * (b + 1)] for b in range(8)]
    ps_x = [bank[s][:, 0:KD * P].rearrange("p (k q) -> p k q", q=P) for s in range(2)]
    ps_h = [bank[2 + s][:, 0:I2] for s in range(2)]
    ps_t = [bank[4 + s][:, 0:KI * P].rearrange("p (k q) -> p k q", q=P) for s in range(2)]
    ps_y = [bank[6 + s][:, 0:D] for s in range(2)]
    ps_logits = bank[4][:, 0:NT * E].rearrange("p (t e) -> p t e", e=E)
    ps_rank = bank[5][:, 0:NT * E].rearrange("p (t e) -> p t e", e=E)
    ps_count = bank[6][0:NE, 0:1]
    ps_base, ps_start = bank[7][:, 0:E], bank[7][0:NB, 32:34]
    ps_tile = bank[6][0:1, 64:64 + NS]
    ps_params = bank[4][:, 0:7 * (NS + 1)].rearrange("p (c s) -> p c s", s=NS + 1)

    names = ("consts", "small_in", "w_shared_in", "w1_in", "w2_in", "dve_chain", "stats_done", "var_ready", "sd_ready",
             "xn_ready", "xln_ready", "x_turned", "xT_ready", "logits_done", "soft_in", "soft_out", "wide_ready",
             "shifted", "exped", "chosen_ready", "ranked", "counted", "wide_count", "started", "onehot_ready",
             "tables_done", "tables_out", "slots_ready", "sent", "ex_turned", "exT_ready", "h_summed", "swi",
             "sig_ready", "t_turned", "tT_ready", "y_summed", "z_added", "y_copied", "pick_ready", "combined",
             "combined_half", "row_kept", "row_numbered", "biases_ready")
    S = {name: sem("b_" + name) for name in names}
    x_landed = [sem(f"b_x_landed{q}") for q in range(4)]
    y_stored = [sem(f"b_y_stored{q}") for q in range(4)]
    y_landed = [sem(f"b_y_landed{q}") for q in range(4)]
    SMALL_DMAS = 4 * PARTS + 2

    with nc.Block() as block:

        @block.sync
        def _(sp):
            sp.dma_start(w1[:, E], dram["L0_ffn_shared_w1"].rearrange("(k p) h -> p k h", p=P)).then_inc(S["w_shared_in"], 16)
            sp.dma_start(w2[0:IH, E], dram["L0_ffn_shared_w2"].rearrange("(k p) d -> p k d", p=IH)).then_inc(S["w_shared_in"], 16)
            for e0 in range(0, E, E // 4):
                some = slice(e0, e0 + E // 4)
                sp.dma_start(w1[:, some].rearrange("p e k h -> p (e k) h"),
                             dram["L0_ffn_expert_w1"][some].rearrange("e (k p) h -> p (e k) h", p=P)).then_inc(S["w1_in"], 16)
                sp.dma_start(w2[0:IH, some].rearrange("p e k d -> p (e k) d"),
                             dram["L0_ffn_expert_w2"][some].rearrange("e (k p) d -> p (e k) d", p=IH)).then_inc(S["w2_in"], 16)
            sp.wait_ge(S["xln_ready"], NT)

            def load(n, q, shared):
                if shared:
                    sp.dma_start(x_in[:, q, 0:D], at(xln, n)).then_inc(x_landed[q], 16)
                else:
                    sp.dma_start(x_in[:, q, 0:D + 1], rows(slot_x, n - NT)).then_inc(x_landed[q], 16)

            sp.wait_ge(S["slots_ready"], 1)
            sp.wait_ge(S["biases_ready"], 1)
            for n in range(4):
                load(n, n, True)
            with sp.Fori(1, NT // 4) as g:
                for q in range(4):
                    sp.wait_ge(S["ex_turned"], g * 4 + (q - 3))
                    load(g * 4 + q, q, True)
            sp.wait_ge(S["sent"], 16 * NT * TOPK)
            for n in range(NT, NT + 4):
                sp.wait_ge(S["ex_turned"], n - 3)
                load(n, n % 4, False)
            with sp.Fori(NT // 4 + 1, (NT + NS) // 4) as g:
                for q in range(4):
                    sp.wait_ge(S["ex_turned"], g * 4 + (q - 3))
                    sp.wait_ge(S["row_kept"], g * 4 + (q - 3))
                    load(g * 4 + q, q, False)
            for q in range(4):
                sp.wait_ge(y_stored[q], 16 * NS // 4)
            results = token_y[SPARE:, :].rearrange("(k t p) d -> t p k d", k=TOPK, p=P)

            def load_results(t, q):
                sp.dma_start(y_in[:, q], results[t] if isinstance(t, int) else
                             results[bass.ds(t, 1)].rearrange("o p k d -> (o p) k d")).then_inc(y_landed[q], 16)

            for t in range(4):
                load_results(t, t)
            with sp.Fori(1, NT // 4) as g:
                for q in range(4):
                    sp.wait_ge(S["combined"], g * 4 + (q - 3))
                    load_results(g * 4 + q, q)

        @block.gpsimd
        def _(pool):
            chain = Chain(pool, S["consts"])
            link = chain.link
            for view, value in ((before, 1.0), (ones16, 1.0), (before_e, 1.0), (same_e, 0.0), (chosen, 0.0), (onehot, 0.0),
                                (part_is, 0.0), (pick_shared, 1.0)):
                link(nc.gpsimd.memset(view, value))
            link(nc.gpsimd.affine_select(out=before, in_=before, compare_op=ALU.is_gt, fill=0.0, base=0,
                                         pattern=[[1, P]], channel_multiplier=-1))
            link(nc.gpsimd.affine_select(out=before_e, in_=before_e, compare_op=ALU.is_gt, fill=0.0, base=0,
                                         pattern=[[0, PARTS], [1, NE]], channel_multiplier=-1))
            link(nc.gpsimd.affine_select(out=same_e, in_=same_e, compare_op=ALU.not_equal, fill=1.0, base=0,
                                         pattern=[[0, PARTS], [1, NE]], channel_multiplier=-1))
            for part in range(PARTS):
                link(nc.gpsimd.affine_select(out=onehot[:, NS:NS + 1], in_=onehot[:, NS:NS + 1], compare_op=ALU.not_equal,
                                             fill=1.0, base=-(part * NE + E), pattern=[[0, 1]], channel_multiplier=1))
                view = part_is[:, part:part + 1]
                link(nc.gpsimd.memset(view, 1.0))
                link(nc.gpsimd.affine_select(out=view, in_=view, compare_op=ALU.is_ge, fill=0.0, base=-part * NE,
                                             pattern=[[0, 1]], channel_multiplier=1))
                link(nc.gpsimd.affine_select(out=view, in_=view, compare_op=ALU.is_ge, fill=0.0, base=(part + 1) * NE - 1,
                                             pattern=[[0, 1]], channel_multiplier=-1))
            link(nc.gpsimd.iota(from_last, pattern=[[1, E]], base=-E, channel_multiplier=0, allow_small_or_imprecise_dtypes=True))
            link(nc.gpsimd.iota(steps128, pattern=[[P, E]], base=0, channel_multiplier=0, allow_small_or_imprecise_dtypes=True))
            link(nc.gpsimd.iota(tile_no, pattern=[[1, NS]], base=0, channel_multiplier=0, allow_small_or_imprecise_dtypes=True))
            link(nc.gpsimd.iota(expert_no[:, 0:1], pattern=[[0, 1]], base=0, channel_multiplier=1, allow_small_or_imprecise_dtypes=True))
            mem["b_consts"] = chain.count
            pool.wait_ge(S["var_ready"], 2)
            for t in range(NT):
                nc.gpsimd.tensor_scalar(xln[:, t], x[:, t], mean[:, t:t + 1], rstd[:, t:t + 1], ALU.subtract, ALU.mult
                                        ).then_inc(S["xln_ready"], 1)
            pool.wait_ge(S["small_in"], 16 * SMALL_DMAS)
            rest = bias_in[0:NB]
            pool.wait_ge(S["x_turned"], NT)
            for part in range(PARTS):
                link(nc.gpsimd.tensor_copy(part16[0:NB], rest))
                if part < PARTS - 1:
                    link(nc.gpsimd.tensor_tensor(rest, rest, part16[0:NB], ALU.subtract))
                if part:
                    link(nc.gpsimd.tensor_scalar(part16[0:NB], part16[0:NB], part_is[0:NB, part:part + 1], None, ALU.mult))
                    link(nc.gpsimd.tensor_tensor(biases[0:NB], biases[0:NB], part16[0:NB], ALU.add))
                else:
                    link(nc.gpsimd.tensor_scalar(biases[0:NB], part16[0:NB], part_is[0:NB, 0:1], None, ALU.mult))
            link(nc.gpsimd.tensor_scalar(pick_shared[0:NB], ones16[0:NB], onehot[0:NB, NS:NS + 1], None, ALU.mult))
            pool.sem_inc(S["biases_ready"], 1)
            for k in range(TOPK):
                if k:
                    pool.wait_ge(S["sent"], 16 * NT)
                nc.gpsimd.iota(row_no, pattern=[[P, NT], [1, 1]], base=SPARE + k * N, channel_multiplier=1,
                                 allow_small_or_imprecise_dtypes=True).then_inc(S["row_numbered"], 1)
                pool.wait_ge(S["row_numbered"], k + 1)
                if k == 0:
                    pool.wait_ge(S["slots_ready"], 1)
                    pool.wait_ge(S["xln_ready"], NT)
                for t in range(NT):
                    nc.gpsimd.indirect_dma_start(
                        out=slot_x, out_offset=bass.IndirectOffsetOnAxis(ap=slots[:, k, t:t + 1], axis=0),
                        in_=mem["xln_row"][:, t, 0:D + 1], in_offset=None).then_inc(S["sent"], 16)

            pool.sem_inc(S["row_kept"], NT)

            def keep_rows(m):
                pool.wait_ge(x_landed[m % 4], 16 * (NT // 4 + m // 4 + 1))
                if m >= 4:
                    pool.wait_ge(y_stored[m % 4], 16 * (m // 4))
                nc.gpsimd.tensor_copy(y_row[:, m % 4], x_in[:, m % 4, D:D + 1]).then_inc(S["row_kept"], 1)

            keep_rows(0)
            for m in range(NS):
                if m < NS - 1:
                    keep_rows(m + 1)
                pool.wait_ge(S["row_kept"], NT + m + 1)
                pool.wait_ge(S["y_copied"], m + 3)
                nc.gpsimd.indirect_dma_start(
                    out=token_y, out_offset=bass.IndirectOffsetOnAxis(ap=y_row[:, m % 4], axis=0),
                    in_=y_out[:, m % 4], in_offset=None).then_inc(y_stored[m % 4], 16)

        consts = mem["b_consts"]

        @block.scalar
        def _(act):
            def small_load(view, ap):
                act.dma_start(view, ap).then_inc(S["small_in"], 16)

            act.wait_ge(S["var_ready"], 1)
            nc.scalar.activation(var, var, ACT.Sqrt).then_inc(S["sd_ready"], 1)
            for part in range(PARTS):
                p0 = part * NE
                small_load(bias_in[p0:p0 + E, 0:I2], dram["L0_ffn_expert_b1"])
                small_load(bias_in[p0 + E:p0 + NE, 0:I2], dram["L0_ffn_shared_b1"].rearrange("(o h) -> o h", o=1))
                small_load(bias_in[p0:p0 + E, I2:I2 + D], dram["L0_ffn_expert_b2"])
                small_load(bias_in[p0 + E:p0 + NE, I2:I2 + D], dram["L0_ffn_shared_b2"].rearrange("(o h) -> o h", o=1))
            small_load(act_table[0:E, 0:5], dram["L0_ffn_expert_act"])
            small_load(act_table[E:NE, 0:5], dram["L0_ffn_shared_act"].rearrange("(o h) -> o h", o=1))

            def xT_out(s, wait, ready):
                act.wait_ge(*wait)
                nc.scalar.activation(xT[:, s], ps_x[s], ACT.Copy).then_inc(ready, 1)

            with act.Fori(0, NT // 2) as g:
                for u in range(2):
                    xT_out(u, (S["x_turned"], g * 2 + (u + 1)), S["xT_ready"])
            act.wait_ge(S["soft_in"], 1)
            nc.scalar.activation(soft[0:NE, 0], soft[0:NE, 0], ACT.Exp, scale=-1.0).then_inc(S["soft_out"], 1)
            act.wait_ge(S["shifted"], 1)
            nc.scalar.activation(prob, prob, ACT.Exp).then_inc(S["exped"], 1)
            act.wait_ge(S["soft_in"], 2)
            nc.scalar.activation(soft[0:NE, 0], soft[0:NE, 0], ACT.Ln).then_inc(S["soft_out"], 1)

            def tT_out(n, s):
                act.wait_ge(S["t_turned"], n + 1)
                nc.scalar.activation(tT[0:IH, s], ps_t[s][0:IH], ACT.Copy).then_inc(S["tT_ready"], 1)

            def y_out_copy(n, s, q, stored):
                act.wait_ge(S["y_summed"], n + 1)
                if stored is not None:
                    act.wait_ge(y_stored[q], stored)
                nc.scalar.activation(y_out[:, q], ps_y[s], ACT.Copy).then_inc(S["y_copied"], 1)

            def step(n, q, g, tail=True, more=True, shared=False, shared_tail=False):
                s = q % 2
                if tail:
                    tT_out(n - 2, s)
                if more:
                    xT_out(1 - s, (S["ex_turned"], n + 2), S["exT_ready"])
                act.wait_ge(S["swi"], n * 4 + 1)
                alpha = params[:, 0, NS:NS + 1] if shared else params_at(params, 0, n - NT)
                nc.scalar.activation(sig[:, s], gate[:, s], ACT.Sigmoid, scale=alpha).then_inc(S["sig_ready"], 1)
                if tail and not shared_tail:
                    y_out_copy(n - 2, s, (q - 2) % 4, None if isinstance(n, int) and n < NT + 6 else (g - NT // 4) * 16)

            act.wait_ge(S["tables_out"], 2)
            xT_out(0, (S["ex_turned"], 1), S["exT_ready"])
            run_tiles(act, step)
            for n in (NT + NS - 2, NT + NS - 1):
                tT_out(n, n % 2)
                y_out_copy(n, n % 2, n % 4, (n // 4 - NT // 4) * 16)

        @block.tensor
        def _(pe):
            def turn(s, rows_, ready):
                for k in range(KD):
                    last = nc.tensor.transpose(ps_x[s][:, k, :], rows_[:, k * P:(k + 1) * P], identity)
                last.then_inc(ready, 1)

            def turn_xn(t, s):
                pe.wait_ge(S["xn_ready"], t + 1)
                turn(s, xn[:, s], S["x_turned"])

            def logits(t, s):
                pe.wait_ge(gate_in, 32)
                pe.wait_ge(S["xT_ready"], t + 1)
                for k in range(KD):
                    nc.tensor.matmul(at(ps_logits, t), xT[:, s, k, :], gate_w[:, k, :], start=(k == 0), stop=False)
                nc.tensor.matmul(at(ps_logits, t), ones[0:1, :], gate_b, start=False, stop=True
                                 ).then_inc(S["logits_done"], 1)

            turn_xn(0, 0)
            with pe.Fori(0, NT // 2 - 1) as g:
                turn_xn(g * 2 + 1, 1)
                logits(g * 2, 0)
                turn_xn(g * 2 + 2, 0)
                logits(g * 2 + 1, 1)
            turn_xn(NT - 1, 1)
            logits(NT - 2, 0)
            logits(NT - 1, 1)
            pe.wait_ge(S["consts"], consts)
            pe.wait_ge(S["chosen_ready"], 1)
            nc.tensor.matmul(ps_rank, before, chosen[:, :, 0:E], start=True, stop=False)
            for back in range(1, NT):
                last = nc.tensor.matmul(ps_rank[:, back:NT, :], ones16, chosen[:, 0:NT - back, 0:E], start=False,
                                        stop=(back == NT - 1))
            last.then_inc(S["ranked"], 1)
            for t in range(NT):
                last = nc.tensor.matmul(ps_count, chosen[:, t, 0:NE], ones16[:, 0:1],
                                        start=(t == 0), stop=(t == NT - 1))
            last.then_inc(S["counted"], 1)
            pe.wait_ge(S["wide_count"], 1)
            nc.tensor.matmul(ps_base, count_wide[0:NE], before_e[0:NE, 0:E], start=True, stop=True)
            nc.tensor.matmul(ps_start[:, 0:1], before_e[0:NE], count16[0:NE, 0:1], start=True, stop=True)
            nc.tensor.matmul(ps_start[:, 1:2], same_e[0:NE], count16[0:NE, 0:1], start=True, stop=True
                             ).then_inc(S["started"], 1)
            pe.wait_ge(S["onehot_ready"], 1)
            pe.wait_ge(S["wide_ready"], 1)
            nc.tensor.matmul(ps_tile, expert_no[0:NE, 0:1], onehot16[0:NE, 0:NS], start=True, stop=True)
            for c in range(7):
                last = nc.tensor.matmul(ps_params[:, c, :], act_wide[0:NE, c, :], onehot[0:NE, :], start=True, stop=True)
            last.then_inc(S["tables_done"], 1)

            def turn_x(n, q, landed):
                pe.wait_ge(x_landed[q], landed)
                turn(q % 2, x_in[:, q], S["ex_turned"])

            def expand(n, q, e, shared):
                s = q % 2
                pe.wait_ge(S["exT_ready"], n + 1)
                if not shared:
                    pe.wait_ge(S["pick_ready"], n - NT + 1)
                for k in range(KD):
                    nc.tensor.matmul(ps_h[s], xT[:, s, k, :], of_expert(w1, e, k), start=(k == 0), stop=False)
                nc.tensor.matmul(ps_h[s], pick_shared[0:NB] if shared else pick[0:NB, q], biases[0:NB, 0:I2],
                                 start=False, stop=True).then_inc(S["h_summed"], 1)

            def turn_t(n, s):
                pe.wait_ge(S["swi"], n * 4 + 4)
                for k in range(KI):
                    last = nc.tensor.transpose(ps_t[s][0:IH, k, :], up[:, s, k * IH:(k + 1) * IH], identity)
                last.then_inc(S["t_turned"], 1)

            def contract(n, q, e, shared):
                s = q % 2
                pe.wait_ge(S["tT_ready"], n + 1)
                if shared:
                    pe.wait_ge(S["z_added"], n + 1)
                else:
                    if q < 2:
                        pe.wait_ge(S["z_added"], NT + q + 1)
                    pe.wait_ge(S["y_copied"], n - NT + 1)
                for k in range(KI):
                    nc.tensor.matmul(ps_y[s], tT[0:IH, s, k, :], of_expert(w2, e, k, IH), start=(k == 0), stop=False)
                nc.tensor.matmul(ps_y[s], pick_shared[0:NB] if shared else pick[0:NB, q], biases[0:NB, I2:I2 + D],
                                 start=False, stop=True).then_inc(S["y_summed"], 1)

            def expert(n, shared):
                if shared:
                    return E
                return pe.value_load(tile_expert[0:1, n - NT:n - NT + 1] if isinstance(n, int)
                                     else tile_expert[0:1, bass.ds(n - NT, 1)], min_val=0, max_val=E - 1)

            def step(n, q, g, tail=True, more=True, shared=False, shared_tail=False):
                if tail:
                    turn_t(n - 2, q % 2)
                if more:
                    turn_x(n + 1, (q + 1) % 4, (g + (0 if q == 2 else 1)) * 16 + 16 if tail else 16)
                if isinstance(n, int) and n == NT:
                    pe.wait_ge(S["w1_in"], 16 * 4)
                    pe.wait_ge(S["w2_in"], 16 * 4)
                expand(n, q, expert(n, shared), shared)
                if tail:
                    contract(n - 2, (q - 2) % 4, expert(n - 2, shared_tail), shared_tail)

            pe.wait_ge(S["tables_out"], 2)
            pe.wait_ge(S["biases_ready"], 1)
            pe.wait_ge(S["w_shared_in"], 32)
            pe.sem_inc(S["z_added"], 2)
            pe.sem_inc(S["y_copied"], 2)
            turn_x(0, 0, 16)
            run_tiles(pe, step)
            for n in (NT + NS - 2, NT + NS - 1):
                turn_t(n, n % 2)
                contract(n, n % 4, expert(n, False), False)

        @block.vector
        def _(dve):
            chain = Chain(dve, S["dve_chain"])
            link = chain.link
            layernorm_spread(dve, nc, chain, stats, mean, var, tmp).then_inc(S["var_ready"], 1)
            dve.wait_ge(S["sd_ready"], 1)
            nc.vector.reciprocal(rstd, var).then_inc(S["var_ready"], 1)
            dve.wait_ge(S["var_ready"], 2)

            def normalise(t, s):
                nc.vector.tensor_scalar(xn[:, s], at(x, t), col(mean, t), col(rstd, t), ALU.subtract, ALU.mult
                                        ).then_inc(S["xn_ready"], 1)

            normalise(0, 0)
            normalise(1, 1)
            with dve.Fori(1, NT // 2) as g:
                for u in range(2):
                    dve.wait_ge(S["x_turned"], g * 2 + (u - 1))
                    normalise(g * 2 + u, u)

            dve.wait_ge(S["small_in"], 16 * SMALL_DMAS)
            raw = act_table[0:NE, 3:5]
            link(nc.vector.scalar_tensor_tensor(out=soft[0:NE, 0], in0=raw, scalar=-1.0, in1=raw, op0=ALU.mult, op1=ALU.max))
            nc.vector.tensor_scalar(soft[0:NE, 1], raw, 0.0, None, ALU.max).then_inc(S["soft_in"], 1)
            dve.wait_ge(S["soft_out"], 1)
            nc.vector.tensor_scalar(soft[0:NE, 0], soft[0:NE, 0], 1.0, None, ALU.add).then_inc(S["soft_in"], 1)

            def over_experts(v):
                return v.unsqueeze(2).to_broadcast([P, NT, E])

            ranks = from_last.unsqueeze(1).to_broadcast([P, NT, E])
            dve.wait_ge(S["logits_done"], NT)
            dve.wait_ge(S["consts"], consts)
            link(nc.vector.tensor_reduce(top[:, 0], ps_logits, AX, ALU.max))
            nc.vector.tensor_tensor(prob, ps_logits, over_experts(top[:, 0]), ALU.subtract).then_inc(S["shifted"], 1)
            dve.wait_ge(S["exped"], 1)
            link(nc.vector.tensor_reduce(top[:, 0], prob, AX, ALU.add))
            link(nc.vector.reciprocal(top[:, 0], top[:, 0]))
            link(nc.vector.tensor_tensor(prob, prob, over_experts(top[:, 0]), ALU.mult))
            for k in range(TOPK):
                link(nc.vector.tensor_reduce(weight[:, k], prob, AX, ALU.max))
                link(nc.vector.tensor_tensor(equal, prob, over_experts(weight[:, k]), ALU.is_equal))
                link(nc.vector.tensor_tensor(first, equal, ranks, ALU.mult))
                link(nc.vector.tensor_reduce(top[:, 1], first, AX, ALU.min))
                link(nc.vector.tensor_tensor(best[k], ranks, over_experts(top[:, 1]), ALU.is_equal))
                if k < TOPK - 1:
                    link(nc.vector.scalar_tensor_tensor(out=prob, in0=best[k], scalar=-4.0, in1=prob, op0=ALU.mult, op1=ALU.add))
            nc.vector.tensor_tensor(chosen[:, :, 0:E], best[0], best[1], ALU.add).then_inc(S["chosen_ready"], 1)
            link(nc.vector.tensor_tensor(top[:, 2], weight[:, 0], weight[:, 1], ALU.add))
            link(nc.vector.reciprocal(top[:, 2], top[:, 2]))
            for k in range(TOPK):
                link(nc.vector.tensor_tensor(weight[:, k], weight[:, k], top[:, 2], ALU.mult))
            dve.wait_ge(S["soft_out"], 2)
            link(nc.vector.tensor_tensor(act_table[0:NE, 3:5], soft[0:NE, 0], soft[0:NE, 1], ALU.add))
            link(nc.vector.tensor_scalar(act_table[0:NE, 5:7], act_table[0:NE, 3:5], -1.0, None, ALU.mult))
            nc.vector.tensor_copy(act_wide[0:NE], act_table[0:NE, 0:7].unsqueeze(2).to_broadcast([NE, 7, P])
                                  ).then_inc(S["wide_ready"], 1)

            dve.wait_ge(S["counted"], 1)
            link(nc.vector.tensor_copy(count[0:NE, 0:1], ps_count))
            link(nc.vector.tensor_scalar(first[0:NE, 0, :], steps128[0:NE], count[0:NE, 0:1], 0.0, ALU.is_lt, ALU.add,
                                         accum_out=count[0:NE, 1:2]))
            link(nc.vector.tensor_copy(count16[0:NE, 0:1], count[0:NE, 1:2]))
            nc.vector.tensor_scalar(count_wide[0:NE], ones16[0:NE], count[0:NE, 1:2], None, ALU.mult).then_inc(S["wide_count"], 1)
            dve.wait_ge(S["started"], 1)
            link(nc.vector.tensor_copy(start[0:NB], ps_start))
            link(nc.vector.tensor_tensor(stop[0:NB, 0:1], start[0:NB, 0:1], start[0:NB, 1:2], ALU.add))
            link(nc.vector.tensor_scalar(onehot[0:NB, 0:NS], tile_no[0:NB], start[0:NB, 0:1], None, ALU.is_ge))
            link(nc.vector.scalar_tensor_tensor(out=onehot[0:NB, 0:NS], in0=tile_no[0:NB], scalar=stop[0:NB, 0:1],
                                                in1=onehot[0:NB, 0:NS], op0=ALU.is_lt, op1=ALU.mult))
            nc.vector.tensor_copy(onehot16[0:NE, 0:NS], onehot[0:NE, 0:NS]).then_inc(S["onehot_ready"], 1)
            link(nc.vector.tensor_scalar(base, ps_base, float(P), None, ALU.mult))
            dve.wait_ge(S["ranked"], 1)
            link(nc.vector.tensor_tensor(first, ps_rank, base.unsqueeze(1).to_broadcast([P, NT, E]), ALU.add))
            for k in range(TOPK):
                link(nc.vector.tensor_tensor(best[k], best[k], first, ALU.mult))
                link(nc.vector.tensor_reduce(top[:, 2 + k], best[k], AX, ALU.add))
                link(nc.vector.tensor_copy(slots[:, k], top[:, 2 + k]))
            nc.vector.tensor_copy(top[:, 0], top[:, 1]).then_inc(S["slots_ready"], 1)
            dve.wait_ge(S["tables_done"], 1)
            nc.vector.tensor_copy(tile_expert[0:1], ps_tile).then_inc(S["tables_out"], 1)
            nc.vector.tensor_copy(params, ps_params).then_inc(S["tables_out"], 1)
            dve.wait_ge(S["tables_out"], 2)

            def pick_expert(n, q):
                nc.vector.tensor_scalar(pick[0:NB, q], ones16[0:NB], col(onehot[0:NB], n - NT), None, ALU.mult
                                        ).then_inc(S["pick_ready"], 1)

            def step(n, q, g, tail=True, more=True, shared=False, shared_tail=False):
                s = q % 2
                tile = NS if shared else n - NT
                if more and not (shared and not (isinstance(n, int) and n == NT - 1)):
                    dve.wait_ge(S["y_summed"], n - 2)
                    pick_expert(n + 1, (q + 1) % 4)
                dve.wait_ge(S["h_summed"], n + 1)
                h = ps_h[s].rearrange("p (i two) -> p i two", two=2)

                def c(which):
                    return params_at(params, which, tile)

                nc.vector.tensor_scalar(gate[:, s], h[:, :, 0], c(3), c(5), ALU.min, ALU.max).then_inc(S["swi"], 1)
                nc.vector.tensor_scalar(up[:, s], h[:, :, 1], c(4), c(6), ALU.min, ALU.max).then_inc(S["swi"], 1)
                dve.wait_ge(S["swi"], n * 4 + 2)
                nc.vector.scalar_tensor_tensor(out=up[:, s], in0=up[:, s], scalar=c(2), in1=gate[:, s],
                                               op0=ALU.add, op1=ALU.mult).then_inc(S["swi"], 1)
                dve.wait_ge(S["sig_ready"], n + 1)
                dve.wait_ge(S["swi"], n * 4 + 3)
                nc.vector.scalar_tensor_tensor(out=up[:, s], in0=up[:, s], scalar=c(1), in1=sig[:, s],
                                               op0=ALU.mult, op1=ALU.mult).then_inc(S["swi"], 1)
                if tail and shared_tail:
                    dve.wait_ge(S["y_summed"], n - 1)
                    nc.vector.tensor_tensor(at(x, n - 2), ps_y[s], at(x, n - 2), ALU.add).then_inc(S["z_added"], 1)

            run_tiles(dve, step)
            dve.wait_ge(S["z_added"], NT + 2)

            def combine(t, q, landed):
                dve.wait_ge(y_landed[q], landed)
                nc.vector.scalar_tensor_tensor(out=at(x, t), in0=y_in[:, q, 0], scalar=col(weight[:, 0], t), in1=at(x, t),
                                               op0=ALU.mult, op1=ALU.add).then_inc(S["combined_half"], 1)
                dve.wait_ge(S["combined_half"], t + 1)
                nc.vector.scalar_tensor_tensor(out=at(x, t), in0=y_in[:, q, 1], scalar=col(weight[:, 1], t), in1=at(x, t),
                                               op0=ALU.mult, op1=ALU.add).then_inc(S["combined"], 1)
                dve.wait_ge(S["combined"], t + 1)
                nc.vector.bn_stats(at(stats, t), at(x, t)).then_inc(S["stats_done"], 1)

            with dve.Fori(0, NT // 4) as g:
                for q in range(4):
                    combine(g * 4 + q, q, g * 16 + 16)
            dve.wait_ge(S["stats_done"], NT)


def run_tiles(engine, step):
    for n in (0, 1):
        step(n, n, 0, tail=False, shared=True)
    with engine.Fori(0, (NT - 4) // 4) as g:
        for u in range(4):
            step(g * 4 + (2 + u), (2 + u) % 4, g, shared=True, shared_tail=True)
    for n in range(NT - 2, NT + 2):
        step(n, n % 4, (n - 2) // 4, shared=n < NT, shared_tail=True)
    for n in range(NT + 2, NT + 6):
        step(n, n % 4, (n - 2) // 4)
    with engine.Fori(NT // 4 + 1, (NT + NS - 4) // 4) as g:
        for u in range(4):
            step(g * 4 + (2 + u), (2 + u) % 4, g)
    for n in (NT + NS - 2, NT + NS - 1):
        step(n, n % 4, (n - 2) // 4, more=n < NT + NS - 1)


def rows(view, i):
    tiles = view.rearrange("(t p) d -> t p d", p=P)
    return tiles[i] if isinstance(i, int) else tiles[bass.ds(i, 1)].rearrange("o p d -> (o p) d")


def params_at(params, which, tile):
    return params[:, which, tile:tile + 1] if isinstance(tile, int) else params[:, which, bass.ds(tile, 1)]


def of_expert(w, e, k, rows_=P):
    if isinstance(e, int):
        return w[0:rows_, e, k, :]
    return w[0:rows_, bass.ds(e, 1), k, :].squeeze(1)


def attention(nc, dram, mem, sem):
    x, edges = mem["x"], mem["edges"]
    identity = mem["identity"]
    mean, rstd = mem["mean"], mem["rstd"]
    psum = mem["PSUM"]
    H = 128
    SLOPE = 0.01
    LOG_SCALE = float(np.log(SCALE16))
    CHUNK = 4
    CHUNKS = NJ // CHUNK
    PLAIN = CHUNKS // 2
    NTP = PLAIN * CHUNK
    assert 2 * NTP == NT
    plain = mem["XLN"][:, 0:NTP * D].rearrange("p (t d) -> p t d", d=D)
    ln16 = mem["XLN"][:, NTP * D:NT * D].bitcast(FP16).rearrange("p (t d) -> p t d", d=2 * D)
    arena = Region(mem["ARENA"], mem["ARENA"].shape[1])
    edge_in = arena.take(BF16, 2, N)
    s_row, l_row, p_row = arena.take(F32, 2, N), arena.take(F32, 2, N), arena.take(F32, 2, N)
    pT = arena.take(F32, PLAIN, CHUNK * P)
    pT_high, pT_low = (arena.take(FP16, CHUNKS - PLAIN, CHUNK * P) for _ in range(2))
    f2 = arena.take(F32, N)
    split = l_row[:, 0].rearrange("p (t d) -> p t d", d=D)
    halves = ((slice(0, NTP), plain), (slice(NTP, NT), split))
    product = [v.rearrange("p s (t d) -> p (s t) d", d=D) for v in (p_row, s_row)]
    small = Region(mem["SMALL"], SMALL_WORDS)
    w1, w23 = small.take(F32, D), small.take(F32, 2)
    b2, b3 = small.take(F32, 2), small.take(F32, 2)
    u_wide = small.take(F32, 2, D)
    stats, var, tmp, slope, offset = mem["stats"], *(small.take(F32, NT) for _ in range(4))
    f1, f1_high, f1_low, f2_col, total, inverse = (small.take(F32, NT) for _ in range(6))
    largest, minus, bound, waited = (small.take(F32, 2) for _ in range(4))
    vals = small.take(F32, 2, D)
    most, least = mem["most"], mem["least"]

    bank = [psum[:, 512 * b:512 * (b + 1)] for b in range(8)]
    ps_u = bank[6].rearrange("p (c d) -> p c d", d=D)
    ps_sum = [bank[6 + s][:, 0:D] for s in range(2)]

    names = ("w_in", "dve_chain", "var_ready", "sd_ready", "slope_ready", "u_summed", "u_ready", "scaled_ready",
             "high_ready", "split_done", "product_ready", "f2_col_ready", "f2_wide", "f2_out", "f1_low_ready", "s_ready",
             "minus_ready", "low_ready", "l_ready", "p_ready", "p_turned", "pT_ready", "pT_high_ready", "pT_low_ready", "summed",
             "inverse_ready", "vals_ready", "x_added", "bound_ready", "stats_done")
    S = {name: sem("c_" + name) for name in names}
    edge_landed = [sem(f"c_edge_landed{s}") for s in range(2)]

    with nc.Block() as block:

        @block.sync
        def _(sp):
            sp.dma_start(w1, dram["L1_gnn_W1"]).then_inc(S["w_in"], 16)
            for c, name in enumerate(("L1_gnn_w2", "L1_gnn_w3")):
                sp.dma_start(w23[:, c:c + 1], dram[name].rearrange("(p o) -> p o", o=1),
                             allow_slow_non_contiguous=True).then_inc(S["w_in"], 16)
            for view, name in ((b2, "L1_gnn_b2"), (b3, "L1_gnn_b3")):
                sp.dma_start(view[:, 0:1], dram[name].rearrange("(p o) -> p o", o=1).to_broadcast([P, 1]),
                             allow_slow_non_contiguous=True).then_inc(S["w_in"], 16)
            for i in range(2):
                sp.dma_start(edge_in[:, i], edges[:, i]).then_inc(edge_landed[i], 16)
            with sp.Fori(1, NT // 2) as g:
                for q in range(2):
                    sp.wait_ge(S["s_ready"], g * 2 + (q - 1))
                    sp.dma_start(edge_in[:, q], at(edges, g * 2 + q)).then_inc(edge_landed[q], 16)

        @block.gpsimd
        def _(pool):
            pool.wait_ge(S["slope_ready"], 1)
            for tiles, view in reversed(halves):
                for t in range(NTP):
                    at_t = tiles.start + t
                    nc.gpsimd.tensor_scalar(view[:, t], x[:, at_t], col(slope, at_t), col(offset, at_t), ALU.mult, ALU.add
                                            ).then_inc(S["scaled_ready"], 1)
            pool.wait_ge(S["u_ready"], 1)
            pool.wait_ge(S["scaled_ready"], NT)
            for tiles, view in halves:
                nc.gpsimd.tensor_tensor(product[0][:, tiles], view, u_wide[:, 0].unsqueeze(1).to_broadcast([P, NTP, D]),
                                        ALU.mult).then_inc(S["product_ready"], 1)

        @block.scalar
        def _(act):
            act.wait_ge(S["var_ready"], 1)
            nc.scalar.activation(var, var, ACT.Sqrt).then_inc(S["sd_ready"], 1)
            act.wait_ge(S["slope_ready"], 1)
            with act.Fori(0, NTP) as t:
                nc.scalar.activation(at(ln16, t)[:, 0:D], at(x, t + NTP), ACT.Identity, bias=col(offset, t + NTP),
                                     scale=col(slope, t + NTP)
                                     ).then_inc(S["high_ready"], 1)
            for c in range(NT * P // 512):
                act.wait_ge(S["f2_wide"], c + 1)
                nc.scalar.activation(f2[:, c * 512:(c + 1) * 512], bank[c], ACT.Copy).then_inc(S["f2_out"], 1)

            def low(i, s):
                act.wait_ge(S["s_ready"], i + 1)
                nc.scalar.activation(l_row[:, s], s_row[:, s], ACT.Identity, bias=col(f1_low, i), scale=SLOPE
                                     ).then_inc(S["low_ready"], 1)

            def exponent(i, s):
                act.wait_ge(S["l_ready"], i + 1)
                act.wait_ge(S["minus_ready"], i + 1)
                nc.scalar.activation(p_row[:, s], l_row[:, s], ACT.Exp, bias=minus[:, s:s + 1],
                                     accum_out=col(total, i)).then_inc(S["p_ready"], 1)

            def turned_out(i, c):
                act.wait_ge(S["p_turned"], i * CHUNKS + (c + 1))
                if c < PLAIN:
                    nc.scalar.activation(pT[:, c], bank[c], ACT.Copy).then_inc(S["pT_ready"], 1)
                else:
                    nc.scalar.activation(pT_high[:, c - PLAIN], bank[c], ACT.Copy).then_inc(S["pT_high_ready"], 1)

            def weighted(i, s):
                act.wait_ge(S["summed"], i + 1)
                act.wait_ge(S["inverse_ready"], i + 1)
                act.wait_ge(S["x_added"], i + 1)
                nc.scalar.activation(vals[:, s], ps_sum[s], ACT.Relu, scale=col(inverse, i)).then_inc(S["vals_ready"], 1)

            def step(i, s, more=2, first=False):
                for c in range(CHUNKS - 1):
                    turned_out(i, c)
                if more >= 1:
                    exponent(i + 1, 1 - s)
                turned_out(i, CHUNKS - 1)
                if not first:
                    weighted(i - 1, 1 - s)
                if more >= 2:
                    act.wait_ge(S["p_ready"], i + 1)
                    low(i + 2, s)

            act.wait_ge(S["f1_low_ready"], 1)
            low(0, 0)
            low(1, 1)
            exponent(0, 0)
            step(0, 0, first=True)
            with act.Fori(0, (NT - 4) // 2) as g:
                for q in range(2):
                    step(g * 2 + (1 + q), (1 + q) % 2)
            step(NT - 3, 1)
            step(NT - 2, 0, more=1)
            step(NT - 1, 1, more=0)
            weighted(NT - 1, 1)

        @block.tensor
        def _(pe):
            pe.wait_ge(S["w_in"], 16 * 5)
            for c in range(2):
                last = nc.tensor.matmul(ps_u[:, c], w23[:, c:c + 1].to_broadcast([H, P]), w1, start=True, stop=True)
            last.then_inc(S["u_summed"], 1)
            pe.wait_ge(S["f2_col_ready"], 1)
            for c in range(NT * P // 512):
                for b in range(CHUNK):
                    t = c * CHUNK + b
                    last = nc.tensor.matmul(bank[c][:, b * P:(b + 1) * P], f2_col[:, t:t + 1].to_broadcast([P, P]), identity,
                                            start=True, stop=True)
                last.then_inc(S["f2_wide"], 1)

            def turn(i, s, c):
                pe.wait_ge(S["p_ready"], i + 1)
                for b in range(CHUNK):
                    j = c * CHUNK + b
                    last = nc.tensor.transpose(bank[c][:, b * P:(b + 1) * P], p_row[:, s, j * P:(j + 1) * P], identity)
                last.then_inc(S["p_turned"], 1)

            def weigh(i, s, c):
                if c == 0:
                    pe.wait_ge(S["vals_ready"], i + 1)
                if c < PLAIN:
                    pe.wait_ge(S["pT_ready"], i * PLAIN + (c + 1))
                else:
                    pe.wait_ge(S["pT_low_ready"], i * (CHUNKS - PLAIN) + (c - PLAIN + 1))
                for b in range(CHUNK):
                    j, here = c * CHUNK + b, slice(b * P, (b + 1) * P)
                    if c < PLAIN:
                        nc.tensor.matmul(ps_sum[s], pT[:, c, here], plain[:, j], start=(j == 0), stop=False)
                    else:
                        high, low = pT_high[:, c - PLAIN, here], pT_low[:, c - PLAIN, here]
                        nc.tensor.matmul(ps_sum[s], high, ln16[:, j - NTP, 0:D], start=False, stop=False)
                        nc.tensor.matmul(ps_sum[s], high, ln16[:, j - NTP, D:2 * D], start=False, stop=False)
                        last = nc.tensor.matmul(ps_sum[s], low, ln16[:, j - NTP, 0:D], start=False, stop=(j == NJ - 1))
                if c == CHUNKS - 1:
                    last.then_inc(S["summed"], 1)

            def step(i, s, more=True):
                turn(i, s, 2)
                weigh(i, s, 0)
                turn(i, s, 3)
                weigh(i, s, 1)
                weigh(i, s, 2)
                if more:
                    turn(i + 1, 1 - s, 0)
                    turn(i + 1, 1 - s, 1)
                weigh(i, s, 3)

            pe.sem_inc(S["vals_ready"], 2)
            pe.wait_ge(S["f2_out"], CHUNKS)
            pe.wait_ge(S["split_done"], NTP)
            turn(0, 0, 0)
            turn(0, 0, 1)
            step(0, 0)
            with pe.Fori(0, (NT - 2) // 2) as g:
                for q in range(2):
                    step(g * 2 + (1 + q), (1 + q) % 2)
            step(NT - 1, 1, more=False)

        @block.vector
        def _(dve):
            chain = Chain(dve, S["dve_chain"])
            link = chain.link
            dve.sem_inc(S["x_added"], 2)
            layernorm_spread(dve, nc, chain, stats, mean, var, tmp).then_inc(S["var_ready"], 1)
            dve.wait_ge(S["sd_ready"], 1)
            link(nc.vector.reciprocal(rstd, var))
            link(nc.vector.tensor_scalar(slope, rstd, SCALE16, None, ALU.mult))
            nc.vector.scalar_tensor_tensor(out=offset, in0=mean, scalar=-1.0, in1=slope, op0=ALU.mult, op1=ALU.mult
                                           ).then_inc(S["slope_ready"], 1)
            dve.wait_ge(S["u_summed"], 1)
            nc.vector.tensor_scalar(u_wide, ps_u, 1.0 / SCALE16, None, ALU.mult).then_inc(S["u_ready"], 1)
            with dve.Fori(0, NTP) as t:
                dve.wait_ge(S["high_ready"], t + 1)
                dve.wait_ge(S["scaled_ready"], t + 1)
                nc.vector.tensor_tensor(at(ln16, t)[:, D:2 * D], at(split, t), at(ln16, t)[:, 0:D], ALU.subtract
                                        ).then_inc(S["split_done"], 1)
            dve.wait_ge(S["scaled_ready"], NT)
            dve.wait_ge(S["u_ready"], 1)
            for tiles, view in halves:
                link(nc.vector.tensor_tensor(product[1][:, tiles], view, u_wide[:, 1].unsqueeze(1).to_broadcast([P, NTP, D]),
                                             ALU.mult))
            link(nc.vector.tensor_reduce(f2_col, product[1], AX, ALU.add))
            dve.wait_ge(S["w_in"], 16 * 5)
            nc.vector.tensor_scalar(f2_col, f2_col, b3[:, 0:1], None, ALU.add).then_inc(S["f2_col_ready"], 1)
            dve.wait_ge(S["product_ready"], 2)
            link(nc.vector.tensor_reduce(f1, product[0], AX, ALU.add))
            link(nc.vector.tensor_scalar(f1, f1, b2[:, 0:1], None, ALU.add))
            link(nc.vector.tensor_scalar(f1_high, f1, LOG_SCALE, None, ALU.add))
            nc.vector.tensor_scalar(f1_low, f1, SLOPE, LOG_SCALE, ALU.mult, ALU.add).then_inc(S["f1_low_ready"], 1)
            dve.wait_ge(S["f1_low_ready"], 1)
            dve.wait_ge(S["f2_out"], CHUNKS)

            def masked(i, s, landed):
                dve.wait_ge(edge_landed[s], landed)
                if not (isinstance(i, int) and i < 2):
                    dve.wait_ge(S["l_ready"], i - 1)
                nc.vector.memset(waited[:, s:s + 1], 0.0)
                nc.vector.tensor_tensor_reduce(out=s_row[:, s], in0=f2, in1=edge_in[:, s], scale=1.0, scalar=-3.0e38,
                                               op0=ALU.add, op1=ALU.max, accum_out=largest[:, s:s + 1]
                                               ).then_inc(S["s_ready"], 1)

            def limit(i, s):
                dve.wait_ge(S["s_ready"], i + 1)
                nc.vector.tensor_scalar(bound[:, s:s + 1], largest[:, s:s + 1], col(f1, i), -1.0, ALU.add, ALU.mult
                                        ).then_inc(S["bound_ready"], 1)
                dve.wait_ge(S["bound_ready"], i + 1)
                nc.vector.scalar_tensor_tensor(out=minus[:, s:s + 1], in0=bound[:, s:s + 1], scalar=SLOPE,
                                               in1=bound[:, s:s + 1], op0=ALU.mult, op1=ALU.min).then_inc(S["minus_ready"], 1)

            def leaky(i, s):
                dve.wait_ge(S["low_ready"], i + 1)
                nc.vector.scalar_tensor_tensor(out=l_row[:, s], in0=s_row[:, s], scalar=col(f1_high, i), in1=l_row[:, s],
                                               op0=ALU.add, op1=ALU.max).then_inc(S["l_ready"], 1)

            def low_half(i, c):
                dve.wait_ge(S["pT_high_ready"], i * (CHUNKS - PLAIN) + (c + 1))
                nc.vector.tensor_tensor(pT_low[:, c], bank[PLAIN + c], pT_high[:, c], ALU.subtract
                                        ).then_inc(S["pT_low_ready"], 1)

            def invert(i):
                nc.vector.reciprocal(col(inverse, i), col(total, i)).then_inc(S["inverse_ready"], 1)

            def finish(i, s):
                dve.wait_ge(S["vals_ready"], i + 3)
                nc.vector.scalar_tensor_tensor(out=at(x, i), in0=vals[:, s], scalar=1.0 / SCALE16, in1=at(x, i),
                                               op0=ALU.mult, op1=ALU.add).then_inc(S["x_added"], 1)
                dve.wait_ge(S["x_added"], i + 3)
                nc.vector.bn_stats(at(stats, i), at(x, i)).then_inc(S["stats_done"], 1)
                nc.vector.tensor_reduce(col(most, i), at(x, i), AX, ALU.max).then_inc(S["stats_done"], 1)
                nc.vector.tensor_reduce(col(least, i), at(x, i), AX, ALU.min).then_inc(S["stats_done"], 1)

            def step(i, s, more=2, landed=None, first=False):
                if more >= 1:
                    leaky(i + 1, 1 - s)
                low_half(i, 0)
                if more >= 2:
                    masked(i + 2, s, landed)
                low_half(i, 1)
                if more >= 2:
                    dve.wait_ge(S["p_ready"], i + 1)
                    limit(i + 2, s)
                invert(i)
                if not first:
                    finish(i - 2, s)

            masked(0, 0, 16)
            limit(0, 0)
            masked(1, 1, 16)
            limit(1, 1)
            leaky(0, 0)
            step(0, 0, landed=32, first=True)
            step(1, 1, landed=32, first=True)
            with dve.Fori(1, (NT - 2) // 2) as g:
                for q in range(2):
                    step(g * 2 + q, q, landed=(g + 2) * 16)
            step(NT - 2, 0, more=1)
            step(NT - 1, 1, more=0)
            finish(NT - 2, 0)
            finish(NT - 1, 1)
            dve.wait_ge(S["stats_done"], 3 * NT)



def fp8_product(nc, dram, mem, sem):
    x = mem["x"]
    identity, identity16, ones = mem["identity"], mem["identity16"], mem["ones"]
    mean, rstd = mem["mean"], mem["rstd"]
    psum = mem["PSUM"]
    arena = Region(mem["ARENA"], mem["ARENA"].shape[1])
    PAIR = 4
    NPAIR = NT // PAIR
    weight, w_clip = arena.take(F32, KD * D), arena.take(F32, KD * D)
    w_exp, w_c, w_sum = (arena.take(F32, KD * D) for _ in range(3))
    w8 = arena.take(BF16, KD, D)
    v, clip, exponent_, c_, sum_ = (arena.take(F32, 2, PAIR * D) for _ in range(5))
    q8 = arena.take(BF16, 2, PAIR * D)
    qT = arena.take(BF16, 2, PAIR * KD, P)
    result = arena.take(F32, 2, PAIR, D)
    small = Region(mem["SMALL"], SMALL_WORDS)
    stats, var, tmp = mem["stats"], small.take(F32, NT), small.take(F32, NT)
    high, low = mem["most"], mem["least"]
    w_high = small.take(F32, 2)
    largest = small.take(F32, 2)
    largest_row = small.take(F32, 2)
    amax, scale8, unscale = (small.take(F32, 2) for _ in range(3))
    out_scale = small.take(F32, 2)
    slope, offset = small.take(F32, NT), small.take(F32, NT)
    MAGIC = 1.5 * 2.0 ** (23 - 3)
    LEAST = 2.0 ** -6

    bank = [psum[:, 512 * b:512 * (b + 1)] for b in range(8)]
    ps_rows = bank[6][0:1, 0:2 * P].rearrange("p (c q) -> p c q", q=P)
    ps_wide = bank[7][:, 0:2]
    ps_q = [bank[s][:, 0:PAIR * KD * P // 2].bitcast(BF16).rearrange("p (b q) -> p b q", q=P) for s in range(2)]
    ps_out = [psum[:, (1 + s) * PAIR * D:(2 + s) * PAIR * D] for s in range(2)]

    names = ("w_in", "dve_chain", "stats_done", "var_ready", "sd_ready", "largest_ready", "rows_turned", "row_ready",
             "wide_ready", "scales_ready", "v_ready", "rounded", "w8_ready", "q_ready", "q_turned", "qT_ready", "summed", "result_ready")
    S = {name: sem("d_" + name) for name in names}
    stored = [sem(f"d_stored{s}") for s in range(2)]
    out_pairs = mem["out"].rearrange("(h t p) d -> h p t d", t=PAIR, p=P)

    with nc.Block() as block:

        @block.sync
        def _(sp):
            sp.dma_start(weight.rearrange("p (k d) -> p k d", d=D), dram["L1_ffn_weight"].rearrange("(k p) d -> p k d", p=P)
                         ).then_inc(S["w_in"], 16)
            with sp.Fori(0, NPAIR // 2) as g:
                for s in range(2):
                    sp.wait_ge(S["result_ready"], g * 2 + (s + 3))
                    sp.dma_start(out_pairs[bass.ds(g * 2 + s, 1)].rearrange("o p t d -> (o p) t d"), result[:, s]
                                 ).then_inc(stored[s], 16)
            for s in range(2):
                sp.wait_ge(stored[s], 16 * (NPAIR // 2 + 1))

        @block.scalar
        def _(act):
            act.wait_ge(S["var_ready"], 1)
            nc.scalar.activation(var, var, ACT.Sqrt).then_inc(S["sd_ready"], 1)

            def scaled(h, s):
                for t in range(PAIR):
                    nc.scalar.activation(v[:, s, t * D:(t + 1) * D], at(x, h * PAIR + t), ACT.Identity,
                                         bias=col(offset, h * PAIR + t), scale=col(slope, h * PAIR + t)
                                         ).then_inc(S["v_ready"], 1)

            def qT_out(h, s):
                act.wait_ge(S["q_turned"], h + 1)
                nc.scalar.activation(qT[:, s], ps_q[s], ACT.Copy).then_inc(S["qT_ready"], 1)

            act.wait_ge(S["scales_ready"], 1)
            scaled(0, 0)
            with act.Fori(0, NPAIR // 2 - 1) as g:
                for s in range(2):
                    act.wait_ge(S["rounded"], (g * 2 + s) * 4 + 1)
                    scaled(g * 2 + (s + 1), 1 - s)
                    qT_out(g * 2 + s, s)
            act.wait_ge(S["rounded"], (NPAIR - 2) * 4 + 1)
            scaled(NPAIR - 1, 1)
            qT_out(NPAIR - 2, 0)
            qT_out(NPAIR - 1, 1)

        @block.tensor
        def _(pe):
            pe.wait_ge(S["largest_ready"], 1)
            for c in range(2):
                last = nc.tensor.transpose(ps_rows[:, c, :], largest[:, c:c + 1], identity)
            last.then_inc(S["rows_turned"], 1)
            pe.wait_ge(S["row_ready"], 1)
            nc.tensor.matmul(ps_wide, ones[0:1, :], largest_row[0:1], start=True, stop=True).then_inc(S["wide_ready"], 1)

            def turn(h, s):
                pe.wait_ge(S["q_ready"], h + 1)
                for b in range(PAIR * KD):
                    last = nc.tensor.transpose(ps_q[s][:, b, :], q8[:, s, b * P:(b + 1) * P], identity16)
                last.then_inc(S["q_turned"], 1)

            def product(h, s):
                pe.wait_ge(S["qT_ready"], h + 1)
                pe.wait_ge(S["result_ready"], h + 1)
                for t in range(PAIR):
                    for k in range(KD):
                        last = nc.tensor.matmul(ps_out[s][:, t * D:(t + 1) * D], qT[:, s, t * KD + k, :], w8[:, k, :],
                                                start=(k == 0), stop=(k == KD - 1))
                last.then_inc(S["summed"], 1)

            turn(0, 0)
            pe.wait_ge(S["w8_ready"], 1)
            with pe.Fori(0, NPAIR // 2 - 1) as g:
                turn(g * 2 + 1, 1)
                product(g * 2, 0)
                turn(g * 2 + 2, 0)
                product(g * 2 + 1, 1)
            turn(NPAIR - 1, 1)
            product(NPAIR - 2, 0)
            product(NPAIR - 1, 1)

        @block.vector
        def _(dve):
            chain = Chain(dve, S["dve_chain"])
            link = chain.link
            dve.sem_inc(S["rounded"], 4)
            dve.sem_inc(S["result_ready"], 2)
            for s in range(2):
                dve.sem_inc(stored[s], 16)
            layernorm_spread(dve, nc, chain, stats, mean, var, tmp).then_inc(S["var_ready"], 1)
            dve.wait_ge(S["w_in"], 16)
            link(nc.vector.tensor_reduce(w_high[:, 0:1], weight, AX, ALU.max))
            link(nc.vector.tensor_reduce(w_high[:, 1:2], weight, AX, ALU.min))
            link(nc.vector.scalar_tensor_tensor(out=largest[:, 1:2], in0=w_high[:, 1:2], scalar=-1.0, in1=w_high[:, 0:1],
                                                op0=ALU.mult, op1=ALU.max))
            dve.wait_ge(S["sd_ready"], 1)
            link(nc.vector.reciprocal(rstd, var))
            for view in (high, low):
                link(nc.vector.tensor_tensor(view, view, mean, ALU.subtract))
                link(nc.vector.tensor_tensor(view, view, rstd, ALU.mult))
            link(nc.vector.scalar_tensor_tensor(out=high, in0=low, scalar=-1.0, in1=high, op0=ALU.mult, op1=ALU.max))
            nc.vector.tensor_reduce(largest[:, 0:1], high, AX, ALU.max).then_inc(S["largest_ready"], 1)
            dve.wait_ge(S["rows_turned"], 1)
            nc.vector.tensor_reduce(largest_row[0:1], ps_rows, AX, ALU.max).then_inc(S["row_ready"], 1)
            dve.wait_ge(S["wide_ready"], 1)
            link(nc.vector.tensor_scalar(amax, ps_wide, 1e-12, None, ALU.max))
            link(nc.vector.reciprocal(scale8, amax))
            link(nc.vector.tensor_scalar(scale8, scale8, FP8_MAX, None, ALU.mult))
            link(nc.vector.reciprocal(unscale, scale8))
            link(nc.vector.tensor_tensor(out_scale[:, 0:1], unscale[:, 0:1], unscale[:, 1:2], ALU.mult))
            link(nc.vector.tensor_scalar(slope, rstd, scale8[:, 0:1], None, ALU.mult))
            nc.vector.scalar_tensor_tensor(out=offset, in0=mean, scalar=-1.0, in1=slope, op0=ALU.mult, op1=ALU.mult
                                           ).then_inc(S["scales_ready"], 1)

            def round_pair(h, s):
                dve.wait_ge(S["v_ready"], (h + 1) * PAIR)
                nc.vector.tensor_scalar(clip[:, s], v[:, s], FP8_MAX, -FP8_MAX, ALU.min, ALU.max).then_inc(S["rounded"], 1)
                dve.wait_ge(S["rounded"], h * 4 + 5)
                nc.vector.tensor_scalar(exponent_[:, s].bitcast(I32), clip[:, s].bitcast(I32), 0x7F800000, None,
                                        ALU.bitwise_and).then_inc(S["rounded"], 1)
                dve.wait_ge(S["rounded"], h * 4 + 6)
                nc.vector.tensor_scalar(c_[:, s], exponent_[:, s], LEAST, MAGIC, ALU.max, ALU.mult).then_inc(S["rounded"], 1)
                dve.wait_ge(S["rounded"], h * 4 + 7)
                nc.vector.tensor_tensor(sum_[:, s], clip[:, s], c_[:, s], ALU.add).then_inc(S["rounded"], 1)
                dve.wait_ge(S["rounded"], h * 4 + 8)
                nc.vector.tensor_tensor(q8[:, s], sum_[:, s], c_[:, s], ALU.subtract).then_inc(S["q_ready"], 1)

            def finish(h, s, stored_):
                dve.wait_ge(S["summed"], h + 1)
                dve.wait_ge(stored[s], stored_)
                nc.vector.scalar_tensor_tensor(out=result[:, s].rearrange("p t d -> p (t d)"), in0=ps_out[s],
                                               scalar=out_scale[:, 0:1], in1=pair_of(x, h, PAIR), op0=ALU.mult, op1=ALU.add
                                               ).then_inc(S["result_ready"], 1)

            round_pair(0, 0)
            link(nc.vector.tensor_scalar(w_clip, weight, scale8[:, 1:2], FP8_MAX, ALU.mult, ALU.min))
            link(nc.vector.tensor_scalar(w_clip, w_clip, -FP8_MAX, None, ALU.max))
            link(nc.vector.tensor_scalar(w_exp.bitcast(I32), w_clip.bitcast(I32), 0x7F800000, None, ALU.bitwise_and))
            link(nc.vector.tensor_scalar(w_c, w_exp, LEAST, MAGIC, ALU.max, ALU.mult))
            link(nc.vector.tensor_tensor(w_sum, w_clip, w_c, ALU.add))
            nc.vector.tensor_tensor(w8.rearrange("p k d -> p (k d)"), w_sum, w_c, ALU.subtract).then_inc(S["w8_ready"], 1)
            round_pair(1, 1)
            finish(0, 0, 16)
            with dve.Fori(1, NPAIR // 2) as g:
                for s in range(2):
                    dve.wait_ge(S["q_turned"], g * 2 + (s - 1))
                    round_pair(g * 2 + s, s)
                    finish(g * 2 + (s - 1), 1 - s, (g + s) * 16)
            finish(NPAIR - 1, 1, NPAIR // 2 * 16)


def pair_of(view, h, tiles):
    if isinstance(h, int):
        return view[:, tiles * h:tiles * (h + 1)].rearrange("p t d -> p (t d)")
    return view[:, bass.ds(h * tiles, tiles)].rearrange("p t d -> p (t d)")


def lay_out(inputs):
    return {name: np.ascontiguousarray(inputs[name]) for name in inputs}


def kernel(**inputs):
    import concourse.bacc as bacc
    from concourse.bass_utils import run_bass_kernel_spmd

    nc = bacc.Bacc("TRN2", target_bir_lowering=False, num_devices=1)
    arrays = lay_out(inputs)
    build(nc, arrays)
    r = run_bass_kernel_spmd(nc, [arrays], core_ids=[0])
    return r.results[0]["out_0_dram"]
```

```python
from contextlib import ExitStack

import numpy as np

import concourse.bass as bass
from concourse import mybir

F32 = mybir.dt.float32
BF16 = mybir.dt.bfloat16
FP16 = mybir.dt.float16
I32 = mybir.dt.int32
U32 = mybir.dt.uint32
ALU = mybir.AluOpType
ACT = mybir.ActivationFunctionType
AX = mybir.AxisListType.X

P = 128
N = 2048
D = 256
NT = N // P
KD = D // P
NJ = N // P
E = 16
NE = E + 1
I2 = 384
I = I2 // 2
KI = 2
IH = I // KI
TOPK = 2
NS = (N * TOPK + E * (P - 1)) // P
ZERO_ROWS = 8
ZERO_DMAS = -(-NS // ZERO_ROWS)
SPARE = ZERO_ROWS * P
PARTS = 3
NB = NE * PARTS
EPS = 1e-5
SCALE16 = 2048.0
NO_EDGE = -float(2 ** 30)
FP8_MAX = 448.0
SMALL_WORDS = 5660


class Region:

    def __init__(self, tensor, words):
        self.tensor, self.words, self.at = tensor, words, 0

    def take(self, dtype, *shape, rows=P):
        size = int(np.prod(shape))
        words = -(-size * (2 if dtype in (BF16, FP16) else 4) // 4)
        words += words % 2
        assert self.at + words <= self.words, (self.at, words, self.words)
        view = self.tensor[0:rows, self.at:self.at + words]
        self.at += words
        if dtype != F32:
            view = view.bitcast(dtype)
        view = view[:, 0:size]
        if len(shape) == 2:
            view = view.rearrange("p (a b) -> p a b", b=shape[1])
        elif len(shape) == 3:
            view = view.rearrange("p (a b c) -> p a b c", b=shape[1], c=shape[2])
        return view


class Chain:

    def __init__(self, engine, semaphore):
        self.engine, self.semaphore, self.count = engine, semaphore, 0

    def link(self, instruction):
        self.count += 1
        instruction.then_inc(self.semaphore, 1)
        self.engine.wait_ge(self.semaphore, self.count)


def at(view, i):
    if isinstance(i, int):
        return view[:, i]
    one = view[:, bass.ds(i, 1)]
    return one.squeeze(1) if len(one.shape) > 2 else one


def build(nc, arrays):
    with ExitStack() as ctx:
        _build(nc, arrays, ctx)


def _build(nc, arrays, ctx):
    dram = {}
    for name, v in arrays.items():
        dram[name] = nc.dram_tensor(name, v.shape, mybir.dt.from_np(v.dtype), kind="ExternalInput").ap()
    out = nc.dram_tensor("out_0_dram", (N, D), F32, kind="ExternalOutput").ap()
    slot_x = nc.dram_tensor("slot_x", (ZERO_DMAS * ZERO_ROWS * P, D + 2), F32, kind="Internal").ap()
    token_y = nc.dram_tensor("token_y", (SPARE + TOPK * N, D), F32, kind="Internal").ap()

    def sb(name, words):
        return ctx.enter_context(nc.sbuf_tensor(name, [P, words], F32))

    ARENA_WORDS = NE * KD * I2 + NE * KI * D
    mem = {
        "X": sb("X", NT * D), "XLN": sb("XLN", NT * (D + 2)), "EDGES": sb("EDGES", NT * N // 2),
        "ARENA": sb("ARENA", ARENA_WORDS), "SMALL": sb("SMALL", SMALL_WORDS),
        "PSUM": ctx.enter_context(nc.psum_tensor("PSUM", [P, 8 * 512], F32)),
        "slot_x": slot_x, "token_y": token_y, "out": out,
    }
    mem["x"] = mem["X"][:, :].rearrange("p (t d) -> p t d", d=D)
    mem["xln_row"] = mem["XLN"][:, :].rearrange("p (t d) -> p t d", d=D + 2)
    mem["xln"] = mem["xln_row"][:, :, 0:D]
    mem["edges"] = mem["EDGES"][:, :].bitcast(BF16).rearrange("p (t n) -> p t n", n=N)
    CONST_WORDS = 1176
    mem["weight8"] = mem["ARENA"][:, ARENA_WORDS - KD * D:]
    mem["CONST"] = sb("CONST", CONST_WORDS)
    mem["const"] = const = Region(mem["CONST"], CONST_WORDS)
    mem["identity"] = const.take(F32, P)
    mem["identity16"] = const.take(BF16, P)
    mem["ones"] = const.take(F32, P)
    mem["mean"] = const.take(F32, NT)
    mem["rstd"] = const.take(F32, NT)
    mem["stats"] = const.take(F32, NT, 6)
    mem["most"], mem["least"] = const.take(F32, NT), const.take(F32, NT)
    mem["f_raw"], mem["u_sum"], mem["f_bias"] = const.take(F32, 2, NT), const.take(F32, 2), const.take(F32, 2)
    def sem(name):
        return ctx.enter_context(nc.semaphore(name))

    mem["gate_w"], mem["gate_b"] = const.take(F32, KD, E), const.take(F32, E, rows=1)
    mem["gate_in"], mem["weight8_in"] = sem("gate_in"), sem("weight8_in")
    mem["w_extremes"] = const.take(F32, 2)

    mean_aggregate(nc, dram, mem, sem)
    mixture(nc, dram, mem, sem)
    attention(nc, dram, mem, sem)
    fp8_product(nc, mem, sem)


def layernorm_spread(nc, chain, stats, mean, var, tmp):
    me, mo, se, so = stats[:, :, 1], stats[:, :, 4], stats[:, :, 2], stats[:, :, 5]
    chain.link(nc.vector.tensor_tensor(mean, me, mo, ALU.add))
    chain.link(nc.vector.tensor_tensor(tmp, me, mo, ALU.subtract))
    chain.link(nc.vector.tensor_tensor(var, se, so, ALU.add))
    chain.link(nc.vector.tensor_scalar(mean, mean, 0.5, None, ALU.mult))
    chain.link(nc.vector.scalar_tensor_tensor(out=tmp, in0=tmp, scalar=0.25, in1=tmp, op0=ALU.mult, op1=ALU.mult))
    chain.link(nc.vector.tensor_scalar(var, var, 1.0 / D, EPS, ALU.mult, ALU.add))
    return nc.vector.tensor_tensor(var, var, tmp, ALU.add)



def mean_aggregate(nc, dram, mem, sem):
    x, edges = mem["x"], mem["edges"]
    identity, identity16, ones = mem["identity"], mem["identity16"], mem["ones"]
    mean, rstd = mem["mean"], mem["rstd"]
    psum = mem["PSUM"]
    arena = Region(mem["ARENA"], mem["ARENA"].shape[1])
    STAGES = 4
    adj_in = arena.take(I32, STAGES, N)
    ln16 = arena.take(FP16, NT, 2 * D)
    maskT = arena.take(BF16, 2, NJ, P)
    mask = arena.take(BF16, 2, N)
    w_self, w_nb = arena.take(F32, KD, D), arena.take(F32, KD, D)
    w_comb = arena.take(F32, 2 * KD, D)
    small = Region(mem["SMALL"], SMALL_WORDS)
    wx, wa = small.take(F32, KD, D), small.take(F32, KD, D)
    b_row = small.take(F32, 2 * D, rows=1)
    b_wide = small.take(F32, 2 * KD * P)
    b_comb = small.take(F32, D, rows=1)
    bias = small.take(F32, D)
    stats = mem["stats"]
    var, tmp, slope, offset = (small.take(F32, NT) for _ in range(4))
    deg, rdeg = small.take(F32, STAGES), small.take(F32, STAGES)
    xn = small.take(F32, 2, D)
    agg_low, agg = small.take(F32, 2, D), small.take(F32, 2, D)
    w_selfT, w_nbT = agg_low, agg
    assert KD == 2
    xnT, aggT = arena.take(F32, 2, KD, P), arena.take(F32, 2, KD, P)
    out_b = small.take(F32, 2, D)
    scaled = mem["xln"]
    zeros = arena.take(F32, ZERO_ROWS * (D + 2))

    ps_mask = [psum[:, 1024 * s:1024 * (s + 1)].bitcast(BF16).rearrange("p (j q) -> p j q", q=P)[:, 0:NJ, :] for s in range(2)]
    ps_agg = [psum[:, 2048 + 512 * s:2048 + 512 * (s + 1)] for s in range(2)]
    ps_turn = psum[:, 3072:3584].rearrange("p (k q) -> p k q", q=P)
    ps_out = psum[:, 3584:3584 + D]

    XCHUNK = 4
    x_in = [sem(f"a_x_in{c}") for c in range(NT // XCHUNK)]
    w_in = sem("a_w_in")
    adj_landed = [sem(f"a_adj_landed{s}") for s in range(STAGES)]
    zeros_ready = sem("a_zeros_ready")
    slots_zeroed = sem("slots_zeroed")
    mem["slots_zeroed"] = slots_zeroed
    const_ready = sem("a_const_ready")
    dve_chain = sem("a_dve_chain")
    stats_done, var_ready, sd_ready = sem("a_stats_done"), sem("a_var_ready"), sem("a_sd_ready")
    mask_ready, turned, maskT_ready = sem("a_mask_ready"), sem("a_turned"), sem("a_maskT_ready")
    agg_summed, agg_ready = sem("a_agg_summed"), sem("a_agg_ready")
    xn_ready, low_ready = sem("a_xn_ready"), sem("a_low_ready")
    both_turned, both_ready = sem("a_both_turned"), sem("a_both_ready")
    out_summed, out_read, x_added = sem("a_out_summed"), sem("a_out_read"), sem("a_x_added")
    wT_turned, wT_ready, w_summed, w_ready = (sem("a_" + n) for n in ("wT_turned", "wT_ready", "w_summed", "w_ready"))
    bias_summed, bias_ready, b_ready = sem("a_bias_summed"), sem("a_bias_ready"), sem("a_b_ready")
    b_widened, slope_ready, scaled_ready, high_ready = (sem("a_" + n) for n in (
        "b_widened", "slope_ready", "scaled_ready", "high_ready"))
    split_done, edges_ready, rdeg_steps = sem("a_split_done"), sem("a_edges_ready"), sem("a_rdeg_steps")

    with nc.Block() as block:

        @block.sync
        def _(sp):
            x_rows = dram["x"].rearrange("(t p) d -> p t d", p=P)
            for c in range(NT // XCHUNK):
                here = slice(c * XCHUNK, (c + 1) * XCHUNK)
                sp.dma_start(x[:, here], x_rows[:, here]).then_inc(x_in[c], 16)
            adj = dram["adj"].rearrange("(t p) n -> t p n", p=P)
            sp.wait_ge(w_in, 6 * 16)
            for s in range(STAGES):
                sp.dma_start(adj_in[:, s], adj[s]).then_inc(adj_landed[s], 16)
            with sp.Fori(1, NT // STAGES) as g:
                i0 = g * STAGES
                for s in range(STAGES):
                    sp.wait_ge(mask_ready, i0 + (s - STAGES + 1))
                    sp.dma_start(adj_in[:, s], at2(adj, i0 + s)).then_inc(adj_landed[s], 16)
            sp.wait_ge(zeros_ready, 2)
            zero_rows = mem["slot_x"].rearrange("(c p r) d -> c p (r d)", p=P, r=ZERO_ROWS)
            for c in range(ZERO_DMAS):
                sp.dma_start(zero_rows[c], zeros).then_inc(slots_zeroed, 16)
            sp.wait_ge(slots_zeroed, 16 * ZERO_DMAS)

        @block.gpsimd
        def _(pool):
            nc.gpsimd.memset(identity, 0.0).then_inc(const_ready, 1)
            nc.gpsimd.memset(ones, 1.0).then_inc(const_ready, 1)
            nc.gpsimd.memset(zeros, 0.0).then_inc(zeros_ready, 1)
            pool.wait_ge(zeros_ready, 1)
            nc.gpsimd.iota(zeros.rearrange("p (r d) -> p r d", d=D + 2)[:, :, D:D + 1], pattern=[[1, ZERO_ROWS], [1, 1]],
                           base=0, channel_multiplier=ZERO_ROWS, allow_small_or_imprecise_dtypes=True).then_inc(zeros_ready, 1)
            pool.wait_ge(const_ready, 2)
            nc.gpsimd.affine_select(out=identity, in_=identity, compare_op=ALU.not_equal, fill=1.0, base=0,
                                    pattern=[[-1, P]], channel_multiplier=1).then_inc(const_ready, 1)
            pool.wait_ge(const_ready, 3)
            nc.gpsimd.tensor_copy(identity16, identity).then_inc(const_ready, 1)
            pool.wait_ge(slope_ready, 1)
            for t in range(NT // 2):
                nc.gpsimd.tensor_scalar(scaled[:, t], x[:, t], col(slope, t), col(offset, t), ALU.mult, ALU.add
                                        ).then_inc(scaled_ready, 1)

        @block.scalar
        def _(act):
            for view, name in ((w_self, "L0_gnn_W_self"), (w_nb, "L0_gnn_W_nb"), (w_comb, "L0_gnn_W_comb")):
                act.dma_start(view, dram[name].rearrange("(k p) d -> p k d", p=P)).then_inc(w_in, 16)
            for n, name in enumerate(("L0_gnn_b_self", "L0_gnn_b_nb")):
                act.dma_start(b_row[:, n * D:(n + 1) * D], dram[name].rearrange("(o d) -> o d", o=1)).then_inc(w_in, 16)
            act.dma_start(b_comb, dram["L0_gnn_b_comb"].rearrange("(o d) -> o d", o=1)).then_inc(w_in, 16)
            act.dma_start(mem["gate_w"], dram["L0_ffn_gate_w"].rearrange("(k p) e -> p k e", p=P)).then_inc(mem["gate_in"], 16)
            act.dma_start(mem["gate_b"], dram["L0_ffn_gate_b"].rearrange("(o e) -> o e", o=1)).then_inc(mem["gate_in"], 16)
            act.wait_ge(b_widened, 1)
            nc.scalar.activation(b_wide, psum[:, 3072:3584], ACT.Copy).then_inc(b_ready, 1)
            for n, view in enumerate((w_selfT, w_nbT)):
                act.wait_ge(wT_turned, n + 1)
                nc.scalar.activation(view.rearrange("p k d -> p (k d)"), ps_agg[n], ACT.Copy).then_inc(wT_ready, 1)
            act.wait_ge(var_ready, 1)
            nc.scalar.activation(var, var, ACT.Sqrt).then_inc(sd_ready, 1)
            for n, view in enumerate((wx, wa)):
                act.wait_ge(w_summed, n + 1)
                nc.scalar.activation(view.rearrange("p k d -> p (k d)"), ps_agg[n], ACT.Copy).then_inc(w_ready, 1)
            act.wait_ge(slope_ready, 1)
            with act.Fori(0, NT // 4) as g:
                for u in range(4):
                    t = g * 4 + u
                    nc.scalar.activation(at(ln16, t)[:, 0:D], at(x, t), ACT.Identity, bias=col(offset, t), scale=col(slope, t)
                                         ).then_inc(high_ready, 1)

            def mask_out(i, s):
                act.wait_ge(turned, i + 1)
                nc.scalar.activation(maskT[:, s], ps_mask[s], ACT.Copy).then_inc(maskT_ready, 1)

            def both_out(i, s):
                act.wait_ge(both_turned, i + 1)
                nc.scalar.activation(xnT[:, s], ps_turn[:, 0:KD], ACT.Copy)
                nc.scalar.activation(aggT[:, s], ps_turn[:, KD:2 * KD], ACT.Copy).then_inc(both_ready, 1)

            mask_out(0, 0)
            mask_out(1, 1)
            with act.Fori(1, NT // 2) as g:
                i0 = g * 2
                for u in range(2):
                    both_out(i0 + (u - 2), u)
                    mask_out(i0 + u, u)
            both_out(NT - 2, 0)
            both_out(NT - 1, 1)

        @block.tensor
        def _(pe):
            pe.wait_ge(const_ready, 4)
            pe.wait_ge(w_in, 6 * 16)
            for m in range(2 * KD):
                last = nc.tensor.matmul(ps_turn[:, m, :], b_row[0:1, m * P:(m + 1) * P], ones[0:1, :], start=True, stop=True)
            last.then_inc(b_widened, 1)
            for n, w in enumerate((w_self, w_nb)):
                for k in range(KD):
                    for m in range(KD):
                        last = nc.tensor.transpose(ps_agg[n][:, m * D + k * P:m * D + (k + 1) * P],
                                                   w[:, k, m * P:(m + 1) * P], identity)
                last.then_inc(wT_turned, 1)
            for n, wT in enumerate((w_selfT, w_nbT)):
                pe.wait_ge(wT_ready, n + 1)
                for rows in range(KD):
                    for m in range(KD):
                        last = nc.tensor.matmul(ps_agg[n][:, rows * D:(rows + 1) * D], wT[:, m, rows * P:(rows + 1) * P],
                                                w_comb[:, n * KD + m, :], start=(m == 0), stop=(m == KD - 1))
                last.then_inc(w_summed, 1)
            pe.wait_ge(b_ready, 1)
            for m in range(2 * KD):
                nc.tensor.matmul(ps_out, b_wide[:, m * P:(m + 1) * P], w_comb[:, m, :], start=(m == 0), stop=False)
            nc.tensor.matmul(ps_out, ones[0:1, :], b_comb, start=False, stop=True).then_inc(bias_summed, 1)

            def turn_mask(i, s):
                pe.wait_ge(mask_ready, i + 1)
                for j in range(NJ):
                    last = nc.tensor.transpose(ps_mask[s][:, j, :], mask[:, s, j * P:(j + 1) * P], identity16)
                last.then_inc(turned, 1)

            def sum_neighbours(i, s):
                pe.wait_ge(maskT_ready, i + 1)
                for j in range(NJ):
                    if isinstance(i, int) and i == 0:
                        pe.wait_ge(split_done, j + 1)
                    last = nc.tensor.matmul(ps_agg[s], maskT[:, s, j, :], ln16[:, j, :], start=(j == 0), stop=(j == NJ - 1))
                last.then_inc(agg_summed, 1)

            def turn_both(i, s):
                pe.wait_ge(agg_ready, i + 1)
                pe.wait_ge(xn_ready, i + 1)
                for n, rows in enumerate((xn, agg)):
                    for k in range(KD):
                        last = nc.tensor.transpose(ps_turn[:, n * KD + k, :], rows[:, s, k * P:(k + 1) * P], identity)
                last.then_inc(both_turned, 1)

            def combine(i, s):
                pe.wait_ge(both_ready, i + 1)
                pe.wait_ge(out_read, i + 1)
                for n, (lhs, w) in enumerate(((xnT, wx), (aggT, wa))):
                    for k in range(KD):
                        last = nc.tensor.matmul(ps_out, lhs[:, s, k, :], w[:, k, :], start=(n == 0 and k == 0),
                                                stop=(n == 1 and k == KD - 1))
                last.then_inc(out_summed, 1)

            turn_mask(0, 0)
            turn_mask(1, 1)

            pe.wait_ge(w_ready, 2)
            sum_neighbours(0, 0)
            pe.wait_ge(bias_ready, 1)
            with pe.Fori(0, NT // 2 - 1) as g:
                i0 = g * 2 + 1
                for u in range(2):
                    s = (1 + u) % 2
                    turn_mask(i0 + (u + 1), 1 - s)
                    turn_both(i0 + (u - 1), 1 - s)
                    sum_neighbours(i0 + u, s)
                    combine(i0 + (u - 1), 1 - s)
            turn_both(NT - 2, 0)
            sum_neighbours(NT - 1, 1)
            combine(NT - 2, 0)
            turn_both(NT - 1, 1)
            combine(NT - 1, 1)

        @block.vector
        def _(dve):
            chain = Chain(dve, dve_chain)
            dve.sem_inc(x_added, 1)
            dve.sem_inc(out_read, 1)
            for c in range(NT // XCHUNK):
                dve.wait_ge(x_in[c], 16)
                for t in range(c * XCHUNK, (c + 1) * XCHUNK):
                    nc.vector.bn_stats(stats[:, t], x[:, t]).then_inc(stats_done, 1)
            dve.wait_ge(stats_done, NT)
            layernorm_spread(nc, chain, stats, mean, var, tmp).then_inc(var_ready, 1)
            def normalise(i, s):
                nc.vector.tensor_scalar(xn[:, s], at(x, i), col(mean, i), col(rstd, i), ALU.subtract, ALU.mult
                                        ).then_inc(xn_ready, 1)

            def make_mask(i, s, stage, landed):
                dve.wait_ge(adj_landed[stage], landed)
                dve.wait_ge(edges_ready, i)
                nc.vector.tensor_scalar(mask[:, s], adj_in[:, stage], 0.0, 0.0, ALU.is_gt, ALU.add,
                                        accum_out=col(deg, stage)).then_inc(mask_ready, 1)
                dve.wait_ge(mask_ready, i + 1)
                nc.vector.tensor_scalar(at(edges, i), mask[:, s], 1.0, -NO_EDGE, ALU.subtract, ALU.mult
                                        ).then_inc(edges_ready, 1)

            def mean_of_neighbours(i, s, stage):
                rdeg_i = col(rdeg, stage)
                nc.vector.tensor_scalar(rdeg_i, col(deg, stage), 1.0, SCALE16, ALU.max, ALU.mult).then_inc(rdeg_steps, 1)
                dve.wait_ge(rdeg_steps, i * 2 + 1)
                nc.vector.reciprocal(rdeg_i, rdeg_i).then_inc(rdeg_steps, 1)
                dve.wait_ge(rdeg_steps, i * 2 + 2)
                dve.wait_ge(agg_summed, i + 1)
                nc.vector.tensor_scalar(agg_low[:, s], ps_agg[s][:, D:2 * D], rdeg_i, None, ALU.mult
                                        ).then_inc(low_ready, 1)
                dve.wait_ge(low_ready, i + 1)
                nc.vector.scalar_tensor_tensor(out=agg[:, s], in0=ps_agg[s][:, 0:D], scalar=rdeg_i,
                                               in1=agg_low[:, s], op0=ALU.mult, op1=ALU.add).then_inc(agg_ready, 1)

            def add_result(i, s):
                dve.wait_ge(out_summed, i + 1)
                nc.vector.tensor_tensor(out_b[:, s], ps_out, bias, ALU.add).then_inc(out_read, 1)
                dve.wait_ge(x_added, i + 1)
                dve.wait_ge(out_read, i + 2)
                nc.vector.scalar_tensor_tensor(out=at(x, i), in0=out_b[:, s], scalar=0.0, in1=at(x, i),
                                               op0=ALU.max, op1=ALU.add).then_inc(x_added, 1)

            def new_stats(i):
                dve.wait_ge(x_added, i + 2)
                nc.vector.bn_stats(at(stats, i), at(x, i)).then_inc(stats_done, 1)

            def step(i, stage, first=False, more=True, landed=None):
                s = stage % 2
                mean_of_neighbours(i - 1, 1 - s, (stage - 1) % STAGES)
                if not first:
                    dve.wait_ge(both_turned, i - 1)
                normalise(i, s)
                if not first:
                    add_result(i - 2, s)
                if more:
                    dve.wait_ge(turned, i + 1)
                    make_mask(i + 2, s, (stage + 2) % STAGES, landed)
                if not first:
                    new_stats(i - 2)

            make_mask(0, 0, 0, 16)
            dve.wait_ge(sd_ready, 1)
            chain.link(nc.vector.reciprocal(rstd, var))
            chain.link(nc.vector.tensor_scalar(slope, rstd, SCALE16, None, ALU.mult))
            nc.vector.scalar_tensor_tensor(out=offset, in0=mean, scalar=-1.0, in1=slope, op0=ALU.mult, op1=ALU.mult
                                           ).then_inc(slope_ready, 1)
            make_mask(1, 1, 1, 16)
            for t in range(NT // 2, NT):
                nc.vector.tensor_scalar(scaled[:, t], x[:, t], col(slope, t), col(offset, t), ALU.mult, ALU.add
                                        ).then_inc(scaled_ready, 1)
            dve.wait_ge(scaled_ready, NT)
            for t in range(NT):
                dve.wait_ge(high_ready, t + 1)
                nc.vector.tensor_tensor(ln16[:, t, D:2 * D], scaled[:, t], ln16[:, t, 0:D], ALU.subtract
                                        ).then_inc(split_done, 1)
            dve.wait_ge(bias_summed, 1)
            nc.vector.tensor_copy(bias, ps_out).then_inc(bias_ready, 1)
            dve.wait_ge(turned, 1)
            make_mask(2, 0, 2, 16)
            normalise(0, 0)
            step(1, 1, first=True, landed=16)
            with dve.Fori(0, (NT - 4) // STAGES) as g:
                i0 = g * STAGES + 2
                for u in range(STAGES):
                    step(i0 + u, (2 + u) % STAGES, landed=i0 * 4 + 24)
            step(NT - 2, 2, more=False)
            step(NT - 1, 3, more=False)
            mean_of_neighbours(NT - 1, 1, 3)
            add_result(NT - 2, 0)
            add_result(NT - 1, 1)
            dve.wait_ge(edges_ready, NT)
            new_stats(NT - 2)
            new_stats(NT - 1)
            dve.wait_ge(stats_done, 2 * NT)


def at2(view, i):
    return view[bass.ds(i, 1)].rearrange("o p n -> (o p) n")


def col(view, i):
    return view[:, i:i + 1] if isinstance(i, int) else view[:, bass.ds(i, 1)]


def mixture(nc, dram, mem, sem):
    x, xln = mem["x"], mem["xln"]
    identity, ones = mem["identity"], mem["ones"]
    mean, rstd = mem["mean"], mem["rstd"]
    psum = mem["PSUM"]
    slot_x, token_y = mem["slot_x"], mem["token_y"]
    row_no = mem["xln_row"][:, :, D:D + 1]
    row_weight = mem["xln_row"][:, :, D + 1:D + 2]
    arena = Region(mem["ARENA"], mem["ARENA"].shape[1])
    w1 = arena.take(F32, NE, KD, I2)
    w2 = arena.take(F32, NE, KI, D)
    small = Region(mem["SMALL"], SMALL_WORDS)
    xT = small.take(F32, 2, KD, P)
    setup_words = small.at
    gate, up, sig = (small.take(F32, 2, I) for _ in range(3))
    tT = small.take(F32, 2, KI, P)
    tiles_words, small.at = small.at, setup_words
    bias_in = small.take(F32, I2)
    act_wide = small.take(F32, 7, P)
    small.at = tiles_words
    pick = small.take(BF16, 4, P)
    pick_shared = small.take(BF16, P)
    biases = small.take(BF16, I2)
    onehot = small.take(F32, NS + 1)
    onehot16 = small.take(BF16, NS + 2)
    params = small.take(F32, 7, NS + 1)
    tile_expert = small.take(I32, NS)
    slots = small.take(U32, TOPK, NT)
    weight = small.take(F32, TOPK, NT)
    stats, var, tmp = mem["stats"], small.take(F32, NT), small.take(F32, NT)
    offset = tmp
    act_table = small.take(F32, 8)
    soft = small.take(F32, 3, 2)
    shared_words = small.at
    xn = small.take(F32, 2, D)
    bias_room = Region(mem["ARENA"][:, (E - 2) * KD * I2:E * KD * I2], 2 * KD * I2)
    part16, *picked16 = (bias_room.take(BF16, I2) for _ in range(PARTS))
    from_last = small.take(F32, E)
    prob, equal, first = (small.take(F32, NT, E) for _ in range(3))
    best = [small.take(F32, NT, E) for _ in range(TOPK)]
    chosen = small.take(BF16, NT, NE + 1)
    top = small.take(F32, 4, NT)
    small.at = shared_words
    x_in = small.take(F32, 4, D + 2)
    y_row = small.take(U32, 4, 1)
    y_weight = small.take(F32, 4, 1)
    y_out = small.take(F32, 4, D)
    after = Region(mem["ARENA"], mem["ARENA"].shape[1])
    SOME = 4
    y_in = [after.take(F32, TOPK, SOME, D) for _ in range(NT // SOME)]
    product = [after.take(F32, NT, D) for _ in range(2)]
    att_w1, att_w23 = after.take(F32, D), after.take(F32, 2)
    u_wide = after.take(F32, 2, D)
    f_raw, u_sum, f_bias = mem["f_raw"], mem["u_sum"], mem["f_bias"]
    const = mem["const"]
    before = const.take(BF16, P)
    ones16 = const.take(BF16, P)
    before_e, same_e = const.take(BF16, NB), const.take(BF16, NB)
    gate_w, gate_b, gate_in = mem["gate_w"], mem["gate_b"], mem["gate_in"]
    steps128, tile_no = const.take(F32, E), const.take(F32, NS)
    expert_no = const.take(BF16, 2)
    part_is = const.take(F32, 4)
    count, count16, start, stop = const.take(F32, 2), const.take(BF16, 4), const.take(F32, 2), const.take(F32, 2)
    count_wide = const.take(BF16, P)
    base = const.take(F32, E)

    bank = [psum[:, 512 * b:512 * (b + 1)] for b in range(8)]
    ps_x = [bank[s][:, 0:KD * P].rearrange("p (k q) -> p k q", q=P) for s in range(2)]
    ps_h = [bank[2 + s][:, 0:I2] for s in range(2)]
    ps_t = [bank[4 + s][:, 0:KI * P].rearrange("p (k q) -> p k q", q=P) for s in range(2)]
    ps_y = [bank[6 + s][:, 0:D] for s in range(2)]
    ps_logits = bank[4][:, 0:NT * E].rearrange("p (t e) -> p t e", e=E)
    ps_rank = bank[5][:, 0:NT * E].rearrange("p (t e) -> p t e", e=E)
    ps_count = bank[6][0:NE, 0:1]
    ps_base, ps_start = bank[7][:, 0:E], bank[7][0:NB, 32:34]
    ps_tile = bank[6][0:1, 64:64 + NS]
    ps_params = bank[4][:, 0:7 * (NS + 1)].rearrange("p (c s) -> p c s", s=NS + 1)

    names = ("consts", "small_in", "w_shared_in", "w_experts_in", "dve_chain", "stats_done", "var_ready", "sd_ready",
             "xn_ready", "xln_ready", "x_turned", "xT_ready", "logits_done", "soft_in", "soft_out", "wide_ready",
             "shifted", "exped", "chosen_ready", "ranked", "counted", "wide_count", "started", "onehot_ready",
             "tables_done", "tables_out", "slots_ready", "sent", "ex_turned", "exT_ready", "h_summed", "swi",
             "sig_ready", "t_turned", "tT_ready", "y_summed", "z_added", "y_copied", "pick_ready", "combined",
             "combined_half", "row_kept", "biases_ready", "bias_rounded",
             "bias_left", "bias_picked", "att_w_in", "u_summed",
             "u_ready", "product_ready", "product2_ready", "f_raw_ready")
    S = {name: sem("b_" + name) for name in names}
    x_landed = [sem(f"b_x_landed{q}") for q in range(4)]
    y_stored = [sem(f"b_y_stored{q}") for q in range(4)]
    y_landed = [sem(f"b_y_landed{c}") for c in range(NT // 4)]
    SMALL_DMAS = 2 * PARTS + 4

    with nc.Block() as block:

        @block.sync
        def _(sp):
            def small_load(view, ap):
                sp.dma_start(view, ap).then_inc(S["small_in"], 16)

            for part in range(PARTS):
                p0 = part * NE
                small_load(bias_in[p0:p0 + E], dram["L0_ffn_expert_b1"])
                small_load(bias_in[p0 + E:p0 + NE], dram["L0_ffn_shared_b1"].rearrange("(o h) -> o h", o=1))
            small_load(act_table[0:E, 0:5], dram["L0_ffn_expert_act"])
            small_load(act_table[E:NE, 0:5], dram["L0_ffn_shared_act"].rearrange("(o h) -> o h", o=1))
            sp.dma_start(w1[:, E], dram["L0_ffn_shared_w1"].rearrange("(k p) h -> p k h", p=P)).then_inc(S["w_shared_in"], 16)
            small_load(w2[IH:IH + 1, 0:E, 0, :], dram["L0_ffn_expert_b2"].rearrange("(o e) d -> o e d", o=1))
            small_load(w2[IH:IH + 1, E, 0, :], dram["L0_ffn_shared_b2"].rearrange("(o d) -> o d", o=1))
            sp.dma_start(w2[0:IH, E], dram["L0_ffn_shared_w2"].rearrange("(k p) d -> p k d", p=IH)).then_inc(S["w_shared_in"], 16)
            def load_experts(part):
                some = slice(part * E // 4, (part + 1) * E // 4)
                sp.dma_start(w1[:, some].rearrange("p e k h -> p (e k) h"),
                             dram["L0_ffn_expert_w1"][some].rearrange("e (k p) h -> p (e k) h", p=P)).then_inc(S["w_experts_in"], 16)
                sp.dma_start(w2[0:IH, some].rearrange("p e k d -> p (e k) d"),
                             dram["L0_ffn_expert_w2"][some].rearrange("e (k p) d -> p (e k) d", p=IH)).then_inc(S["w_experts_in"], 16)
            load_experts(0)
            load_experts(1)
            sp.wait_ge(S["xln_ready"], NT)

            def load(n, q, shared):
                if shared:
                    sp.dma_start(x_in[:, q, 0:D], at(xln, n)).then_inc(x_landed[q], 16)
                else:
                    sp.dma_start(x_in[:, q], rows(slot_x, n - NT)).then_inc(x_landed[q], 16)

            sp.wait_ge(S["slots_ready"], 1)
            sp.wait_ge(S["biases_ready"], 1)
            for n in range(4):
                load(n, n, True)
            load_experts(2)
            for n in range(4, 8):
                sp.wait_ge(S["ex_turned"], n - 3)
                load(n, n % 4, True)
            load_experts(3)
            with sp.Fori(2, NT // 4) as g:
                for q in range(4):
                    sp.wait_ge(S["ex_turned"], g * 4 + (q - 3))
                    load(g * 4 + q, q, True)
            sp.wait_ge(S["sent"], 16 * NT * TOPK)
            for n in range(NT, NT + 4):
                sp.wait_ge(S["ex_turned"], n - 3)
                load(n, n % 4, False)
            with sp.Fori(NT // 4 + 1, (NT + NS) // 4) as g:
                for q in range(4):
                    sp.wait_ge(S["ex_turned"], g * 4 + (q - 3))
                    sp.wait_ge(S["row_kept"], g * 4 + (q - 3))
                    load(g * 4 + q, q, False)
            for n in range((NT + NS) // 4 * 4, NT + NS):
                sp.wait_ge(S["ex_turned"], n - 3)
                sp.wait_ge(S["row_kept"], n - 3)
                load(n, n % 4, False)
            for q in range(4):
                sp.wait_ge(y_stored[q], 16 * len(range(q, NS, 4)))
            results = token_y[SPARE:, :].rearrange("(k c t p) d -> k c p t d", k=TOPK, t=SOME, p=P)
            for c in range(NT // SOME):
                for k in range(TOPK):
                    sp.dma_start(y_in[c][:, k], results[k, c]).then_inc(y_landed[c], 16)

        @block.gpsimd
        def _(pool):
            chain = Chain(pool, S["consts"])
            link = chain.link
            for view, value in ((before, 1.0), (ones16, 1.0), (before_e, 1.0), (same_e, 0.0), (chosen, 0.0), (onehot, 0.0),
                                (part_is, 0.0), (pick_shared, 1.0), (tT[IH:IH + 1, :, 0, :], 1.0)):
                link(nc.gpsimd.memset(view, value))
            link(nc.gpsimd.affine_select(out=before, in_=before, compare_op=ALU.is_gt, fill=0.0, base=0,
                                         pattern=[[1, P]], channel_multiplier=-1))
            link(nc.gpsimd.affine_select(out=before_e, in_=before_e, compare_op=ALU.is_gt, fill=0.0, base=0,
                                         pattern=[[0, PARTS], [1, NE]], channel_multiplier=-1))
            link(nc.gpsimd.affine_select(out=same_e, in_=same_e, compare_op=ALU.not_equal, fill=1.0, base=0,
                                         pattern=[[0, PARTS], [1, NE]], channel_multiplier=-1))
            for part in range(PARTS):
                link(nc.gpsimd.affine_select(out=onehot[:, NS:NS + 1], in_=onehot[:, NS:NS + 1], compare_op=ALU.not_equal,
                                             fill=1.0, base=-(part * NE + E), pattern=[[0, 1]], channel_multiplier=1))
                view = part_is[:, part:part + 1]
                link(nc.gpsimd.memset(view, 1.0))
                link(nc.gpsimd.affine_select(out=view, in_=view, compare_op=ALU.is_ge, fill=0.0, base=-part * NE,
                                             pattern=[[0, 1]], channel_multiplier=1))
                link(nc.gpsimd.affine_select(out=view, in_=view, compare_op=ALU.is_ge, fill=0.0, base=(part + 1) * NE - 1,
                                             pattern=[[0, 1]], channel_multiplier=-1))
            link(nc.gpsimd.iota(from_last, pattern=[[1, E]], base=-E, channel_multiplier=0, allow_small_or_imprecise_dtypes=True))
            link(nc.gpsimd.iota(steps128, pattern=[[P, E]], base=0, channel_multiplier=0, allow_small_or_imprecise_dtypes=True))
            link(nc.gpsimd.iota(tile_no, pattern=[[1, NS]], base=0, channel_multiplier=0, allow_small_or_imprecise_dtypes=True))
            link(nc.gpsimd.iota(expert_no[:, 0:1], pattern=[[0, 1]], base=0, channel_multiplier=1, allow_small_or_imprecise_dtypes=True))
            mem["b_consts"] = chain.count
            for part in range(PARTS - 1):
                pool.wait_ge(S["bias_rounded"], part + 1)
                nc.gpsimd.tensor_tensor(bias_in[0:NB], bias_in[0:NB], part16[0:NB], ALU.subtract).then_inc(S["bias_left"], 1)
            for part in range(1, PARTS):
                pool.wait_ge(S["bias_picked"], part + 1)
                link(nc.gpsimd.tensor_tensor(biases[0:NB], biases[0:NB], picked16[part - 1][0:NB], ALU.add))
            link(nc.gpsimd.tensor_scalar(pick_shared[0:NB], ones16[0:NB], onehot[0:NB, NS:NS + 1], None, ALU.mult))
            pool.sem_inc(S["biases_ready"], 1)
            for k in range(TOPK):
                if k:
                    pool.wait_ge(S["sent"], 16 * NT)
                link(nc.gpsimd.iota(row_no, pattern=[[P, NT], [1, 1]], base=SPARE + k * N, channel_multiplier=1,
                                    allow_small_or_imprecise_dtypes=True))
                if k == 0:
                    pool.wait_ge(S["slots_ready"], 1)
                    pool.wait_ge(S["xln_ready"], NT)
                link(nc.gpsimd.tensor_copy(row_weight, weight[:, k].unsqueeze(2)))
                for t in range(NT):
                    nc.gpsimd.indirect_dma_start(
                        out=slot_x, out_offset=bass.IndirectOffsetOnAxis(ap=slots[:, k, t:t + 1], axis=0),
                        in_=mem["xln_row"][:, t], in_offset=None).then_inc(S["sent"], 16)

            pool.sem_inc(S["row_kept"], NT)

            def keep_rows(m):
                pool.wait_ge(x_landed[m % 4], 16 * (NT // 4 + m // 4 + 1))
                if m >= 4:
                    pool.wait_ge(y_stored[m % 4], 16 * (m // 4))
                nc.gpsimd.tensor_copy(y_weight[:, m % 4], x_in[:, m % 4, D + 1:D + 2])
                nc.gpsimd.tensor_copy(y_row[:, m % 4], x_in[:, m % 4, D:D + 1]).then_inc(S["row_kept"], 1)

            keep_rows(0)
            for m in range(NS):
                if m < NS - 1:
                    keep_rows(m + 1)
                pool.wait_ge(S["row_kept"], NT + m + 1)
                pool.wait_ge(S["y_copied"], m + 3)
                nc.gpsimd.indirect_dma_start(
                    out=token_y, out_offset=bass.IndirectOffsetOnAxis(ap=y_row[:, m % 4], axis=0),
                    in_=y_out[:, m % 4], in_offset=None).then_inc(y_stored[m % 4], 16)

            def both_results(c):
                pool.wait_ge(y_landed[c], 16 * TOPK)
                nc.gpsimd.tensor_tensor(y_in[c][:, 0], y_in[c][:, 0], y_in[c][:, 1], ALU.add).then_inc(S["combined_half"], 1)

            pool.wait_ge(S["u_ready"], 1)
            both_results(0)
            for c in range(NT // SOME):
                if c + 1 < NT // SOME:
                    both_results(c + 1)
                pool.wait_ge(S["combined"], c + 1)
                some = slice(c * SOME, (c + 1) * SOME)
                nc.gpsimd.tensor_tensor(product[0][:, some], x[:, some], u_wide[:, 0].unsqueeze(1).to_broadcast([P, SOME, D]),
                                        ALU.mult).then_inc(S["product_ready"], 1)

        consts = mem["b_consts"]

        @block.scalar
        def _(act):
            act.wait_ge(S["var_ready"], 1)
            nc.scalar.activation(var, var, ACT.Sqrt).then_inc(S["sd_ready"], 1)
            def xT_out(s, wait, ready):
                act.wait_ge(*wait)
                nc.scalar.activation(xT[:, s], ps_x[s], ACT.Copy).then_inc(ready, 1)

            act.wait_ge(S["var_ready"], 3)
            with act.Fori(0, NT // 2) as g:
                for u in range(2):
                    t = g * 2 + u
                    nc.scalar.activation(at(xln, t), at(x, t), ACT.Identity, bias=col(offset, t), scale=col(rstd, t)
                                         ).then_inc(S["xln_ready"], 1)
                    xT_out(u, (S["x_turned"], t + 1), S["xT_ready"])

            def bias_part(part):
                if part:
                    act.wait_ge(S["bias_left"], part)
                    act.wait_ge(S["bias_picked"], part)
                nc.scalar.activation(part16[0:NB], bias_in[0:NB], ACT.Copy).then_inc(S["bias_rounded"], 1)
                act.wait_ge(S["bias_rounded"], part + 1)
                nc.scalar.activation(picked16[part - 1][0:NB] if part else biases[0:NB], part16[0:NB], ACT.Copy,
                                     scale=part_is[0:NB, part:part + 1]).then_inc(S["bias_picked"], 1)

            act.wait_ge(S["consts"], consts)
            act.wait_ge(S["small_in"], 16 * SMALL_DMAS)
            bias_part(0)
            act.wait_ge(S["soft_in"], 1)
            nc.scalar.activation(soft[0:NE, 0], soft[0:NE, 0], ACT.Exp, scale=-1.0).then_inc(S["soft_out"], 1)
            act.wait_ge(S["shifted"], 1)
            nc.scalar.activation(prob, prob, ACT.Exp).then_inc(S["exped"], 1)
            act.wait_ge(S["soft_in"], 2)
            nc.scalar.activation(soft[0:NE, 0], soft[0:NE, 0], ACT.Ln).then_inc(S["soft_out"], 1)
            bias_part(1)
            bias_part(2)

            def tT_out(n, s):
                act.wait_ge(S["t_turned"], n + 1)
                nc.scalar.activation(tT[0:IH, s], ps_t[s][0:IH], ACT.Copy).then_inc(S["tT_ready"], 1)

            def y_out_copy(n, s, q, stored):
                act.wait_ge(S["y_summed"], n + 1)
                if stored is not None:
                    act.wait_ge(y_stored[q], stored)
                act.wait_ge(S["row_kept"], n + 1)
                nc.scalar.activation(y_out[:, q], ps_y[s], ACT.Copy, scale=y_weight[:, q]).then_inc(S["y_copied"], 1)

            def step(n, q, g, tail=True, more=True, shared=False, shared_tail=False):
                s = q % 2
                if tail:
                    tT_out(n - 2, s)
                if more:
                    xT_out(1 - s, (S["ex_turned"], n + 2), S["exT_ready"])
                act.wait_ge(S["swi"], n * 4 + 1)
                alpha = params[:, 0, NS:NS + 1] if shared else params_at(params, 0, n - NT)
                nc.scalar.activation(sig[:, s], gate[:, s], ACT.Sigmoid, scale=alpha).then_inc(S["sig_ready"], 1)
                if tail and not shared_tail:
                    y_out_copy(n - 2, s, (q - 2) % 4, None if isinstance(n, int) and n < NT + 6 else (g - NT // 4) * 16)

            act.wait_ge(S["tables_out"], 2)
            xT_out(0, (S["ex_turned"], 1), S["exT_ready"])
            run_tiles(act, step)
            for n in (NT + NS - 2, NT + NS - 1):
                tT_out(n, n % 2)
                y_out_copy(n, n % 2, n % 4, (n // 4 - NT // 4) * 16)
            act.dma_start(att_w1, dram["L1_gnn_W1"]).then_inc(S["att_w_in"], 16)
            for c, name in enumerate(("L1_gnn_w2", "L1_gnn_w3")):
                act.dma_start(att_w23[:, c:c + 1], dram[name].rearrange("(p o) -> p o", o=1),
                              allow_slow_non_contiguous=True).then_inc(S["att_w_in"], 16)
            for c, name in enumerate(("L1_gnn_b2", "L1_gnn_b3")):
                act.dma_start(f_bias[:, c:c + 1], dram[name].rearrange("(p o) -> p o", o=1).to_broadcast([P, 1]),
                              allow_slow_non_contiguous=True).then_inc(S["att_w_in"], 16)
            act.wait_ge(S["u_summed"], 1)
            nc.scalar.activation(u_wide.rearrange("p c d -> p (c d)"), bank[0], ACT.Copy).then_inc(S["u_ready"], 1)
            for c in range(NT // SOME):
                for which, made in ((1, "product2_ready"), (0, "product_ready")):
                    if which and c == NT // SOME - 1:
                        continue
                    act.wait_ge(S[made], c + 1)
                    for t in range(c * SOME, (c + 1) * SOME):
                        nc.scalar.activation(product[which][:, t], product[which][:, t], ACT.Identity,
                                             accum_out=f_raw[:, which, t:t + 1]).then_inc(S["f_raw_ready"], 1)

        @block.tensor
        def _(pe):
            def turn(s, rows_, ready):
                for k in range(KD):
                    last = nc.tensor.transpose(ps_x[s][:, k, :], rows_[:, k * P:(k + 1) * P], identity)
                last.then_inc(ready, 1)

            def turn_xn(t, s):
                pe.wait_ge(S["xn_ready"], t + 1)
                turn(s, xn[:, s], S["x_turned"])

            def logits(t, s):
                pe.wait_ge(S["xT_ready"], t + 1)
                for k in range(KD):
                    last = nc.tensor.matmul(at(ps_logits, t), xT[:, s, k, :], gate_w[:, k, :], start=False,
                                            stop=(isinstance(t, int) and t == NT - 1 and k == KD - 1))
                last.then_inc(S["logits_done"], 1)

            pe.wait_ge(gate_in, 32)
            nc.tensor.matmul(ps_logits, ones[0:1, :], gate_b.unsqueeze(1).to_broadcast([1, NT, E]), start=True, stop=False)
            turn_xn(0, 0)
            with pe.Fori(0, NT // 2 - 1) as g:
                turn_xn(g * 2 + 1, 1)
                logits(g * 2, 0)
                turn_xn(g * 2 + 2, 0)
                logits(g * 2 + 1, 1)
            turn_xn(NT - 1, 1)
            logits(NT - 2, 0)
            logits(NT - 1, 1)
            pe.wait_ge(S["consts"], consts)
            pe.wait_ge(S["chosen_ready"], 1)
            nc.tensor.matmul(ps_rank, before, chosen[:, :, 0:E], start=True, stop=False)
            for back in range(1, NT):
                last = nc.tensor.matmul(ps_rank[:, back:NT, :], ones16, chosen[:, 0:NT - back, 0:E], start=False,
                                        stop=(back == NT - 1))
            last.then_inc(S["ranked"], 1)
            for t in range(NT):
                last = nc.tensor.matmul(ps_count, chosen[:, t, 0:NE], ones16[:, 0:1],
                                        start=(t == 0), stop=(t == NT - 1))
            last.then_inc(S["counted"], 1)
            pe.wait_ge(S["wide_count"], 1)
            nc.tensor.matmul(ps_base, count_wide[0:NE], before_e[0:NE, 0:E], start=True, stop=True)
            nc.tensor.matmul(ps_start[:, 0:1], before_e[0:NE], count16[0:NE, 0:1], start=True, stop=True)
            nc.tensor.matmul(ps_start[:, 1:2], same_e[0:NE], count16[0:NE, 0:1], start=True, stop=True
                             ).then_inc(S["started"], 1)
            pe.wait_ge(S["onehot_ready"], 1)
            pe.wait_ge(S["wide_ready"], 1)
            nc.tensor.matmul(ps_tile, expert_no[0:NE, 0:1], onehot16[0:NE, 0:NS], start=True, stop=True)
            for c in range(7):
                last = nc.tensor.matmul(ps_params[:, c, :], act_wide[0:NE, c, :], onehot[0:NE, :], start=True, stop=True)
            last.then_inc(S["tables_done"], 1)

            def turn_x(n, q, landed):
                pe.wait_ge(x_landed[q], landed)
                turn(q % 2, x_in[:, q], S["ex_turned"])

            def expand(n, q, e, shared):
                s = q % 2
                pe.wait_ge(S["exT_ready"], n + 1)
                if not shared:
                    pe.wait_ge(S["pick_ready"], n - NT + 1)
                for k in range(KD):
                    nc.tensor.matmul(ps_h[s], xT[:, s, k, :], of_expert(w1, e, k), start=(k == 0), stop=False)
                nc.tensor.matmul(ps_h[s], pick_shared[0:NB] if shared else pick[0:NB, q], biases[0:NB],
                                 start=False, stop=True).then_inc(S["h_summed"], 1)

            def turn_t(n, s):
                pe.wait_ge(S["swi"], n * 4 + 4)
                for k in range(KI):
                    last = nc.tensor.transpose(ps_t[s][0:IH, k, :], up[:, s, k * IH:(k + 1) * IH], identity)
                last.then_inc(S["t_turned"], 1)

            def contract(n, q, e, shared):
                s = q % 2
                pe.wait_ge(S["tT_ready"], n + 1)
                if shared:
                    pe.wait_ge(S["z_added"], n + 1)
                else:
                    if q < 2:
                        pe.wait_ge(S["z_added"], NT + q + 1)
                    pe.wait_ge(S["y_copied"], n - NT + 1)
                for k in range(KI):
                    rows_ = IH + 1 if k == 0 else IH
                    last = nc.tensor.matmul(ps_y[s], tT[0:rows_, s, k, :], of_expert(w2, e, k, rows_), start=(k == 0),
                                            stop=(k == KI - 1))
                last.then_inc(S["y_summed"], 1)

            def expert(n, shared):
                if shared:
                    return E
                return pe.value_load(tile_expert[0:1, n - NT:n - NT + 1] if isinstance(n, int)
                                     else tile_expert[0:1, bass.ds(n - NT, 1)], min_val=0, max_val=E - 1)

            def step(n, q, g, tail=True, more=True, shared=False, shared_tail=False):
                if tail:
                    turn_t(n - 2, q % 2)
                if more:
                    turn_x(n + 1, (q + 1) % 4, (g + (0 if q == 2 else 1)) * 16 + 16 if tail else 16)
                if isinstance(n, int) and n == NT:
                    pe.wait_ge(S["w_experts_in"], 16 * 8)
                expand(n, q, expert(n, shared), shared)
                if tail:
                    contract(n - 2, (q - 2) % 4, expert(n - 2, shared_tail), shared_tail)

            pe.wait_ge(S["tables_out"], 2)
            pe.wait_ge(S["biases_ready"], 1)
            pe.wait_ge(S["w_shared_in"], 32)
            pe.sem_inc(S["z_added"], 2)
            pe.sem_inc(S["y_copied"], 2)
            turn_x(0, 0, 16)
            run_tiles(pe, step)
            for n in (NT + NS - 2, NT + NS - 1):
                turn_t(n, n % 2)
                contract(n, n % 4, expert(n, False), False)
            pe.wait_ge(S["att_w_in"], 16 * 5)
            for c in range(2):
                last = nc.tensor.matmul(bank[0][:, c * D:(c + 1) * D], att_w23[:, c:c + 1].to_broadcast([P, P]), att_w1,
                                        start=True, stop=True)
            last.then_inc(S["u_summed"], 1)

        @block.vector
        def _(dve):
            chain = Chain(dve, S["dve_chain"])
            link = chain.link
            layernorm_spread(nc, chain, stats, mean, var, tmp).then_inc(S["var_ready"], 1)
            dve.wait_ge(S["sd_ready"], 1)
            nc.vector.reciprocal(rstd, var).then_inc(S["var_ready"], 1)
            dve.wait_ge(S["var_ready"], 2)
            nc.vector.scalar_tensor_tensor(out=offset, in0=mean, scalar=-1.0, in1=rstd, op0=ALU.mult, op1=ALU.mult
                                           ).then_inc(S["var_ready"], 1)

            def normalise(t, s):
                nc.vector.tensor_scalar(xn[:, s], at(x, t), col(mean, t), col(rstd, t), ALU.subtract, ALU.mult
                                        ).then_inc(S["xn_ready"], 1)

            normalise(0, 0)
            normalise(1, 1)
            with dve.Fori(1, NT // 2) as g:
                for u in range(2):
                    dve.wait_ge(S["x_turned"], g * 2 + (u - 1))
                    normalise(g * 2 + u, u)

            dve.wait_ge(S["small_in"], 16 * SMALL_DMAS)
            raw = act_table[0:NE, 3:5]
            link(nc.vector.scalar_tensor_tensor(out=soft[0:NE, 0], in0=raw, scalar=-1.0, in1=raw, op0=ALU.mult, op1=ALU.max))
            nc.vector.tensor_scalar(soft[0:NE, 1], raw, 0.0, None, ALU.max).then_inc(S["soft_in"], 1)
            dve.wait_ge(S["soft_out"], 1)
            nc.vector.tensor_scalar(soft[0:NE, 0], soft[0:NE, 0], 1.0, None, ALU.add).then_inc(S["soft_in"], 1)

            def over_experts(v):
                return v.unsqueeze(2).to_broadcast([P, NT, E])

            ranks = from_last.unsqueeze(1).to_broadcast([P, NT, E])
            dve.wait_ge(S["logits_done"], NT)
            dve.wait_ge(S["consts"], consts)
            link(nc.vector.tensor_reduce(top[:, 0], ps_logits, AX, ALU.max))
            nc.vector.tensor_tensor(prob, ps_logits, over_experts(top[:, 0]), ALU.subtract).then_inc(S["shifted"], 1)
            dve.wait_ge(S["exped"], 1)
            link(nc.vector.tensor_reduce(top[:, 0], prob, AX, ALU.add))
            link(nc.vector.reciprocal(top[:, 0], top[:, 0]))
            link(nc.vector.tensor_tensor(prob, prob, over_experts(top[:, 0]), ALU.mult))
            for k in range(TOPK):
                link(nc.vector.tensor_reduce(weight[:, k], prob, AX, ALU.max))
                link(nc.vector.tensor_tensor(equal, prob, over_experts(weight[:, k]), ALU.is_equal))
                link(nc.vector.tensor_tensor(first, equal, ranks, ALU.mult))
                link(nc.vector.tensor_reduce(top[:, 1], first, AX, ALU.min))
                link(nc.vector.tensor_tensor(best[k], ranks, over_experts(top[:, 1]), ALU.is_equal))
                if k < TOPK - 1:
                    link(nc.vector.scalar_tensor_tensor(out=prob, in0=best[k], scalar=-4.0, in1=prob, op0=ALU.mult, op1=ALU.add))
            nc.vector.tensor_tensor(chosen[:, :, 0:E], best[0], best[1], ALU.add).then_inc(S["chosen_ready"], 1)
            link(nc.vector.tensor_tensor(top[:, 2], weight[:, 0], weight[:, 1], ALU.add))
            link(nc.vector.reciprocal(top[:, 2], top[:, 2]))
            for k in range(TOPK):
                link(nc.vector.tensor_tensor(weight[:, k], weight[:, k], top[:, 2], ALU.mult))
            dve.wait_ge(S["soft_out"], 2)
            link(nc.vector.tensor_tensor(act_table[0:NE, 3:5], soft[0:NE, 0], soft[0:NE, 1], ALU.add))
            link(nc.vector.tensor_scalar(act_table[0:NE, 5:7], act_table[0:NE, 3:5], -1.0, None, ALU.mult))
            nc.vector.tensor_copy(act_wide[0:NE], act_table[0:NE, 0:7].unsqueeze(2).to_broadcast([NE, 7, P])
                                  ).then_inc(S["wide_ready"], 1)

            dve.wait_ge(S["counted"], 1)
            link(nc.vector.tensor_copy(count[0:NE, 0:1], ps_count))
            link(nc.vector.tensor_scalar(first[0:NE, 0, :], steps128[0:NE], count[0:NE, 0:1], 0.0, ALU.is_lt, ALU.add,
                                         accum_out=count[0:NE, 1:2]))
            link(nc.vector.tensor_copy(count16[0:NE, 0:1], count[0:NE, 1:2]))
            nc.vector.tensor_scalar(count_wide[0:NE], ones16[0:NE], count[0:NE, 1:2], None, ALU.mult).then_inc(S["wide_count"], 1)
            dve.wait_ge(S["started"], 1)
            link(nc.vector.tensor_copy(start[0:NB], ps_start))
            link(nc.vector.tensor_tensor(stop[0:NB, 0:1], start[0:NB, 0:1], start[0:NB, 1:2], ALU.add))
            link(nc.vector.tensor_scalar(onehot[0:NB, 0:NS], tile_no[0:NB], start[0:NB, 0:1], None, ALU.is_ge))
            link(nc.vector.scalar_tensor_tensor(out=onehot[0:NB, 0:NS], in0=tile_no[0:NB], scalar=stop[0:NB, 0:1],
                                                in1=onehot[0:NB, 0:NS], op0=ALU.is_lt, op1=ALU.mult))
            nc.vector.tensor_copy(onehot16[0:NE, 0:NS], onehot[0:NE, 0:NS]).then_inc(S["onehot_ready"], 1)
            link(nc.vector.tensor_scalar(base, ps_base, float(P), None, ALU.mult))
            dve.wait_ge(S["ranked"], 1)
            link(nc.vector.tensor_tensor(first, ps_rank, base.unsqueeze(1).to_broadcast([P, NT, E]), ALU.add))
            for k in range(TOPK):
                link(nc.vector.tensor_tensor(best[k], best[k], first, ALU.mult))
                link(nc.vector.tensor_reduce(top[:, 2 + k], best[k], AX, ALU.add))
                link(nc.vector.tensor_copy(slots[:, k], top[:, 2 + k]))
            nc.vector.tensor_copy(top[:, 0], top[:, 1]).then_inc(S["slots_ready"], 1)
            dve.wait_ge(S["tables_done"], 1)
            nc.vector.tensor_copy(tile_expert[0:1], ps_tile).then_inc(S["tables_out"], 1)
            nc.vector.tensor_copy(params, ps_params).then_inc(S["tables_out"], 1)
            dve.wait_ge(S["tables_out"], 2)

            def pick_expert(n, q):
                nc.vector.tensor_scalar(pick[0:NB, q], ones16[0:NB], col(onehot[0:NB], n - NT), None, ALU.mult
                                        ).then_inc(S["pick_ready"], 1)

            def step(n, q, g, tail=True, more=True, shared=False, shared_tail=False):
                s = q % 2
                tile = NS if shared else n - NT
                if more and not (shared and not (isinstance(n, int) and n == NT - 1)):
                    dve.wait_ge(S["y_summed"], n - 2)
                    pick_expert(n + 1, (q + 1) % 4)
                dve.wait_ge(S["h_summed"], n + 1)
                h = ps_h[s].rearrange("p (i two) -> p i two", two=2)

                def c(which):
                    return params_at(params, which, tile)

                nc.vector.tensor_scalar(gate[:, s], h[:, :, 0], c(3), c(5), ALU.min, ALU.max).then_inc(S["swi"], 1)
                nc.vector.tensor_scalar(up[:, s], h[:, :, 1], c(4), c(6), ALU.min, ALU.max).then_inc(S["swi"], 1)
                dve.wait_ge(S["swi"], n * 4 + 2)
                nc.vector.scalar_tensor_tensor(out=up[:, s], in0=up[:, s], scalar=c(2), in1=gate[:, s],
                                               op0=ALU.add, op1=ALU.mult).then_inc(S["swi"], 1)
                dve.wait_ge(S["sig_ready"], n + 1)
                dve.wait_ge(S["swi"], n * 4 + 3)
                nc.vector.scalar_tensor_tensor(out=up[:, s], in0=up[:, s], scalar=c(1), in1=sig[:, s],
                                               op0=ALU.mult, op1=ALU.mult).then_inc(S["swi"], 1)
                if tail and shared_tail:
                    dve.wait_ge(S["y_summed"], n - 1)
                    nc.vector.tensor_tensor(at(x, n - 2), ps_y[s], at(x, n - 2), ALU.add).then_inc(S["z_added"], 1)

            run_tiles(dve, step)
            dve.wait_ge(S["z_added"], NT + 2)

            for c in range(NT // SOME):
                tiles = range(c * SOME, (c + 1) * SOME)
                some = slice(c * SOME, (c + 1) * SOME)
                dve.wait_ge(S["combined_half"], c + 1)
                nc.vector.tensor_tensor(x[:, some], x[:, some], y_in[c][:, 0], ALU.add).then_inc(S["combined"], 1)
                dve.wait_ge(S["combined"], c + 1)
                for t in tiles:
                    nc.vector.bn_stats(stats[:, t], x[:, t]).then_inc(S["stats_done"], 1)
                if c == 0:
                    dve.wait_ge(S["u_ready"], 1)
                    link(nc.vector.tensor_reduce(u_sum, u_wide, AX, ALU.add))
                nc.vector.tensor_tensor(product[1][:, some], x[:, some], u_wide[:, 1].unsqueeze(1).to_broadcast([P, SOME, D]),
                                        ALU.mult).then_inc(S["product2_ready"], 1)
            dve.wait_ge(S["product2_ready"], NT // SOME)
            nc.vector.tensor_reduce(f_raw[:, 1, some], product[1][:, some], AX, ALU.add).then_inc(S["f_raw_ready"], 1)
            dve.wait_ge(S["stats_done"], NT)
            dve.wait_ge(S["f_raw_ready"], 2 * NT - SOME + 1)


def run_tiles(engine, step):
    for n in (0, 1):
        step(n, n, 0, tail=False, shared=True)
    with engine.Fori(0, (NT - 4) // 4) as g:
        for u in range(4):
            step(g * 4 + (2 + u), (2 + u) % 4, g, shared=True, shared_tail=True)
    for n in range(NT - 2, NT + 2):
        step(n, n % 4, (n - 2) // 4, shared=n < NT, shared_tail=True)
    for n in range(NT + 2, NT + 6):
        step(n, n % 4, (n - 2) // 4)
    with engine.Fori(NT // 4 + 1, (NT + NS - 2) // 4) as g:
        for u in range(4):
            step(g * 4 + (2 + u), (2 + u) % 4, g)
    for n in range((NT + NS - 2) // 4 * 4 + 2, NT + NS):
        step(n, n % 4, (n - 2) // 4, more=n < NT + NS - 1)


def rows(view, i):
    tiles = view.rearrange("(t p) d -> t p d", p=P)
    return tiles[i] if isinstance(i, int) else tiles[bass.ds(i, 1)].rearrange("o p d -> (o p) d")


def params_at(params, which, tile):
    return params[:, which, tile:tile + 1] if isinstance(tile, int) else params[:, which, bass.ds(tile, 1)]


def of_expert(w, e, k, rows_=P):
    if isinstance(e, int):
        return w[0:rows_, e, k, :]
    return w[0:rows_, bass.ds(e, 1), k, :].squeeze(1)


def attention(nc, dram, mem, sem):
    x, edges = mem["x"], mem["edges"]
    identity = mem["identity"]
    mean, rstd = mem["mean"], mem["rstd"]
    psum = mem["PSUM"]
    SLOPE = 0.01
    LOG_SCALE = float(np.log(SCALE16))
    CHUNK = 4
    CHUNKS = NJ // CHUNK
    PLAIN = CHUNKS // 2
    NTP = PLAIN * CHUNK
    assert 2 * NTP == NT
    plain = mem["XLN"][:, 0:NTP * D].rearrange("p (t d) -> p t d", d=D)
    ln16 = mem["XLN"][:, NTP * D:NT * D].bitcast(FP16).rearrange("p (t d) -> p t d", d=2 * D)
    arena = Region(mem["ARENA"], mem["ARENA"].shape[1] - KD * D)
    edge_in = arena.take(BF16, 2, N)
    s_row, l_row, p_row = arena.take(F32, 2, N), arena.take(F32, 2, N), arena.take(F32, 2, N)
    pT = arena.take(F32, PLAIN, CHUNK * P)
    pT_high, pT_low = (arena.take(FP16, CHUNKS - PLAIN, CHUNK * P) for _ in range(2))
    f2 = arena.take(F32, N)
    split = l_row[:, 1].rearrange("p (t d) -> p t d", d=D)
    small = Region(mem["SMALL"], SMALL_WORDS)
    f_raw, u_sum, f_bias = mem["f_raw"], mem["u_sum"], mem["f_bias"]
    stats, var, tmp, slope, offset = mem["stats"], *(small.take(F32, NT) for _ in range(4))
    f_col, f_tmp = small.take(F32, 2, NT), small.take(F32, 2, NT)
    f1, f2_col = f_col[:, 0], f_col[:, 1]
    f1_high, f1_low, total, inverse = (small.take(F32, NT) for _ in range(4))
    largest, minus, bound, waited = (small.take(F32, 4) for _ in range(4))
    vals = small.take(F32, 2, D)
    most, least = mem["most"], mem["least"]

    bank = [psum[:, 512 * b:512 * (b + 1)] for b in range(8)]
    ps_sum = [bank[6 + s][:, 0:D] for s in range(2)]

    names = ("dve_chain", "var_ready", "sd_ready", "slope_ready", "plain_ready", "scaled_ready",
             "high_ready", "split_done", "f2_col_ready", "f2_wide", "f2_out", "f1_low_ready", "s_ready",
             "minus_ready", "low_ready", "l_ready", "p_ready", "p_turned", "pT_ready", "pT_high_ready", "pT_low_ready", "summed",
             "inverse_ready", "vals_ready", "x_added", "bound_ready", "stats_done")
    S = {name: sem("c_" + name) for name in names}
    edge_landed = [sem(f"c_edge_landed{s}") for s in range(2)]

    with nc.Block() as block:

        @block.sync
        def _(sp):
            for i in range(2):
                sp.dma_start(edge_in[:, i], edges[:, i]).then_inc(edge_landed[i], 16)
            sp.dma_start(mem["weight8"].rearrange("p (k d) -> p k d", d=D),
                         dram["L1_ffn_weight"].rearrange("(k p) d -> p k d", p=P)).then_inc(mem["weight8_in"], 16)
            with sp.Fori(1, NT // 2) as g:
                for q in range(2):
                    sp.wait_ge(S["s_ready"], g * 2 + (q - 1))
                    sp.dma_start(edge_in[:, q], at(edges, g * 2 + q)).then_inc(edge_landed[q], 16)

        @block.scalar
        def _(act):
            act.wait_ge(S["var_ready"], 1)
            nc.scalar.activation(var, var, ACT.Sqrt).then_inc(S["sd_ready"], 1)
            nc.scalar.activation(waited[:, 2:3], mem["ones"][:, 0:1], ACT.Exp)
            act.wait_ge(S["slope_ready"], 1)
            with act.Fori(0, NTP // 2) as g:
                for u in range(2):
                    t = g * 2 + u
                    nc.scalar.activation(at(ln16, t)[:, 0:D], at(x, t + NTP), ACT.Identity, bias=col(offset, t + NTP),
                                         scale=col(slope, t + NTP)).then_inc(S["high_ready"], 1)
            for c in range(NT * P // 512):
                act.wait_ge(S["f2_wide"], c + 1)
                nc.scalar.activation(f2[:, c * 512:(c + 1) * 512], bank[c], ACT.Copy).then_inc(S["f2_out"], 1)

            def low(i, s):
                act.wait_ge(S["s_ready"], i + 1)
                nc.scalar.activation(l_row[:, s], s_row[:, s], ACT.Identity, bias=col(f1_low, i), scale=SLOPE
                                     ).then_inc(S["low_ready"], 1)

            def exponent(i, s):
                act.wait_ge(S["l_ready"], i + 1)
                act.wait_ge(S["minus_ready"], i + 1)
                nc.scalar.activation(p_row[:, s], l_row[:, s], ACT.Exp, bias=minus[:, s:s + 1],
                                     accum_out=col(total, i)).then_inc(S["p_ready"], 1)

            def turned_out(i, c):
                act.wait_ge(S["p_turned"], i * CHUNKS + (c + 1))
                if c < PLAIN:
                    nc.scalar.activation(pT[:, c], bank[c], ACT.Copy).then_inc(S["pT_ready"], 1)
                else:
                    nc.scalar.activation(pT_high[:, c - PLAIN], bank[c], ACT.Copy).then_inc(S["pT_high_ready"], 1)

            def weighted(i, s):
                act.wait_ge(S["summed"], i + 1)
                act.wait_ge(S["inverse_ready"], i + 1)
                act.wait_ge(S["x_added"], i + 1)
                nc.scalar.activation(vals[:, s], ps_sum[s], ACT.Relu, scale=col(inverse, i)).then_inc(S["vals_ready"], 1)

            def step(i, s, more=2, first=False):
                for c in range(CHUNKS - 1):
                    turned_out(i, c)
                if more >= 1:
                    exponent(i + 1, 1 - s)
                turned_out(i, CHUNKS - 1)
                if not first:
                    weighted(i - 1, 1 - s)
                if more >= 2:
                    act.wait_ge(S["p_ready"], i + 1)
                    low(i + 2, s)

            def in_float32(first, last):
                with act.Fori(first, last) as g:
                    for u in range(2):
                        t = g * 2 + u
                        nc.scalar.activation(at(plain, t), at(x, t), ACT.Identity, bias=col(offset, t), scale=col(slope, t)
                                             ).then_inc(S["plain_ready"], 1)

            in_float32(0, NTP // 4)
            act.wait_ge(S["f1_low_ready"], 1)
            low(0, 0)
            in_float32(NTP // 4, NTP // 2)
            exponent(0, 0)
            low(1, 1)
            step(0, 0, first=True)
            with act.Fori(0, (NT - 4) // 2) as g:
                for q in range(2):
                    step(g * 2 + (1 + q), (1 + q) % 2)
            step(NT - 3, 1)
            step(NT - 2, 0, more=1)
            step(NT - 1, 1, more=0)
            weighted(NT - 1, 1)

        @block.tensor
        def _(pe):
            pe.wait_ge(S["f2_col_ready"], 1)
            for c in range(NT * P // 512):
                for b in range(CHUNK):
                    t = c * CHUNK + b
                    last = nc.tensor.matmul(bank[c][:, b * P:(b + 1) * P], f2_col[:, t:t + 1].to_broadcast([P, P]), identity,
                                            start=True, stop=True)
                last.then_inc(S["f2_wide"], 1)

            def turn(i, s, c):
                pe.wait_ge(S["p_ready"], i + 1)
                for b in range(CHUNK):
                    j = c * CHUNK + b
                    last = nc.tensor.transpose(bank[c][:, b * P:(b + 1) * P], p_row[:, s, j * P:(j + 1) * P], identity)
                last.then_inc(S["p_turned"], 1)

            def weigh(i, s, c):
                if c == 0:
                    pe.wait_ge(S["vals_ready"], i + 1)
                if c < PLAIN:
                    pe.wait_ge(S["pT_ready"], i * PLAIN + (c + 1))
                else:
                    pe.wait_ge(S["pT_low_ready"], i * (CHUNKS - PLAIN) + (c - PLAIN + 1))
                for b in range(CHUNK):
                    j, here = c * CHUNK + b, slice(b * P, (b + 1) * P)
                    if c < PLAIN:
                        nc.tensor.matmul(ps_sum[s], pT[:, c, here], plain[:, j], start=(j == 0), stop=False)
                    else:
                        high, low = pT_high[:, c - PLAIN, here], pT_low[:, c - PLAIN, here]
                        nc.tensor.matmul(ps_sum[s], high, ln16[:, j - NTP, 0:D], start=False, stop=False)
                        nc.tensor.matmul(ps_sum[s], high, ln16[:, j - NTP, D:2 * D], start=False, stop=False)
                        last = nc.tensor.matmul(ps_sum[s], low, ln16[:, j - NTP, 0:D], start=False, stop=(j == NJ - 1))
                if c == CHUNKS - 1:
                    last.then_inc(S["summed"], 1)

            def step(i, s, more=True):
                turn(i, s, 2)
                weigh(i, s, 0)
                turn(i, s, 3)
                weigh(i, s, 1)
                weigh(i, s, 2)
                if more:
                    turn(i + 1, 1 - s, 0)
                    turn(i + 1, 1 - s, 1)
                weigh(i, s, 3)

            pe.sem_inc(S["vals_ready"], 2)
            pe.wait_ge(S["f2_out"], CHUNKS)
            pe.wait_ge(S["split_done"], NTP)
            pe.wait_ge(S["plain_ready"], NTP)
            turn(0, 0, 0)
            turn(0, 0, 1)
            step(0, 0)
            with pe.Fori(0, (NT - 2) // 2) as g:
                for q in range(2):
                    step(g * 2 + (1 + q), (1 + q) % 2)
            step(NT - 1, 1, more=False)

        @block.vector
        def _(dve):
            chain = Chain(dve, S["dve_chain"])
            link = chain.link
            dve.sem_inc(S["x_added"], 2)
            layernorm_spread(nc, chain, stats, mean, var, tmp).then_inc(S["var_ready"], 1)
            dve.wait_ge(S["sd_ready"], 1)
            link(nc.vector.reciprocal(rstd, var))
            link(nc.vector.tensor_scalar(slope, rstd, SCALE16, None, ALU.mult))
            nc.vector.scalar_tensor_tensor(out=offset, in0=mean, scalar=-1.0, in1=slope, op0=ALU.mult, op1=ALU.mult
                                           ).then_inc(S["slope_ready"], 1)
            for which in (1, 0):
                link(nc.vector.scalar_tensor_tensor(out=f_tmp[:, which], in0=mean, scalar=u_sum[:, which:which + 1],
                                                    in1=f_raw[:, which], op0=ALU.mult, op1=ALU.subtract))
                link(nc.vector.tensor_tensor(f_tmp[:, which], f_tmp[:, which], rstd, ALU.mult))
                of_f = nc.vector.tensor_scalar(f_col[:, which], f_tmp[:, which], -1.0, f_bias[:, which:which + 1],
                                               ALU.mult, ALU.add)
                if which:
                    of_f.then_inc(S["f2_col_ready"], 1)
            link(of_f)
            link(nc.vector.tensor_scalar(f1_high, f1, LOG_SCALE, None, ALU.add))
            nc.vector.tensor_scalar(f1_low, f1, SLOPE, LOG_SCALE, ALU.mult, ALU.add).then_inc(S["f1_low_ready"], 1)
            with dve.Fori(0, NTP // 2) as g:
                for u in range(2):
                    t = g * 2 + u
                    nc.vector.tensor_scalar(at(split, t), at(x, t + NTP), col(slope, t + NTP), col(offset, t + NTP),
                                            ALU.mult, ALU.add).then_inc(S["scaled_ready"], 1)
            dve.wait_ge(S["f1_low_ready"], 1)
            dve.wait_ge(S["f2_out"], CHUNKS)

            def masked(i, s, landed):
                dve.wait_ge(edge_landed[s], landed)
                if not (isinstance(i, int) and i < 2):
                    dve.wait_ge(S["l_ready"], i - 1)
                nc.vector.memset(waited[:, s:s + 1], 0.0)
                nc.vector.tensor_tensor_reduce(out=s_row[:, s], in0=f2, in1=edge_in[:, s], scale=1.0, scalar=-3.0e38,
                                               op0=ALU.add, op1=ALU.max, accum_out=largest[:, s:s + 1]
                                               ).then_inc(S["s_ready"], 1)

            def limit(i, s):
                dve.wait_ge(S["s_ready"], i + 1)
                nc.vector.tensor_scalar(bound[:, s:s + 1], largest[:, s:s + 1], col(f1, i), -1.0, ALU.add, ALU.mult
                                        ).then_inc(S["bound_ready"], 1)
                dve.wait_ge(S["bound_ready"], i + 1)
                nc.vector.scalar_tensor_tensor(out=minus[:, s:s + 1], in0=bound[:, s:s + 1], scalar=SLOPE,
                                               in1=bound[:, s:s + 1], op0=ALU.mult, op1=ALU.min).then_inc(S["minus_ready"], 1)

            def leaky(i, s):
                dve.wait_ge(S["low_ready"], i + 1)
                nc.vector.scalar_tensor_tensor(out=l_row[:, s], in0=s_row[:, s], scalar=col(f1_high, i), in1=l_row[:, s],
                                               op0=ALU.add, op1=ALU.max).then_inc(S["l_ready"], 1)

            def low_half(i, c):
                dve.wait_ge(S["pT_high_ready"], i * (CHUNKS - PLAIN) + (c + 1))
                nc.vector.tensor_tensor(pT_low[:, c], bank[PLAIN + c], pT_high[:, c], ALU.subtract
                                        ).then_inc(S["pT_low_ready"], 1)

            def invert(i):
                nc.vector.reciprocal(col(inverse, i), col(total, i)).then_inc(S["inverse_ready"], 1)

            def finish(i, s):
                dve.wait_ge(S["vals_ready"], i + 3)
                nc.vector.scalar_tensor_tensor(out=at(x, i), in0=vals[:, s], scalar=1.0 / SCALE16, in1=at(x, i),
                                               op0=ALU.mult, op1=ALU.add).then_inc(S["x_added"], 1)
                dve.wait_ge(S["x_added"], i + 3)
                nc.vector.bn_stats(at(stats, i), at(x, i)).then_inc(S["stats_done"], 1)
                nc.vector.tensor_reduce(col(most, i), at(x, i), AX, ALU.max).then_inc(S["stats_done"], 1)
                nc.vector.tensor_reduce(col(least, i), at(x, i), AX, ALU.min).then_inc(S["stats_done"], 1)

            def step(i, s, more=2, landed=None, first=False):
                if more >= 1:
                    leaky(i + 1, 1 - s)
                low_half(i, 0)
                if more >= 2:
                    masked(i + 2, s, landed)
                low_half(i, 1)
                if more >= 2:
                    dve.wait_ge(S["p_ready"], i + 1)
                    limit(i + 2, s)
                invert(i)
                if not first:
                    finish(i - 2, s)

            masked(0, 0, 16)
            limit(0, 0)
            dve.wait_ge(S["scaled_ready"], NTP)
            with dve.Fori(0, NTP // 2) as g:
                for u in range(2):
                    t = g * 2 + u
                    dve.wait_ge(S["high_ready"], t + 1)
                    nc.vector.tensor_tensor(at(ln16, t)[:, D:2 * D], at(split, t), at(ln16, t)[:, 0:D], ALU.subtract
                                            ).then_inc(S["split_done"], 1)
            dve.wait_ge(S["split_done"], NTP)
            leaky(0, 0)
            masked(1, 1, 16)
            limit(1, 1)
            dve.wait_ge(mem["weight8_in"], 16)
            link(nc.vector.tensor_reduce(mem["w_extremes"][:, 0:1], mem["weight8"], AX, ALU.max))
            link(nc.vector.tensor_reduce(mem["w_extremes"][:, 1:2], mem["weight8"], AX, ALU.min))
            step(0, 0, landed=32, first=True)
            step(1, 1, landed=32, first=True)
            with dve.Fori(1, (NT - 2) // 2) as g:
                for q in range(2):
                    step(g * 2 + q, q, landed=(g + 2) * 16)
            step(NT - 2, 0, more=1)
            step(NT - 1, 1, more=0)
            finish(NT - 2, 0)
            finish(NT - 1, 1)
            dve.wait_ge(S["stats_done"], 3 * NT)



def fp8_product(nc, mem, sem):
    x = mem["x"]
    identity, identity16, ones = mem["identity"], mem["identity16"], mem["ones"]
    mean, rstd = mem["mean"], mem["rstd"]
    psum = mem["PSUM"]
    arena = Region(mem["ARENA"], mem["ARENA"].shape[1] - KD * D)
    PART = 4
    sizes = [PART // 2] + [PART] * (NT // PART - 1) + [PART // 2]
    parts = [range(sum(sizes[:h]), sum(sizes[:h + 1])) for h in range(len(sizes))]
    LAST = len(parts) - 1
    HELPED = LAST - 2
    weight, w_clip = mem["weight8"], arena.take(F32, KD * D)
    w_exp, w_c, w_sum = (arena.take(F32, KD * D) for _ in range(3))
    w8 = arena.take(BF16, KD, D)
    v, clip, exponent_, c_, sum_ = (arena.take(F32, 2, PART * D) for _ in range(5))
    q8 = arena.take(BF16, 2, PART * D)
    qT = arena.take(BF16, 2, PART * KD, P)
    result = arena.take(F32, 2, PART * D)
    small = Region(mem["SMALL"], SMALL_WORDS)
    stats, var, tmp = mem["stats"], small.take(F32, NT), small.take(F32, NT)
    high, low = mem["most"], mem["least"]
    w_high = mem["w_extremes"]
    largest = small.take(F32, 2)
    largest_row = small.take(F32, 2)
    amax, scale8, unscale = (small.take(F32, 2) for _ in range(3))
    out_scale = small.take(F32, 2)
    slope, offset = small.take(F32, NT), small.take(F32, NT)
    MAGIC = 1.5 * 2.0 ** (23 - 3)
    LEAST = 2.0 ** -6

    bank = [psum[:, 512 * b:512 * (b + 1)] for b in range(8)]
    ps_rows = bank[6][0:1, 0:2 * P].rearrange("p (c q) -> p c q", q=P)
    ps_wide = bank[7][:, 0:2]
    ps_q = [bank[s][:, 0:PART * KD * P // 2].bitcast(BF16).rearrange("p (b q) -> p b q", q=P) for s in range(2)]
    ps_out = [psum[:, (1 + s) * PART * D:(2 + s) * PART * D] for s in range(2)]

    names = ("dve_chain", "var_ready", "sd_ready", "largest_ready", "extremes_out", "row_ready",
             "scales_ready", "v_ready", "rounded", "w_rounded", "q_ready", "q_turned", "qT_ready", "summed",
             "result_scaled", "result_ready", "last_ready")
    S = {name: sem("d_" + name) for name in names}
    stored = sem("d_stored")
    out_tiles = mem["out"].rearrange("(t p) d -> p t d", p=P)

    def tiles_of(h):
        return x[:, parts[h][0]:parts[h][-1] + 1]

    def flat(h):
        return tiles_of(h).rearrange("p t d -> p (t d)")

    with nc.Block() as block:

        @block.sync
        def _(sp):
            for h, tiles in enumerate(parts):
                if h < HELPED:
                    sp.wait_ge(S["result_ready"], h + 1)
                else:
                    sp.wait_ge(S["last_ready"], h - HELPED + 1)
                sp.dma_start(out_tiles[:, tiles[0]:tiles[-1] + 1], tiles_of(h)).then_inc(stored, 16)
            sp.wait_ge(stored, 16 * len(parts))

        @block.gpsimd
        def _(pool):
            pool.wait_ge(S["w_rounded"], 1)
            nc.gpsimd.tensor_tensor(w_sum, w_clip, w_c, ALU.add).then_inc(S["w_rounded"], 1)
            pool.wait_ge(S["w_rounded"], 2)
            nc.gpsimd.tensor_tensor(w8.rearrange("p k d -> p (k d)"), w_sum, w_c, ALU.subtract).then_inc(S["w_rounded"], 1)
            for h in range(HELPED):
                pool.wait_ge(S["result_scaled"], h + 1)
                nc.gpsimd.tensor_tensor(flat(h), result[:, h % 2, 0:len(parts[h]) * D], flat(h), ALU.add
                                        ).then_inc(S["result_ready"], 1)

        @block.scalar
        def _(act):
            act.wait_ge(S["var_ready"], 1)
            nc.scalar.activation(var, var, ACT.Sqrt).then_inc(S["sd_ready"], 1)

            def scaled(h):
                if h >= 2:
                    act.wait_ge(S["rounded"], (h - 2) * 4 + 1)
                for i, t in enumerate(parts[h]):
                    nc.scalar.activation(v[:, h % 2, i * D:(i + 1) * D], x[:, t], ACT.Identity,
                                         bias=col(offset, t), scale=col(slope, t)).then_inc(S["v_ready"], 1)

            def qT_out(h):
                blocks = len(parts[h]) * KD
                act.wait_ge(S["q_turned"], h + 1)
                nc.scalar.activation(qT[:, h % 2, 0:blocks], ps_q[h % 2][:, 0:blocks], ACT.Copy).then_inc(S["qT_ready"], 1)

            def scale_result(h):
                width = len(parts[h]) * D
                act.wait_ge(S["summed"], h + 1)
                if h >= 2:
                    act.wait_ge(S["result_ready"], h - 1)
                nc.scalar.activation(result[:, h % 2, 0:width], ps_out[h % 2][:, 0:width],
                                     ACT.Copy, scale=out_scale[:, 0:1]).then_inc(S["result_scaled"], 1)

            act.wait_ge(S["scales_ready"], 1)
            scaled(0)
            scaled(1)
            for h in range(LAST + 1):
                qT_out(h)
                if h + 2 <= LAST:
                    scaled(h + 2)
                if 1 <= h <= HELPED:
                    scale_result(h - 1)

        @block.tensor
        def _(pe):
            pe.wait_ge(S["largest_ready"], 1)
            for c in range(2):
                last = nc.tensor.transpose(ps_rows[:, c, :], largest[:, c:c + 1], identity)
            last.then_inc(S["extremes_out"], 1)
            pe.wait_ge(S["row_ready"], 1)
            nc.tensor.matmul(ps_wide, ones[0:1, :], largest_row[0:1], start=True, stop=True).then_inc(S["extremes_out"], 1)

            def turn(h):
                pe.wait_ge(S["q_ready"], h + 1)
                for b in range(len(parts[h]) * KD):
                    last = nc.tensor.transpose(ps_q[h % 2][:, b, :], q8[:, h % 2, b * P:(b + 1) * P], identity16)
                last.then_inc(S["q_turned"], 1)

            def product(h):
                pe.wait_ge(S["qT_ready"], h + 1)
                if 0 <= h - 2 < HELPED:
                    pe.wait_ge(S["result_scaled"], h - 1)
                elif h - 2 >= HELPED:
                    pe.wait_ge(S["last_ready"], h - 1 - HELPED)
                for i in range(len(parts[h])):
                    for k in range(KD):
                        last = nc.tensor.matmul(ps_out[h % 2][:, i * D:(i + 1) * D], qT[:, h % 2, i * KD + k, :], w8[:, k, :],
                                                start=(k == 0), stop=(k == KD - 1))
                last.then_inc(S["summed"], 1)

            turn(0)
            pe.wait_ge(S["w_rounded"], 3)
            for h in range(LAST + 1):
                if h < LAST:
                    turn(h + 1)
                product(h)

        @block.vector
        def _(dve):
            chain = Chain(dve, S["dve_chain"])
            link = chain.link
            layernorm_spread(nc, chain, stats, mean, var, tmp).then_inc(S["var_ready"], 1)
            link(nc.vector.scalar_tensor_tensor(out=largest[:, 1:2], in0=w_high[:, 1:2], scalar=-1.0, in1=w_high[:, 0:1],
                                                op0=ALU.mult, op1=ALU.max))
            dve.wait_ge(S["sd_ready"], 1)
            link(nc.vector.reciprocal(rstd, var))
            for view in (high, low):
                link(nc.vector.tensor_tensor(view, view, mean, ALU.subtract))
                link(nc.vector.tensor_tensor(view, view, rstd, ALU.mult))
            link(nc.vector.scalar_tensor_tensor(out=high, in0=low, scalar=-1.0, in1=high, op0=ALU.mult, op1=ALU.max))
            nc.vector.tensor_reduce(largest[:, 0:1], high, AX, ALU.max).then_inc(S["largest_ready"], 1)
            dve.wait_ge(S["extremes_out"], 1)
            nc.vector.tensor_reduce(largest_row[0:1], ps_rows, AX, ALU.max).then_inc(S["row_ready"], 1)
            dve.wait_ge(S["extremes_out"], 2)
            link(nc.vector.tensor_scalar(amax, ps_wide, 1e-12, None, ALU.max))
            link(nc.vector.reciprocal(scale8, amax))
            link(nc.vector.tensor_scalar(scale8, scale8, FP8_MAX, None, ALU.mult))
            link(nc.vector.reciprocal(unscale, scale8))
            link(nc.vector.tensor_tensor(out_scale[:, 0:1], unscale[:, 0:1], unscale[:, 1:2], ALU.mult))
            link(nc.vector.tensor_scalar(slope, rstd, scale8[:, 0:1], None, ALU.mult))
            nc.vector.scalar_tensor_tensor(out=offset, in0=mean, scalar=-1.0, in1=slope, op0=ALU.mult, op1=ALU.mult
                                           ).then_inc(S["scales_ready"], 1)

            def round_part(h):
                s, width = h % 2, slice(0, len(parts[h]) * D)
                if h >= 2:
                    dve.wait_ge(S["q_turned"], h - 1)
                dve.wait_ge(S["v_ready"], parts[h][-1] + 1)
                nc.vector.tensor_scalar(clip[:, s, width], v[:, s, width], FP8_MAX, -FP8_MAX, ALU.min, ALU.max
                                        ).then_inc(S["rounded"], 1)
                dve.wait_ge(S["rounded"], h * 4 + 1)
                nc.vector.tensor_scalar(exponent_[:, s, width].bitcast(I32), clip[:, s, width].bitcast(I32), 0x7F800000, None,
                                        ALU.bitwise_and).then_inc(S["rounded"], 1)
                dve.wait_ge(S["rounded"], h * 4 + 2)
                nc.vector.tensor_scalar(c_[:, s, width], exponent_[:, s, width], LEAST, MAGIC, ALU.max, ALU.mult
                                        ).then_inc(S["rounded"], 1)
                dve.wait_ge(S["rounded"], h * 4 + 3)
                nc.vector.tensor_tensor(sum_[:, s, width], clip[:, s, width], c_[:, s, width], ALU.add).then_inc(S["rounded"], 1)
                dve.wait_ge(S["rounded"], h * 4 + 4)
                nc.vector.tensor_tensor(q8[:, s, width], sum_[:, s, width], c_[:, s, width], ALU.subtract
                                        ).then_inc(S["q_ready"], 1)

            def finish(h):
                dve.wait_ge(S["summed"], h + 1)
                nc.vector.scalar_tensor_tensor(out=flat(h), in0=ps_out[h % 2][:, 0:len(parts[h]) * D],
                                               scalar=out_scale[:, 0:1], in1=flat(h), op0=ALU.mult, op1=ALU.add
                                               ).then_inc(S["last_ready"], 1)

            link(nc.vector.tensor_scalar(w_clip, weight, scale8[:, 1:2], FP8_MAX, ALU.mult, ALU.min))
            link(nc.vector.tensor_scalar(w_clip, w_clip, -FP8_MAX, None, ALU.max))
            link(nc.vector.tensor_scalar(w_exp.bitcast(I32), w_clip.bitcast(I32), 0x7F800000, None, ALU.bitwise_and))
            nc.vector.tensor_scalar(w_c, w_exp, LEAST, MAGIC, ALU.max, ALU.mult).then_inc(S["w_rounded"], 1)
            for h in range(LAST + 1):
                round_part(h)
            for h in range(HELPED, LAST + 1):
                finish(h)


def lay_out(inputs):
    return {name: np.ascontiguousarray(inputs[name]) for name in inputs}


def kernel(**inputs):
    import concourse.bacc as bacc
    from concourse.bass_utils import run_bass_kernel_spmd

    nc = bacc.Bacc("TRN2", target_bir_lowering=False, num_devices=1)
    arrays = lay_out(inputs)
    build(nc, arrays)
    r = run_bass_kernel_spmd(nc, [arrays], core_ids=[0])
    return r.results[0]["out_0_dram"]
```
